# Optimizing a Trainium2 kernel written in Bass

```python
import numpy as np
import jax
import jax.numpy as jnp

def _softmax(x, axis=-1):
    return jax.nn.softmax(x, axis=axis)

def _gelu(x):
    return jax.nn.gelu(x, approximate=True)

def _silu(x):
    return jax.nn.silu(x)

def _sigmoid(x):
    return jax.nn.sigmoid(x)

def _layernorm(x, axis=-1, eps=1e-05):
    m = jnp.mean(x, axis=axis, keepdims=True)
    v = jnp.var(x, axis=axis, keepdims=True)
    return (x - m) / jnp.sqrt(v + eps)

def _scatter_add(tgt, idx, src, axis=0):
    return tgt.at[idx].add(src)

def _segment_sum(src, seg, n):
    return jax.ops.segment_sum(src, seg, n)
kernel_name = 'mk_vit_tower_postln_d2_tok_img256_r4_97b34a'

def setup_inputs(seed: int=0):
    np.random.seed(seed)
    _w = jnp.asarray

    def _rec_inputs():
        import jax
        import jax.numpy as jnp
        _rk = jax.random.key(seed)
        x = -0.000596345 + 1.00056 * jax.random.normal(jax.random.fold_in(_rk, 1), (64, 64, 64, 3), jnp.float32)
        return x
    x = _rec_inputs()

    def _L0_tok_setup():
        import jax, jax.numpy as jnp
        import numpy as np
        B, H, W = (16, 64, 64)
        WIDTH, LAYERS, M1, M2 = (32, 4, 12, 12)
        EPS = 1e-05

        def layer_norm(x, g, b):
            mu = jnp.mean(x, axis=-1, keepdims=True)
            var = jnp.mean((x - mu) ** 2, axis=-1, keepdims=True)
            return (x - mu) * jax.lax.rsqrt(var + EPS) * g + b

        def gelu(x):
            return jax.nn.gelu(x, approximate=False)

        def spectral_conv(x, w1, w2):
            b, c, h, w = x.shape
            x_ft = jnp.fft.rfft2(x)
            out_ft = jnp.zeros((b, w1.shape[1], h, w // 2 + 1), dtype=x_ft.dtype)
            out_ft = out_ft.at[:, :, :M1, :M2].set(jnp.einsum('bixy,ioxy->boxy', x_ft[:, :, :M1, :M2], w1))
            out_ft = out_ft.at[:, :, -M1:, :M2].set(jnp.einsum('bixy,ioxy->boxy', x_ft[:, :, -M1:, :M2], w2))
            return jnp.fft.irfft2(out_ft, s=(h, w))
        key = jax.random.key(seed)
        ks = jax.random.split(key, 16)
        scale = 1.0 / (WIDTH * WIDTH)
        d = {'x': jax.random.normal(ks[0], (B, H, W, 3), jnp.float32), 'fc0_w': jax.random.normal(ks[1], (3, WIDTH), jnp.float32) * 0.5, 'fc0_b': jnp.zeros((WIDTH,), jnp.float32), 'ln0_g': jnp.ones((WIDTH,), jnp.float32), 'ln0_b': jnp.zeros((WIDTH,), jnp.float32), 'w1r': jax.random.uniform(ks[2], (LAYERS, WIDTH, WIDTH, M1, M2), jnp.float32) * scale, 'w1i': jax.random.uniform(ks[3], (LAYERS, WIDTH, WIDTH, M1, M2), jnp.float32) * scale, 'w2r': jax.random.uniform(ks[4], (LAYERS, WIDTH, WIDTH, M1, M2), jnp.float32) * scale, 'w2i': jax.random.uniform(ks[5], (LAYERS, WIDTH, WIDTH, M1, M2), jnp.float32) * scale, 'conv_w': jax.random.normal(ks[6], (LAYERS, WIDTH, WIDTH), jnp.float32) * (1.0 / np.sqrt(WIDTH)), 'conv_b': jnp.zeros((LAYERS, WIDTH), jnp.float32), 'ln_g': jnp.ones((LAYERS, WIDTH), jnp.float32), 'ln_b': jnp.zeros((LAYERS, WIDTH), jnp.float32), 'fc1_w': jax.random.normal(ks[7], (WIDTH, 128), jnp.float32) * (1.0 / np.sqrt(WIDTH)), 'fc1_b': jnp.zeros((128,), jnp.float32), 'fc2_w': jax.random.normal(ks[8], (128, 64), jnp.float32) * (1.0 / np.sqrt(128)), 'fc2_b': jnp.zeros((64,), jnp.float32), 'fc3_w': jax.random.normal(ks[9], (64, 1), jnp.float32) * (1.0 / np.sqrt(64)), 'fc3_b': jnp.zeros((1,), jnp.float32)}
        return d
    _L0_tok_all = _L0_tok_setup()
    _L0_tok_in = {k: v for k, v in _L0_tok_all.items() if k in ('fc0_w', 'fc0_b', 'ln0_g', 'ln0_b', 'w1r', 'w1i', 'w2r', 'w2i', 'conv_w', 'conv_b', 'ln_g', 'ln_b', 'fc1_w', 'fc1_b', 'fc2_w', 'fc2_b', 'fc3_w', 'fc3_b')}
    del _L0_tok_all

    def _L0_attn_setup():
        import jax, jax.numpy as jnp
        import numpy as np
        key = jax.random.key(seed)
        ks = jax.random.split(key, 4)
        B, S, D = (4, 1024, 64)
        x = jax.random.normal(ks[0], (B, S, D), dtype=jnp.float32)
        Wq = jax.random.normal(ks[1], (D, D), dtype=jnp.float32) * 0.02
        Wk = jax.random.normal(ks[2], (D, D), dtype=jnp.float32) * 0.02
        Wv = jax.random.normal(ks[3], (D, D), dtype=jnp.float32) * 0.02
        bq = jnp.zeros((D,), dtype=jnp.float32)
        bk = jnp.zeros((D,), dtype=jnp.float32)
        bv = jnp.zeros((D,), dtype=jnp.float32)
        return {'x': x, 'Wq': Wq, 'bq': bq, 'Wk': Wk, 'bk': bk, 'Wv': Wv, 'bv': bv}
    _L0_attn_all = _L0_attn_setup()
    _L0_attn_in = {k: v for k, v in _L0_attn_all.items() if k in ('Wq', 'bq', 'Wk', 'bk', 'Wv', 'bv')}
    del _L0_attn_all

    def _L0_ffn_setup():
        import math
        import jax, jax.numpy as jnp
        import numpy as np
        CAPACITY_FACTOR = 1.25
        key = jax.random.key(seed)
        ks = jax.random.split(key, 5)
        B, L, D, F, E = (8, 2048, 64, 256, 8)
        h = jax.random.normal(ks[0], (B, L, D), dtype=jnp.float32)
        gate_w = jax.random.normal(ks[1], (D, E), dtype=jnp.float32) * 0.02
        gate_b = jnp.zeros((E,), dtype=jnp.float32)
        w1 = jax.random.normal(ks[2], (E, D, F), dtype=jnp.float32) * (1.0 / math.sqrt(D))
        b1 = jnp.zeros((E, F), dtype=jnp.float32)
        w2 = jax.random.normal(ks[3], (E, F, D), dtype=jnp.float32) * (1.0 / math.sqrt(F))
        b2 = jnp.zeros((E, D), dtype=jnp.float32)
        return {'h': h, 'gate_w': gate_w, 'gate_b': gate_b, 'w1': w1, 'b1': b1, 'w2': w2, 'b2': b2}
    _L0_ffn_all = _L0_ffn_setup()
    _L0_ffn_in = {k: v for k, v in _L0_ffn_all.items() if k in ('gate_w', 'gate_b', 'w1', 'b1', 'w2', 'b2')}
    del _L0_ffn_all

    def _L1_attn_setup():
        import jax, jax.numpy as jnp
        import numpy as np
        B, S, DIN, DH = (8, 2048, 64, 64)

        def _log_g(x):
            return jnp.where(x >= 0, jnp.log(jax.nn.relu(x) + 0.5), -jax.nn.softplus(-x))

        def _mingru_layer(x, W, b):
            gh = jnp.einsum('bsd,ed->bse', x, W) + b
            gate, hidden = jnp.split(gh, 2, axis=-1)
            log_coeffs = -jax.nn.softplus(gate)
            log_vals = -jax.nn.softplus(-gate) + _log_g(hidden)
            Bb, Ss, Dd = log_coeffs.shape
            log_h0 = jnp.full((Bb, 1, Dd), jnp.log(0.5), log_coeffs.dtype)
            log_values = jnp.concatenate([log_h0, log_vals], axis=1)
            a_star = jnp.concatenate([jnp.zeros((Bb, 1, Dd), log_coeffs.dtype), jnp.cumsum(log_coeffs, axis=1)], axis=1)
            log_h = a_star + jax.lax.cumlogsumexp(log_values - a_star, axis=1)
            return jnp.exp(log_h)[:, 1:]

        def _reference_tuple_inner(x, W0, b0, W1, b1):
            out0 = _mingru_layer(x, W0, b0)
            out1 = _mingru_layer(out0, W1, b1)
            h = jnp.stack([out0[:, -1:], out1[:, -1:]])
            return (out1, h)
        key = jax.random.key(seed)
        k0, k1, k2, k3, k4 = jax.random.split(key, 5)
        stdv = 1.0 / np.sqrt(DIN)
        x = jax.random.normal(k0, (B, S, DIN), jnp.float32)
        W0 = jax.random.uniform(k1, (2 * DH, DIN), jnp.float32, -stdv, stdv)
        b0 = jax.random.uniform(k2, (2 * DH,), jnp.float32, -stdv, stdv)
        stdv2 = 1.0 / np.sqrt(DH)
        W1 = jax.random.uniform(k3, (2 * DH, DH), jnp.float32, -stdv2, stdv2)
        b1 = jax.random.uniform(k4, (2 * DH,), jnp.float32, -stdv2, stdv2)
        return {'x': x, 'W0': W0, 'b0': b0, 'W1': W1, 'b1': b1}
    _L1_attn_all = _L1_attn_setup()
    _L1_attn_in = {k: v for k, v in _L1_attn_all.items() if k in ('W0', 'b0', 'W1', 'b1')}
    del _L1_attn_all

    def _L1_ffn_setup():
        import jax, jax.numpy as jnp
        import numpy as np
        B, S, H, F, E, K = (8, 1024, 64, 128, 16, 2)
        EPS = 1e-05
        key = jax.random.key(seed)
        ks = jax.random.split(key, 9)
        sc = 0.02
        return {'x': jax.random.normal(ks[0], (B, S, H), dtype=jnp.float32), 'gate_w': jax.random.normal(ks[1], (H, E), dtype=jnp.float32) * sc, 'gate_b': jnp.zeros((E,), dtype=jnp.float32), 'w1': jax.random.normal(ks[2], (E, H, F), dtype=jnp.float32) * sc, 'b1': jnp.zeros((E, F), dtype=jnp.float32), 'w2': jax.random.normal(ks[3], (E, F, H), dtype=jnp.float32) * sc, 'b2': jnp.zeros((E, H), dtype=jnp.float32), 'gamma': jnp.ones((H,), dtype=jnp.float32), 'beta': jnp.zeros((H,), dtype=jnp.float32)}
    _L1_ffn_all = _L1_ffn_setup()
    _L1_ffn_in = {k: v for k, v in _L1_ffn_all.items() if k in ('gate_w', 'gate_b', 'w1', 'b1', 'w2', 'b2', 'gamma', 'beta')}
    del _L1_ffn_all
    return {'x': x, 'L0_tok_fc0_w': _L0_tok_in['fc0_w'], 'L0_tok_fc0_b': _L0_tok_in['fc0_b'], 'L0_tok_ln0_g': _L0_tok_in['ln0_g'], 'L0_tok_ln0_b': _L0_tok_in['ln0_b'], 'L0_tok_w1r': _L0_tok_in['w1r'], 'L0_tok_w1i': _L0_tok_in['w1i'], 'L0_tok_w2r': _L0_tok_in['w2r'], 'L0_tok_w2i': _L0_tok_in['w2i'], 'L0_tok_conv_w': _L0_tok_in['conv_w'], 'L0_tok_conv_b': _L0_tok_in['conv_b'], 'L0_tok_ln_g': _L0_tok_in['ln_g'], 'L0_tok_ln_b': _L0_tok_in['ln_b'], 'L0_tok_fc1_w': _L0_tok_in['fc1_w'], 'L0_tok_fc1_b': _L0_tok_in['fc1_b'], 'L0_tok_fc2_w': _L0_tok_in['fc2_w'], 'L0_tok_fc2_b': _L0_tok_in['fc2_b'], 'L0_tok_fc3_w': _L0_tok_in['fc3_w'], 'L0_tok_fc3_b': _L0_tok_in['fc3_b'], 'L0_attn_Wq': _L0_attn_in['Wq'], 'L0_attn_bq': _L0_attn_in['bq'], 'L0_attn_Wk': _L0_attn_in['Wk'], 'L0_attn_bk': _L0_attn_in['bk'], 'L0_attn_Wv': _L0_attn_in['Wv'], 'L0_attn_bv': _L0_attn_in['bv'], 'L0_ffn_gate_w': _L0_ffn_in['gate_w'], 'L0_ffn_gate_b': _L0_ffn_in['gate_b'], 'L0_ffn_w1': _L0_ffn_in['w1'], 'L0_ffn_b1': _L0_ffn_in['b1'], 'L0_ffn_w2': _L0_ffn_in['w2'], 'L0_ffn_b2': _L0_ffn_in['b2'], 'L1_attn_W0': _L1_attn_in['W0'], 'L1_attn_b0': _L1_attn_in['b0'], 'L1_attn_W1': _L1_attn_in['W1'], 'L1_attn_b1': _L1_attn_in['b1'], 'L1_ffn_gate_w': _L1_ffn_in['gate_w'], 'L1_ffn_gate_b': _L1_ffn_in['gate_b'], 'L1_ffn_w1': _L1_ffn_in['w1'], 'L1_ffn_b1': _L1_ffn_in['b1'], 'L1_ffn_w2': _L1_ffn_in['w2'], 'L1_ffn_b2': _L1_ffn_in['b2'], 'L1_ffn_gamma': _L1_ffn_in['gamma'], 'L1_ffn_beta': _L1_ffn_in['beta']}

def reference(x, L0_tok_fc0_w, L0_tok_fc0_b, L0_tok_ln0_g, L0_tok_ln0_b, L0_tok_w1r, L0_tok_w1i, L0_tok_w2r, L0_tok_w2i, L0_tok_conv_w, L0_tok_conv_b, L0_tok_ln_g, L0_tok_ln_b, L0_tok_fc1_w, L0_tok_fc1_b, L0_tok_fc2_w, L0_tok_fc2_b, L0_tok_fc3_w, L0_tok_fc3_b, L0_attn_Wq, L0_attn_bq, L0_attn_Wk, L0_attn_bk, L0_attn_Wv, L0_attn_bv, L0_ffn_gate_w, L0_ffn_gate_b, L0_ffn_w1, L0_ffn_b1, L0_ffn_w2, L0_ffn_b2, L1_attn_W0, L1_attn_b0, L1_attn_W1, L1_attn_b1, L1_ffn_gate_w, L1_ffn_gate_b, L1_ffn_w1, L1_ffn_b1, L1_ffn_w2, L1_ffn_b2, L1_ffn_gamma, L1_ffn_beta):
    import jax
    import jax.numpy as jnp

    def _L0_tok_ref(x, fc0_w, fc0_b, ln0_g, ln0_b, w1r, w1i, w2r, w2i, conv_w, conv_b, ln_g, ln_b, fc1_w, fc1_b, fc2_w, fc2_b, fc3_w, fc3_b):
        import jax, jax.numpy as jnp
        import numpy as np
        B, H, W = (16, 64, 64)
        WIDTH, LAYERS, M1, M2 = (32, 4, 12, 12)
        EPS = 1e-05

        def layer_norm(x, g, b):
            mu = jnp.mean(x, axis=-1, keepdims=True)
            var = jnp.mean((x - mu) ** 2, axis=-1, keepdims=True)
            return (x - mu) * jax.lax.rsqrt(var + EPS) * g + b

        def gelu(x):
            return jax.nn.gelu(x, approximate=False)

        def spectral_conv(x, w1, w2):
            b, c, h, w = x.shape
            x_ft = jnp.fft.rfft2(x)
            out_ft = jnp.zeros((b, w1.shape[1], h, w // 2 + 1), dtype=x_ft.dtype)
            out_ft = out_ft.at[:, :, :M1, :M2].set(jnp.einsum('bixy,ioxy->boxy', x_ft[:, :, :M1, :M2], w1))
            out_ft = out_ft.at[:, :, -M1:, :M2].set(jnp.einsum('bixy,ioxy->boxy', x_ft[:, :, -M1:, :M2], w2))
            return jnp.fft.irfft2(out_ft, s=(h, w))
        h = layer_norm(x @ fc0_w + fc0_b, ln0_g, ln0_b)
        h = jnp.transpose(h, (0, 3, 1, 2))
        for i in range(LAYERS):
            w1 = w1r[i] + 1j * w1i[i]
            w2 = w2r[i] + 1j * w2i[i]
            x1 = spectral_conv(h, w1, w2)
            x2 = jnp.einsum('bchw,oc->bohw', h, conv_w[i]) + conv_b[i][None, :, None, None]
            h = x1 + x2
            h = jnp.transpose(h, (0, 2, 3, 1))
            h = layer_norm(h, ln_g[i], ln_b[i])
            if i < LAYERS - 1:
                h = gelu(h)
            h = jnp.transpose(h, (0, 3, 1, 2))
        h = jnp.transpose(h, (0, 2, 3, 1))
        h = gelu(h @ fc1_w + fc1_b)
        h = gelu(h @ fc2_w + fc2_b)
        h = h @ fc3_w + fc3_b
        return h[..., 0]

    def _L0_attn_ref(x, Wq, bq, Wk, bk, Wv, bv):
        import jax, jax.numpy as jnp
        import numpy as np
        Q = jnp.einsum('bsd,de->bse', x, Wq) + bq
        K = jnp.einsum('bsd,de,->bse'.replace(',->', '->'), x, Wk) + bk
        V = jnp.einsum('bsd,de->bse', x, Wv) + bv
        scale = 1.0 / jnp.sqrt(jnp.asarray(Q.shape[-1], dtype=jnp.float32))
        scores = jnp.einsum('bqd,bkd->bqk', Q, K) * scale
        weights = jax.nn.softmax(scores, axis=-1)
        return jnp.einsum('bqk,bkd->bqd', weights, V)

    def _L0_ffn_ref(h, gate_w, gate_b, w1, b1, w2, b2):
        import math
        import jax, jax.numpy as jnp
        import numpy as np
        CAPACITY_FACTOR = 1.25
        B, L, D = h.shape
        E = gate_w.shape[1]
        T = B * L
        C = max(1, math.ceil(CAPACITY_FACTOR * T / E))
        x = h.reshape(T, D)
        logits = x @ gate_w + gate_b
        probs = jax.nn.softmax(logits, axis=-1)
        idx = jnp.argmax(probs, axis=-1)
        prb = jnp.take_along_axis(probs, idx[:, None], axis=1)[:, 0]
        one_hot = jax.nn.one_hot(idx, E, dtype=jnp.float32)
        pos = (jnp.cumsum(one_hot, axis=0) * one_hot).sum(-1).astype(jnp.int32) - 1
        kept = pos < C
        pos_safe = jnp.where(kept, pos, C)
        buf = jnp.zeros((E, C, D), dtype=h.dtype).at[idx, pos_safe].set(x, mode='drop')
        hmid = jax.nn.relu(jnp.einsum('ecd,edf->ecf', buf, w1) + b1[:, None, :])
        ybuf = jnp.einsum('ecf,efd->ecd', hmid, w2) + b2[:, None, :]
        pos_g = jnp.minimum(pos, C - 1)
        y_tok = ybuf[idx, pos_g] * (prb * kept)[:, None]
        y = y_tok.reshape(B, L, D)
        y = jnp.nan_to_num(y, nan=0.0, posinf=10000.0, neginf=-10000.0)
        return y

    def _L1_attn_ref(x, W0, b0, W1, b1):
        import jax, jax.numpy as jnp
        import numpy as np
        B, S, DIN, DH = (8, 2048, 64, 64)

        def _log_g(x):
            return jnp.where(x >= 0, jnp.log(jax.nn.relu(x) + 0.5), -jax.nn.softplus(-x))

        def _mingru_layer(x, W, b):
            gh = jnp.einsum('bsd,ed->bse', x, W) + b
            gate, hidden = jnp.split(gh, 2, axis=-1)
            log_coeffs = -jax.nn.softplus(gate)
            log_vals = -jax.nn.softplus(-gate) + _log_g(hidden)
            Bb, Ss, Dd = log_coeffs.shape
            log_h0 = jnp.full((Bb, 1, Dd), jnp.log(0.5), log_coeffs.dtype)
            log_values = jnp.concatenate([log_h0, log_vals], axis=1)
            a_star = jnp.concatenate([jnp.zeros((Bb, 1, Dd), log_coeffs.dtype), jnp.cumsum(log_coeffs, axis=1)], axis=1)
            log_h = a_star + jax.lax.cumlogsumexp(log_values - a_star, axis=1)
            return jnp.exp(log_h)[:, 1:]

        def _reference_tuple_inner(x, W0, b0, W1, b1):
            out0 = _mingru_layer(x, W0, b0)
            out1 = _mingru_layer(out0, W1, b1)
            h = jnp.stack([out0[:, -1:], out1[:, -1:]])
            return (out1, h)
        return _reference_tuple_inner(x, W0, b0, W1, b1)[0]

    def _L1_ffn_ref(x, gate_w, gate_b, w1, b1, w2, b2, gamma, beta):
        import jax, jax.numpy as jnp
        import numpy as np
        B, S, H, F, E, K = (8, 1024, 64, 128, 16, 2)
        EPS = 1e-05
        gate_logits = x @ gate_w + gate_b
        topk_vals, topk_idx = jax.lax.top_k(gate_logits, K)
        topk_w = jax.nn.softmax(topk_vals, axis=-1)
        h = jax.nn.relu(jnp.einsum('bsh,ehf->bsef', x, w1) + b1)
        expert_out = jnp.einsum('bsef,efh->bseh', h, w2) + b2
        sel = jnp.take_along_axis(expert_out, topk_idx[:, :, :, None], axis=2)
        moe = jnp.sum(topk_w[..., None] * sel, axis=2)
        y = x + moe
        mu = jnp.mean(y, axis=-1, keepdims=True)
        var = jnp.var(y, axis=-1, keepdims=True)
        return (y - mu) / jnp.sqrt(var + EPS) * gamma + beta
    h = _L0_tok_ref(x, L0_tok_fc0_w, L0_tok_fc0_b, L0_tok_ln0_g, L0_tok_ln0_b, L0_tok_w1r, L0_tok_w1i, L0_tok_w2r, L0_tok_w2i, L0_tok_conv_w, L0_tok_conv_b, L0_tok_ln_g, L0_tok_ln_b, L0_tok_fc1_w, L0_tok_fc1_b, L0_tok_fc2_w, L0_tok_fc2_b, L0_tok_fc3_w, L0_tok_fc3_b)
    h = _layernorm(h + _L0_attn_ref(h, L0_attn_Wq, L0_attn_bq, L0_attn_Wk, L0_attn_bk, L0_attn_Wv, L0_attn_bv), axis=-1)
    h = _layernorm(h + _L0_ffn_ref(h, L0_ffn_gate_w, L0_ffn_gate_b, L0_ffn_w1, L0_ffn_b1, L0_ffn_w2, L0_ffn_b2), axis=-1)
    h = _layernorm(h + _L1_attn_ref(h, L1_attn_W0, L1_attn_b0, L1_attn_W1, L1_attn_b1), axis=-1)
    h = _layernorm(h + _L1_ffn_ref(h, L1_ffn_gate_w, L1_ffn_gate_b, L1_ffn_w1, L1_ffn_b1, L1_ffn_w2, L1_ffn_b2, L1_ffn_gamma, L1_ffn_beta), axis=-1)
    return h

_drawn_inputs = setup_inputs


def setup_inputs(seed=0):
    import zlib

    import numpy as np

    out = dict(_drawn_inputs(seed))
    spreads = {'L0_tok_fc0_b': (0.0, 0.1),
     'L0_tok_ln0_g': (1.0, 0.2),
     'L0_tok_ln0_b': (0.0, 0.1),
     'L0_tok_conv_b': (0.0, 0.1),
     'L0_tok_ln_g': (1.0, 0.2),
     'L0_tok_ln_b': (0.0, 0.1),
     'L0_tok_fc1_b': (0.0, 0.1),
     'L0_tok_fc2_b': (0.0, 0.1),
     'L0_attn_bq': (0.0, 0.8),
     'L0_attn_bk': (0.0, 2.0),
     'L0_attn_bv': (0.0, 0.1),
     'L0_ffn_gate_b': (0.0, 0.1),
     'L0_ffn_b1': (0.0, 0.796),
     'L0_ffn_b2': (0.0, 0.612),
     'L1_ffn_gate_b': (0.0, 0.283),
     'L1_ffn_b1': (0.0, 0.8),
     'L1_ffn_b2': (0.0, 0.283),
     'L1_ffn_gamma': (1.0, 0.2),
     'L1_ffn_beta': (0.0, 0.1)}
    factors = {'L0_tok_w1r': 8.0,
     'L0_tok_w1i': 8.0,
     'L0_tok_w2r': 8.0,
     'L0_tok_w2i': 8.0,
     'L0_attn_Wq': 8.0,
     'L0_attn_Wk': 8.0,
     'L1_ffn_w1': 7.657,
     'L1_ffn_w2': 5.715}
    for name, (base, spread) in spreads.items():
        noise = np.random.default_rng([zlib.crc32(name.encode()), seed]).standard_normal(out[name].shape)
        drawn = base * np.exp(spread * noise) if base else spread * noise
        out[name] = jnp.asarray(drawn.astype(out[name].dtype))
    for name, factor in factors.items():
        out[name] = (out[name] * factor).astype(out[name].dtype)
    return out
```

```python
from contextlib import ExitStack

import math

import numpy as np

import concourse.bass as bass
import concourse.mybir as mybir

F32 = mybir.dt.float32
ACT = mybir.ActivationFunctionType
ALU = mybir.AluOpType
AX = mybir.AxisListType.X

P = 128
S = 64
C = 32
LAYERS = 4
M1, M2 = 12, 12
KY, KX = 2 * M1, M2
NQ = 32
EPS = 1e-5
GI = 4
NPIX = S * S
E1, F1 = 8, 256
E2, F2 = 16, 128
CAPACITY = 1.25
N_PARAMS = 18 + 16 + 12
HUGE = 3.0e38
F32_MAX = float(np.finfo(np.float32).max)

CONST_COLS = {}


def constants():
    parts, at = [], 0

    def put(name, a):
        nonlocal at
        full = np.zeros((P, a.shape[1]), np.float32)
        full[:a.shape[0]] = a
        CONST_COLS[name] = (at, a.shape[0], a.shape[1])
        parts.append(full)
        at += a.shape[1]

    y = np.arange(S)
    ang = lambda k, t: 2 * np.pi * ((k * t) % S) / S
    kys = np.array(list(range(M1)) + list(range(-M1, 0)))
    put("ident", np.eye(P))
    f1 = np.zeros((2, S, 2, NQ))
    for b in range(2):
        for q in range(M1 + 1):
            f1[b, :, b, q] = np.cos(ang(q, y))
        for q in range(1, M1 + 1):
            f1[b, :, b, M1 + q] = np.sin(ang(q, y))
    put("dft_y", f1.reshape(P, 2 * NQ))
    f2 = np.zeros((2, S, 2, KX, 4))
    for c in range(2):
        for k in range(KX):
            f2[c, :, c, k, 0] = np.cos(ang(k, y))
            f2[c, :, c, k, 1] = -np.sin(ang(k, y))
            f2[c, :, c, k, 2] = -np.sin(ang(k, y))
            f2[c, :, c, k, 3] = -np.cos(ang(k, y))
    put("dft_x", f2.reshape(P, 2, KX // 2, 2, 2, 2).transpose(0, 1, 2, 4, 3, 5).reshape(P, 2 * KX * 4))
    mc = np.zeros((GI, NQ, KY, GI))
    ms = np.zeros((GI, NQ, KY, GI))
    for b in range(GI):
        for n, k in enumerate(kys):
            mc[b, abs(k), n, b] = 1
            if k:
                ms[b, M1 + abs(k), n, b] = np.sign(k)
    put("mix_cos", mc.reshape(P, KY * GI))
    put("mix_sin", ms.reshape(P, KY * GI))
    bre = np.zeros((2, KY, 2, 2, S))
    bim = np.zeros((2, KY, 2, 2, S))
    for b in range(2):
        for n, k in enumerate(kys):
            bre[b, n, 0, b], bre[b, n, 1, b] = np.cos(ang(k, y)), -np.sin(ang(k, y))
            bim[b, n, 0, b], bim[b, n, 1, b] = np.sin(ang(k, y)), np.cos(ang(k, y))
    put("idft_y_re", bre.reshape(96, P))
    put("idft_y_im", bim.reshape(96, P))
    i2 = np.zeros((4, 2, KX, 4, 4, 16))
    for o in range(4):
        for k in range(KX):
            w = (1 if k == 0 else 2) / NPIX
            i2[o, 0, k, :, o, :] = (w * np.cos(ang(k, y))).reshape(4, 16)
            i2[o, 1, k, :, o, :] = (-w * np.sin(ang(k, y))).reshape(4, 16)
    put("idft_x", i2.reshape(96, 256))
    put("upto", np.triu(np.ones((P, P))))
    put("ones", np.ones((P, P)))
    put("falling", np.tile(np.arange(E2, 0, -1), (P, 1)))
    return np.concatenate(parts, 1).astype(np.float32)


CONSTS = constants()
NC_COLS = CONSTS.shape[1]


PER = {
    "d_out":         (14, 12, 18, 0),
    "s_out":         (10, 12, 12, 0),
    "acc":           (8, 0, 8, 8),
    "squared":       (8, 0, 8, 8),
    "summed":        (8, 0, 8, 8),
    "rstd":          (4, 0, 4, 4),
    "pool_chain":    (52, 0, 52, 52),
    "normed":        (8, 0, 8, 8),
    "turned":        (8, 0, 8, 8),
    "h_new":         (8, 0, 8, 8),
    "in_loaded":     (16, 0, 48, 48),
    "stored":        (16, 0, 16, 0),
    "y_stored":      (0, 32, 0, 0),
    "w_loaded":      (0, 16 * 16, 0, 0),
    "w_signed":      (0, 4, 0, 0),
    "y_chain":       (0, 4, 0, 0),
}


def rsqrt(eng, out, var, tmp, chain, value, done, alone):
    k = 0

    def after(ins):
        nonlocal k
        k += 1
        ins.then_inc(chain, 1)
        eng.wait_ge(chain, value(k))
        alone(eng)

    v, a, b = tmp[0][:, 0:var.shape[1]], tmp[1][:, 0:var.shape[1]], tmp[2][:, 0:var.shape[1]]
    after(eng.tensor_scalar(v, var, EPS, None, ALU.add))
    after(eng.tensor_scalar(out.bitcast(mybir.dt.int32), v.bitcast(mybir.dt.int32), -0.5, float(0x5F3759DF), ALU.mult, ALU.add))
    for step in range(2):
        after(eng.tensor_tensor(a, out, out, ALU.mult))
        after(eng.tensor_tensor(a, a, v, ALU.mult))
        after(eng.tensor_scalar(b, a, 0.375, -1.25, ALU.mult, ALU.add))
        after(eng.tensor_tensor(a, a, b, ALU.mult))
        after(eng.tensor_scalar(a, a, 1.875, None, ALU.add))
        if step == 0:
            after(eng.tensor_tensor(out, out, a, ALU.mult))
        else:
            eng.tensor_tensor(out, out, a, ALU.mult).then_inc(done, 1)


def build(nc, ins, out_ap, B, debug=None, stop=None):
    NG = B // GI
    NT = B // 2
    TOKENS = B * S
    CAP = max(1, math.ceil(CAPACITY * TOKENS / E1))
    PER["s_out"] = (10, 12, 12, 4 + 4 + 2 * 16 + 2)
    PER["d_out"] = (14, 12, 18, 16)

    def at(name, ph, L, g, n):
        f, x, m, l = PER[name]
        per_layer = x + NG * m
        if ph == "first":
            return g * f + n
        if ph == "mix":
            return NG * f + L * per_layer + n
        if ph == "mid":
            return NG * f + x + L * per_layer + g * m + n
        return NG * f + 3 * per_layer + x + g * l + n

    ctx = ExitStack()
    with ctx:
        sb = lambda name, shape: ctx.enter_context(nc.sbuf_tensor(name, shape, F32))
        pb = lambda name: ctx.enter_context(nc.psum_tensor(name, [P, 512], F32))
        sem = lambda name: ctx.enter_context(nc.semaphore(name))

        h_dram = nc.dram_tensor("h_scratch", [NG, P, 2 * 16 * P], F32, kind="Internal").ap()
        y_dram = nc.dram_tensor("y_scratch", [B, KY * 2 * KX * C], F32, kind="Internal").ap()

        cst = sb("cst", [P, NC_COLS])
        const = {k: cst[0:r, a:a + n] for k, (a, r, n) in CONST_COLS.items()}
        ident = const["ident"]
        spec = sb("spec", [P, 6 * KY * B])
        spec_v = spec[:].rearrange("p (q k b) -> p q k b", q=6, b=B)
        w_sb = sb("w_sb", [P, 2 * 2 * C * M1 * M2])
        w_v = w_sb[:].rearrange("p (w s o m) -> p w s o m", w=2, s=2, o=C)
        arena = sb("arena", [P, 9216])
        y_mix = arena[:].rearrange("p (k r x o) -> p k r x o", k=M1, r=2, x=KX)
        raw_more = sb("raw_more", [P, 3 * 512])
        raw = [arena[:, 0:512], arena[:, 512:1024]] + [raw_more[:, 512 * i:512 * i + 512] for i in range(3)]
        V = arena[:, 1024:3072]
        T = arena[:, 3072:5120]
        Xs = arena[:, 5120:6656]
        Z = [arena[:, 6656 + 768 * i:6656 + 768 * (i + 1)] for i in range(2)]
        sq = [arena[:, 8192 + 512 * i:8192 + 512 * (i + 1)] for i in range(2)]
        h_in = sb("h_in", [P, 4096])
        h_new = sb("h_new", [P, 4096])
        h_rows = sb("h_rows", [P, 4096])
        y_in = sb("y_in", [96, 768])
        conv_bd = sb("conv_bd", [P, P])
        gam = sb("gam", [P, LAYERS + 1])
        bet = sb("bet", [P, LAYERS + 1])
        small = sb("small", [P, 224])
        var = [small[:, 32 * i:32 * i + 32] for i in range(2)]
        rstd = [small[:, 64 + 32 * i:96 + 32 * i] for i in range(2)]
        newton = [small[:, 128 + 32 * i:160 + 32 * i] for i in range(3)]
        y_mean = h_in[:, 0:288]
        cbias = small[:, 0:32]
        x_in = h_in[:, 0:384].rearrange("p (t n) -> p t n", t=2)
        xT = w_sb[0:65, 0:1024].rearrange("p (t n) -> p t n", t=2)
        fc0 = w_sb[0:65, 1024:1536].rearrange("p (x o) -> p x o", x=16)
        fc0_mean = w_sb[0:65, 1536:1552]
        fc0_row = w_sb[64:65, 1600:1632]
        fc1_pad = w_sb[:, 0:512].rearrange("p (j f) -> p j f", j=4)
        fc1_b = w_sb[:, 512:513]
        fc2_w = w_sb[:, 513:577]
        fc2_b = w_sb[:, 577:578]
        fc3_w = w_sb[:, 578:580]
        fc3_b = w_sb[:, 580:581]
        G1 = [w_sb[:, 1024 + 512 * i:1536 + 512 * i] for i in range(4)]
        G2 = w_sb[:, 4096:8192].rearrange("p (n c) -> p n c", n=8)
        tok = sb("tok", [P, NT * S]) if False else w_sb[:, 8192:8192 + NT * S]

        at_col = [0]

        def param(rows, cols):
            a = at_col[0]
            at_col[0] += cols
            return spec[0:rows, a:a + cols]

        w1a, w2a = param(65, E1 * F1), param(P, E1 * F1 // P * S)
        w1b, w2b = param(65, E2 * F2), param(P, E2 * F2 // P * S)
        b2a, b2b = param(8 * E1, 512), param(8 * E2, 512)
        wq, wk, wv = param(65, S), param(65, S), param(65, S)
        gwa, gwb = param(65, E1), param(65, E2)
        wg0, wg1 = param(P, P), param(P, P)
        wg0T, wg1T = param(P, P), param(P, P)
        gbias = param(P, 4)
        ngbias = param(P, 2)
        gamma, beta = param(P, S), param(P, S)
        XT = h_rows[0:65, 0:TOKENS]
        QT, KT = arena[0:64, 0:4096], arena[0:64, 4096:8192]
        VB = h_in[0:64, :]
        Sx = h_new[:, 0:2048]
        PT = w_sb[0:64, 10240:14336]
        hid = [w_sb[:, 14336 + 512 * i:14848 + 512 * i] for i in range(8)]
        X = tok
        Y = h_new[:, 2048:4096]
        Z2 = w_sb[:, 0:2048]
        Z3 = w_sb[:, 2048:4096]
        tiny = w_sb[:, 4096:4096 + 16 * 512]
        tiny = [w_sb[:, 4096 + 512 * i:4608 + 512 * i] for i in range(8)]
        gates = arena[:, 8192:8704]
        GT = arena[:, 8704:9216]
        GA, GZ = arena[:, 0:2048], arena[:, 2048:4096]
        GS, GV = arena[:, 4096:6144], arena[:, 6144:8192]
        OUT0, OUT1 = h_in[:, 0:2048], h_in[:, 2048:4096]

        pA = [pb("pA0"), pb("pA1")]
        pT = [pb("pT0"), pb("pT1")]
        pD = [pb("pD0"), pb("pD1")]
        pS = [pb("pS0"), pb("pS1")]

        names = ["d_full", "d_free", "s_full", "s_free", "acc_full", "squared", "summed", "rstd_ok",
                 "turned", "h_new_ok", "in_loaded", "stored", "y_stored", "w_loaded",
                 "w_signed", "conv_cleared", "conv_loaded", "conv_chain", "cst_loaded", "ln_loaded",
                 "fc0_loaded", "fc0_chain", "mlp_cleared", "mlp_loaded", "y_chain", "normed", "pool_chain"]
        names += ["td_full", "td_free", "ts_full", "ts_free", "par_cleared", "par_loaded", "tok_ready", "v_chain", "shifted",
                  "exped", "e_subbed", "e_exped", "gated", "part_done", "part_used", "acc_done", "out_stored", "wg_scaled",
                  "scored", "gru_a", "gru_act", "gru_out", "ones_set", "passed"]
        s = {n: sem(n) for n in names}
        TD = [pD[0], pD[1], pA[0], pA[1]]
        TS = [pS[0], pS[1], pT[0], pT[1]]
        ctx.enter_context(nc.allow_non_contiguous_dma(reason="small parameters, once per layer"))
        block = ctx.enter_context(nc.Block())
        h_v = lambda t: t[:].rearrange("p (t q n) -> p t q n", t=2, q=16)
        hin_v, hnew_v = h_v(h_in), h_v(h_new)
        hrow_v = h_rows[:].rearrange("p (t n) -> p t n", t=2)

        LAYER1 = dict(E=E1, H=F1 // P, w1=w1a, w2=w2a, gw=gwa, b2=b2a, tiles=8)
        LAYER2 = dict(E=E2, H=F2 // P, w1=w1b, w2=w2b, gw=gwb, b2=b2b, tiles=8)

        def token_pe(pe):
            n = {"d": 0, "s": 0}
            ring = {"d": TD, "s": TS}

            def bank(which):
                pe.wait_ge(s[f"t{which}_free"], n[which] + 1)
                return ring[which][n[which] % 4]

            def sent(which, mm):
                mm.then_inc(s[f"t{which}_full"], 1)
                n[which] += 1

            def taken(which, back=0):
                pe.wait_ge(s[f"t{which}_free"], n[which] + 4 - back)

            def turn_x(stage):
                pe.wait_ge(s["tok_ready"], stage)
                for j in range(8):
                    b = bank("s")
                    for i in range(4):
                        t = 4 * j + i
                        mm = pe.transpose(b[0:64, 128 * i:128 * i + 128], X[:, S * t:S * t + S], ident)
                    sent("s", mm)
                taken("s")

            pe.wait_ge(s["par_loaded"], 16 * N_PARAMS)
            turn_x(1)
            pe.wait_ge(s["ones_set"], 1)
            for j in range(8):
                for which, w in (("d", wq), ("s", wk)):
                    b = bank(which)
                    sent(which, pe.matmul(b[0:64, :], w, XT[:, 512 * j:512 * j + 512], start=True, stop=True))
            for j in range(8):
                b = bank("d")
                for i in range(8):
                    mm = pe.matmul(b[0:64, S * i:S * i + S], XT[:, S * (8 * j + i):S * (8 * j + i + 1)], wv, start=True, stop=True)
                sent("d", mm)
            taken("d")
            taken("s")
            for j in range(4):
                b = bank("d")
                for i in range(8):
                    for h in range(2):
                        c = 128 * (8 * j + i) + 64 * h
                        mm = pe.matmul(b[64 * h:64 * h + 64, S * i:S * i + S], QT[:, c:c + 64], KT[:, c:c + 64], start=True, stop=True)
                sent("d", mm)
            for j in range(8):
                pe.wait_ge(s["exped"], j // 2 + 1)
                b = bank("s")
                for i in range(4):
                    t = 4 * j + i
                    mm = pe.transpose(b[0:64, 128 * i:128 * i + 128], Sx[:, S * t:S * t + S], ident)
                sent("s", mm)
            taken("s")
            for j in range(4):
                b = bank("d")
                for i in range(8):
                    for h in range(2):
                        c = 128 * (8 * j + i) + 64 * h
                        mm = pe.matmul(b[64 * h:64 * h + 64, S * i:S * i + S], PT[:, c:c + 64],
                                       VB[:, c:c + 64], start=True, stop=True)
                sent("d", mm)

            def experts(stage, E, H, w1, w2, gw, b2, tiles):
                turn_x(stage)
                b = bank("d")
                for t in range(NT):
                    mm = pe.matmul(b[:, E * t:E * t + E], XT[:, 128 * t:128 * t + 128], gw, start=True, stop=True)
                sent("d", mm)
                if E == E1:
                    pe.wait_ge(s["scored"], 1)
                    for lhs in ("upto", "ones"):
                        b = bank("d")
                        sent("d", pe.matmul(b[:, 0:E * NT], const[lhs], gates[:, 0:E * NT], start=True, stop=True))

                def hidden(e, k):
                    for h in range(H):
                        b = bank("s")
                        c = (e * H + h) * P
                        sent("s", pe.matmul(b[:], w1[:, c:c + P], XT[:, 512 * k:512 * k + 512], start=True, stop=True))

                def output(e, k, b):
                    for i in range(4):
                        for h in range(H):
                            slot = ((e * 8 + k) * H + h) % 8
                            mm = pe.matmul(b[:, S * (4 * (k % 2) + i):S * (4 * (k % 2) + i) + S],
                                           hid[slot][:, 128 * i:128 * i + 128], w2[:, (e * H + h) * S:(e * H + h) * S + S],
                                           start=(h == 0), stop=(h == H - 1))
                    return mm

                todo = [(e, k) for e in range(E) for k in range(8)]
                hidden(*todo[0])
                for i, (e, k) in enumerate(todo):
                    if i + 1 < len(todo):
                        hidden(*todo[i + 1])
                    taken("s", H if i + 1 < len(todo) else 0)
                    if k % 2 == 0:
                        b = bank("d")
                    mm = output(e, k, b)
                    if k % 2:
                        sent("d", mm)
                pe.wait_ge(s["gated"], 1 if E == E1 else 2)
                b = bank("s")
                for j in range(NT // 8):
                    mm = pe.transpose(b[0:8 * E, 128 * j:128 * j + 128], gates[:, 8 * E * j:8 * E * j + 8 * E], ident)
                sent("s", mm)
                taken("s")
                for j in range(NT // 8):
                    b = bank("d")
                    sent("d", pe.matmul(b[:], GT[0:8 * E, 128 * j:128 * j + 128], b2[0:8 * E, :], start=True, stop=True))

            experts(2, **LAYER1)

            b = bank("s")
            pe.transpose(b[:, 0:P], wg0, ident)
            sent("s", pe.transpose(b[:, P:2 * P], wg1, ident))
            turn_x(3)
            for n_layer in range(2):
                if n_layer == 1:
                    pe.wait_ge(s["gru_out"], 1)
                for part in range(2):
                    for j in range(4):
                        b = bank("s" if part == 0 else "d")
                        for h in range(2):
                            if n_layer == 0:
                                mm = pe.matmul(b[64 * h:64 * h + 64, :], wg0T[0:64, 64 * part:64 * part + 64],
                                               XT[0:64, 2048 * h + 512 * j:2048 * h + 512 * j + 512], start=True, stop=True)
                            else:
                                q = slice(64 * h, 64 * h + 64)
                                mm = pe.matmul(b[q, :], wg1T[q, 64 * part:64 * part + 64], OUT0[q, 512 * j:512 * j + 512],
                                               start=True, stop=True)
                        sent("s" if part == 0 else "d", mm)
            pe.wait_ge(s["gru_out"], 2)
            for j in range(4):
                b = bank("d")
                for i in range(4):
                    t = 4 * j + i
                    mm = pe.transpose(b[:, 128 * i:128 * i + 128], OUT1[:, 128 * t:128 * t + 128], ident)
                sent("d", mm)

            experts(4, **LAYER2)

        def token_act(act):
            n = [0]
            act.sem_inc(s["ts_free"], 4)

            def take():
                n[0] += 1
                act.wait_ge(s["ts_full"], n[0])
                return TS[(n[0] - 1) % 4]

            act.wait_ge(s["s_free"], at("s_out", "last", LAYERS - 1, NG, 0) + 2)
            act.sem_inc(s["tok_ready"], 1)

            def turn_x():
                for j in range(8):
                    act.copy(XT[0:64, 512 * j:512 * j + 512], take()[0:64, :]).then_inc(s["ts_free"], 1)

            turn_x()
            for j in range(8):
                act.copy(KT[:, 512 * j:512 * j + 512], take()[0:64, :]).then_inc(s["ts_free"], 1)
            for j in range(4):
                act.wait_ge(s["shifted"], j + 1)
                act.activation(Sx[:, 512 * j:512 * j + 512], Sx[:, 512 * j:512 * j + 512], ACT.Exp, scale=S ** -0.5).then_inc(s["exped"], 1)
            for j in range(8):
                act.copy(PT[:, 512 * j:512 * j + 512], take()[0:64, :]).then_inc(s["ts_free"], 1)

            def experts(E, H, **_):
                turn_x()
                act.wait_ge(s["e_subbed"], 1 if E == E1 else 2)
                m = E * NT if E == E1 else NT
                act.activation(tiny[1][:, 0:m], tiny[0][:, 0:m], ACT.Exp).then_inc(s["e_exped"], 1)
                for i in range(E * 8 * H):
                    act.activation(hid[i % 8], take()[:], ACT.Relu).then_inc(s["ts_free"], 1)
                act.copy(GT[0:8 * E, :], take()[0:8 * E, :]).then_inc(s["ts_free"], 1)

            experts(**LAYER1)
            b = take()
            act.copy(wg0T, b[:, 0:P])
            act.copy(wg1T, b[:, P:2 * P]).then_inc(s["ts_free"], 1)
            turn_x()
            act.wait_ge(s["wg_scaled"], 1)
            for layer in range(2):
                for j in range(4):
                    c = slice(512 * j, 512 * j + 512)
                    b = take()
                    act.activation(GZ[:, c], b[:], ACT.Sigmoid, bias=gbias[:, 2 * layer:2 * layer + 1])
                    act.activation(GA[:, c], b[:], ACT.Sigmoid, bias=ngbias[:, layer:layer + 1], scale=-1.0).then_inc(s["ts_free"], 1)
                for j in range(4):
                    c = slice(512 * j, 512 * j + 512)
                    act.wait_ge(s["td_full"], GRU_D[layer] + j + 1)
                    act.activation(GS[:, c], TD[(GRU_D[layer] + j) % 4][:], ACT.Sigmoid,
                                   bias=gbias[:, 2 * layer + 1:2 * layer + 2]).then_inc(s["gru_act"], 1)
            experts(**LAYER2)

        d_attn = 8 + 8 + 4 + 4
        d_ffn = 1 + 2 + E1 * 4 + NT // 8
        GRU_D = [d_attn + d_ffn, d_attn + d_ffn + 4]

        def token_dve(dve):
            n = [0]
            chain = [0]
            dve.sem_inc(s["td_free"], 4)

            def take():
                n[0] += 1
                dve.wait_ge(s["td_full"], n[0])
                return TD[(n[0] - 1) % 4]

            def link(ins):
                chain[0] += 1
                ins.then_inc(s["v_chain"], 1)
                dve.wait_ge(s["v_chain"], chain[0])

            by_tile = lambda a, w=S: a.rearrange("p (t x) -> p t x", x=w)
            wide = lambda a, w=S, m=NT: a.rearrange("p (t x) -> p t x", x=1).broadcast_to([P, m, w])

            def rsqrt_here(out, var):
                v, a, b = tiny[5][:, 0:NT], tiny[6][:, 0:NT], tiny[7][:, 0:NT]
                link(dve.tensor_scalar(v, var, EPS, None, ALU.add))
                link(dve.tensor_scalar(out.bitcast(mybir.dt.int32), v.bitcast(mybir.dt.int32), -0.5, float(0x5F3759DF), ALU.mult, ALU.add))
                for _ in range(2):
                    link(dve.tensor_tensor(a, out, out, ALU.mult))
                    link(dve.tensor_tensor(a, a, v, ALU.mult))
                    link(dve.tensor_scalar(b, a, 0.375, -1.25, ALU.mult, ALU.add))
                    link(dve.tensor_tensor(a, a, b, ALU.mult))
                    link(dve.scalar_tensor_tensor(out=out, in0=a, scalar=1.875, in1=out, op0=ALU.add, op1=ALU.mult))

            def layer_norm(x):
                mean, var, r = tiny[4][:, 0:NT], tiny[4][:, 64:64 + NT], tiny[4][:, 128:128 + NT]
                link(dve.reduce_sum(mean, by_tile(x), axis=AX))
                link(dve.scalar_tensor_tensor(out=by_tile(x), in0=wide(mean), scalar=-1.0 / S, in1=by_tile(x), op0=ALU.mult, op1=ALU.add))
                link(dve.tensor_tensor(Z2, x, x, ALU.mult))
                link(dve.reduce_sum(var, by_tile(Z2), axis=AX))
                link(dve.tensor_scalar(var, var, 1.0 / S, None, ALU.mult))
                rsqrt_here(r, var)
                link(dve.tensor_tensor(by_tile(x), by_tile(x), wide(r), ALU.mult))

            dve.wait_ge(s["par_loaded"], 16 * N_PARAMS)
            dve.memset(XT[64:65, :], 1.0).then_inc(s["ones_set"], 1)
            link(dve.tensor_scalar(ngbias, gbias.rearrange("p (l g) -> p g l", g=2)[:, 0, :], -1.0, None, ALU.mult))
            for j in range(8):
                dve.tensor_copy(QT[:, 512 * j:512 * j + 512], take()[0:64, :]).then_inc(s["td_free"], 1)
            for j in range(8):
                dve.tensor_copy(VB[:, 512 * j:512 * j + 512], take()[0:64, :]).then_inc(s["td_free"], 1)
            top, den = tiny[0][:, 0:NT], tiny[1][:, 0:NT]
            for j in range(4):
                b = take()
                m = top[:, 8 * j:8 * j + 8]
                link(dve.reduce_max(m, by_tile(b[:]), axis=AX))
                dve.tensor_tensor(by_tile(Sx[:, 512 * j:512 * j + 512]), by_tile(b[:]), wide(m, m=8), ALU.subtract).then_inc(s["shifted"], 1)
                dve.wait_ge(s["shifted"], j + 1)
                dve.sem_inc(s["td_free"], 1)
            for j in range(4):
                dve.wait_ge(s["exped"], j + 1)
                dve.reduce_sum(den[:, 8 * j:8 * j + 8], by_tile(Sx[:, 512 * j:512 * j + 512]), axis=AX)
            link(dve.memset(tiny[2][:, 0:1], 0.0))
            link(dve.reciprocal(den, den))
            for j in range(4):
                b = take()
                c = slice(512 * j, 512 * j + 512)
                dve.tensor_tensor(by_tile(Y[:, c]), by_tile(b[:]), wide(den[:, 8 * j:8 * j + 8], m=8), ALU.mult).then_inc(s["td_free"], 1)
            dve.wait_ge(s["td_free"], n[0] + 4)
            link(dve.tensor_tensor(X, X, Y, ALU.add))
            layer_norm(X)
            dve.sem_inc(s["tok_ready"], 1)

            def combine(E, tiles_y):
                for e in range(E):
                    for j in range(4):
                        b = take()
                        c = slice(512 * j, 512 * j + 512)
                        g = gates.rearrange("p (t e) -> p e t", e=E)[:, e, 8 * j:8 * j + 8] if False else None
                        gv = gates[:, 8 * E * j:8 * E * j + 8 * E].rearrange("p (t e) -> p t e", e=E)[:, :, e:e + 1].broadcast_to([P, 8, S])
                        if e == 0:
                            dve.tensor_tensor(by_tile(Y[:, c]), by_tile(b[:]), gv, ALU.mult).then_inc(s["td_free"], 1)
                        else:
                            dve.tensor_tensor(by_tile(Z3[:, c]), by_tile(b[:]), gv, ALU.mult).then_inc(s["td_free"], 1)
                            dve.wait_ge(s["td_free"], n[0] + 4)
                            dve.tensor_tensor(Y[:, c], Y[:, c], Z3[:, c], ALU.add)
                link(dve.memset(tiny[2][:, 0:1], 0.0))
                for j in range(4):
                    b = take()
                    c = slice(512 * j, 512 * j + 512)
                    dve.tensor_tensor(Y[:, c], Y[:, c], b[:], ALU.add).then_inc(s["td_free"], 1)
                dve.wait_ge(s["td_free"], n[0] + 4)

            def first_best(out, value, best, E):
                fall = const["falling"][:, E2 - E:E2].rearrange("p (t e) -> p t e", t=1).broadcast_to([P, NT, E])
                a, m = tiny[2][:, 0:E * NT], tiny[3][:, 0:NT]
                link(dve.tensor_tensor(by_tile(a, E), by_tile(value, E), wide(best, E), ALU.is_equal))
                link(dve.tensor_tensor(by_tile(a, E), by_tile(a, E), fall, ALU.mult))
                link(dve.reduce_max(m, by_tile(a, E), axis=AX))
                link(dve.tensor_tensor(by_tile(out, E), by_tile(a, E), wide(m, E), ALU.is_equal))

            E = E1
            m = E * NT
            logits, best, shifted = tiny[0][:, m:2 * m], tiny[4][:, 256:256 + NT], tiny[0][:, 0:m]
            link(dve.tensor_copy(logits, take()[:, 0:m]))
            dve.sem_inc(s["td_free"], 1)
            link(dve.reduce_max(best, by_tile(logits, E), axis=AX))
            dve.tensor_tensor(by_tile(shifted, E), by_tile(logits, E), wide(best, E), ALU.subtract).then_inc(s["e_subbed"], 1)
            first_best(gates[:, 0:m], logits, best, E)
            dve.sem_inc(s["scored"], 1)
            inclusive, totals, running, rank = tiny[5][:, 0:m], tiny[5][:, m:2 * m], tiny[6][:, 0:m], tiny[3][:, 64:64 + NT]
            link(dve.tensor_copy(inclusive, take()[:, 0:m]))
            dve.sem_inc(s["td_free"], 1)
            link(dve.tensor_copy(totals, take()[:, 0:m]))
            dve.sem_inc(s["td_free"], 1)
            for e in range(E):
                by_e = lambda a: a.rearrange("p (t e) -> p e t", e=E)[:, e, :]
                dve.tensor_tensor_scan(by_e(running), const["ones"][:, 0:NT], by_e(totals), 0.0, ALU.mult, ALU.add)
            link(dve.memset(tiny[7][:, 0:1], 0.0))
            link(dve.tensor_tensor(running, running, totals, ALU.subtract))
            link(dve.tensor_tensor(running, running, inclusive, ALU.add))
            link(dve.tensor_tensor(running, running, gates[:, 0:m], ALU.mult))
            link(dve.reduce_sum(rank, by_tile(running, E), axis=AX))
            keep, total = tiny[3][:, 128:128 + NT], tiny[3][:, 192:192 + NT]
            link(dve.tensor_scalar(keep, rank, float(CAP), None, ALU.is_le))
            dve.wait_ge(s["e_exped"], 1)
            link(dve.reduce_sum(total, by_tile(tiny[1][:, 0:m], E), axis=AX))
            link(dve.reciprocal(total, total))
            link(dve.tensor_tensor(keep, keep, total, ALU.mult))
            link(dve.tensor_tensor(by_tile(gates[:, 0:m], E), by_tile(gates[:, 0:m], E), wide(keep, E), ALU.mult))
            dve.sem_inc(s["gated"], 1)
            combine(E1, NT)
            I32 = mybir.dt.int32
            link(dve.memset(Z2, 0.0))
            link(dve.tensor_tensor(Z3.bitcast(I32), Y, Y, ALU.not_equal))
            link(dve.copy_predicated(Y, Z3.bitcast(I32), Z2))
            link(dve.memset(Z2, 1.0e4))
            link(dve.tensor_scalar(Z3.bitcast(I32), Y, F32_MAX, None, ALU.is_gt))
            link(dve.copy_predicated(Y, Z3.bitcast(I32), Z2))
            link(dve.memset(Z2, -1.0e4))
            link(dve.tensor_scalar(Z3.bitcast(I32), Y, -F32_MAX, None, ALU.is_lt))
            link(dve.copy_predicated(Y, Z3.bitcast(I32), Z2))
            link(dve.tensor_tensor(X, X, Y, ALU.add))
            layer_norm(X)
            dve.sem_inc(s["wg_scaled"], 1)
            dve.sem_inc(s["tok_ready"], 1)

            for layer in range(2):
                for j in range(4):
                    c = slice(512 * j, 512 * j + 512)
                    b = take()
                    dve.wait_ge(s["gru_act"], 4 * layer + j + 1)
                    link(dve.tensor_scalar(GV[:, c], b[:], gbias[:, 2 * layer + 1:2 * layer + 2], 0.5, ALU.add, ALU.add))
                    dve.sem_inc(s["td_free"], 1)
                    link(dve.tensor_tensor(GV[:, c], GV[:, c], GS[:, c], ALU.max))
                    link(dve.tensor_tensor(GV[:, c], GV[:, c], GZ[:, c], ALU.mult))
                head = lambda a: a.rearrange("p (b t) -> p b t", t=S)[:, :, 0]
                link(dve.scalar_tensor_tensor(out=head(GV), in0=head(GA), scalar=0.5, in1=head(GV), op0=ALU.mult, op1=ALU.add))
                link(dve.memset(head(GA), 0.0))
                dve.tensor_tensor_scan((OUT0, OUT1)[layer], GA, GV, 0.0, ALU.mult, ALU.add).then_inc(s["gru_out"], 1)
            xv = X.rearrange("p (h t x) -> p t h x", h=2, x=S)
            for j in range(4):
                b = take()
                dve.tensor_tensor(xv[:, 4 * j:4 * j + 4], xv[:, 4 * j:4 * j + 4],
                                  b[:].rearrange("p (t h x) -> p t h x", h=2, x=S), ALU.add).then_inc(s["td_free"], 1)
            dve.wait_ge(s["td_free"], n[0] + 4)
            layer_norm(X)
            dve.sem_inc(s["tok_ready"], 1)

            E = E2
            m = E * NT
            logits, best, second = tiny[2][:, 0:m], tiny[4][:, 256:256 + NT], tiny[4][:, 320:320 + NT]
            logits = Z2[:, 0:m]
            rest = Z2[:, m:2 * m]
            pick1, pick2 = Z2[:, 2 * m:3 * m], Z2[:, 3 * m:4 * m]
            link(dve.tensor_copy(logits, take()[:, 0:m]))
            dve.sem_inc(s["td_free"], 1)
            link(dve.reduce_max(best, by_tile(logits, E), axis=AX))
            first_best(pick1, logits, best, E)
            link(dve.scalar_tensor_tensor(out=rest, in0=pick1, scalar=-HUGE, in1=logits, op0=ALU.mult, op1=ALU.add))
            link(dve.reduce_max(second, by_tile(rest, E), axis=AX))
            dve.tensor_tensor(tiny[0][:, 0:NT], second, best, ALU.subtract).then_inc(s["e_subbed"], 1)
            first_best(pick2, rest, second, E)
            dve.wait_ge(s["e_exped"], 2)
            ex, inv = tiny[1][:, 0:NT], tiny[3][:, 64:64 + NT]
            link(dve.tensor_scalar(inv, ex, 1.0, None, ALU.add))
            link(dve.reciprocal(inv, inv))
            link(dve.tensor_tensor(by_tile(pick1, E), by_tile(pick1, E), wide(inv, E), ALU.mult))
            link(dve.tensor_tensor(inv, inv, ex, ALU.mult))
            link(dve.tensor_tensor(by_tile(pick2, E), by_tile(pick2, E), wide(inv, E), ALU.mult))
            link(dve.tensor_tensor(gates[:, 0:m], pick1, pick2, ALU.add))
            dve.sem_inc(s["gated"], 1)
            combine(E2, NT)
            link(dve.tensor_tensor(Y, Y, X, ALU.add))
            layer_norm(Y)
            g_t = lambda a: a.rearrange("p (t x) -> p t x", t=1).broadcast_to([P, NT, S])
            link(dve.tensor_tensor(by_tile(Y), by_tile(Y), g_t(gamma), ALU.mult))
            link(dve.tensor_tensor(by_tile(Y), by_tile(Y), g_t(beta), ALU.add))
            link(dve.tensor_tensor(X, X, Y, ALU.add))
            layer_norm(X)
            dve.sem_inc(s["acc_done"], 1)

        def token_pool(pool):
            pass

        def alone(eng):
            eng.sem_inc(s["passed"], 1)

        def phases(eng, mix, group):
            with eng.Fori(0, NG) as g:
                group("first", 0, g)
            with eng.Fori(0, LAYERS - 1) as L:
                mix(L)
                with eng.Fori(0, NG) as g:
                    group("mid", L, g)
            mix(LAYERS - 1)
            with eng.Fori(0, NG) as g:
                group("last", LAYERS - 1, g)

        @block.sync
        def _(sp):
            sp.dma_start(cst[:], ins["consts"]).then_inc(s["cst_loaded"], 16)
            for j in range(4):
                q = slice(32 * j, 32 * j + 32)
                sp.dma_start(gam[q, 0:1], ins["L0_tok_ln0_g"].rearrange("(p o) -> p o", o=1)).then_inc(s["ln_loaded"], 16)
                sp.dma_start(bet[q, 0:1], ins["L0_tok_ln0_b"].rearrange("(p o) -> p o", o=1)).then_inc(s["ln_loaded"], 16)
                for L in range(LAYERS):
                    sp.dma_start(gam[q, L + 1:L + 2], ins["L0_tok_ln_g"][L].rearrange("(p o) -> p o", o=1)).then_inc(s["ln_loaded"], 16)
                    sp.dma_start(bet[q, L + 1:L + 2], ins["L0_tok_ln_b"][L].rearrange("(p o) -> p o", o=1)).then_inc(s["ln_loaded"], 16)
            sp.wait_ge(s["fc0_chain"], 1)
            for x in range(16):
                sp.dma_start(fc0[3 * x:3 * x + 3, x, :], ins["L0_tok_fc0_w"]).then_inc(s["fc0_loaded"], 16)
            sp.dma_start(fc0_row, ins["L0_tok_fc0_b"].rearrange("(p o) -> p o", p=1)).then_inc(s["fc0_loaded"], 16)

            def load_first(g):
                src = ins["x"].rearrange("(g t b) y x c -> g (b y) t (x c)", t=2, b=2)
                sp.dma_start(x_in, src[g]).then_inc(s["in_loaded"], 16)

            def store(ph, L, g):
                sp.wait_ge(s["h_new_ok"], at("h_new", ph, L, g, 8))
                sp.dma_start(h_dram[g], h_new[:]).then_inc(s["stored"], 16)

            def load_group(g):
                sp.dma_start(h_in[:], h_dram[g]).then_inc(s["in_loaded"], 16)
                for t in range(2):
                    src = y_dram.rearrange("(g t b) (k n) -> g t (b k) n", t=2, b=2, k=2 * KY)
                    sp.dma_start(y_in[:, 384 * t:384 * t + 384], src[g, t]).then_inc(s["in_loaded"], 16)

            def weights(L):
                for w, (wr, wi) in enumerate((("L0_tok_w1r", "L0_tok_w1i"), ("L0_tok_w2r", "L0_tok_w2i"))):
                    for k in range(2):
                        for r in range(2):
                            q = slice(64 * k + 32 * r, 64 * k + 32 * r + 32)
                            for slot in range(2):
                                name = wr if slot == r else wi
                                sp.dma_start(w_v[q, w, slot].rearrange("p o m -> p (o m)"),
                                             ins[name][L].rearrange("i o x y -> i (o x y)")).then_inc(s["w_loaded"], 16)

            def conv_params(L):
                sp.wait_ge(s["conv_cleared"], 1)
                sp.wait_ge(s["acc_full"], at("acc", "mix", L, 0, 0))
                for j in range(4):
                    sp.dma_start(conv_bd[32 * j:32 * j + 32, 32 * j:32 * j + 32],
                                 ins["L0_tok_conv_w"][L].rearrange("o c -> c o")).then_inc(s["conv_loaded"], 16)
                sp.wait_ge(s["rstd_ok"], at("rstd", "mix", L, 0, 0))
                sp.dma_start(cbias[0:B, :], ins["L0_tok_conv_b"][L].partition_broadcast(B)).then_inc(s["conv_loaded"], 16)

            def y_store(L):
                sp.wait_ge(s["y_chain"], at("y_chain", "mix", L, 0, 4))
                for w in range(2):
                    dst = y_dram.rearrange("b (w n) -> w b n", w=2)[w]
                    sp.dma_start(dst, arena[64 * w:64 * w + B, :]).then_inc(s["y_stored"], 16)
                sp.wait_ge(s["y_stored"], at("y_stored", "mix", L, 0, 32))

            def token_params():
                sp.wait_ge(s["par_cleared"], 1)
                col = lambda a: a.rearrange("(p o) -> p o", o=1)
                row = lambda a: a.rearrange("(o n) -> o n", o=1)
                dmas = [
                    (wq[0:64], ins["L0_attn_Wq"]), (wq[64:65], row(ins["L0_attn_bq"])),
                    (wk[0:64], ins["L0_attn_Wk"]), (wk[64:65], row(ins["L0_attn_bk"])),
                    (wv[0:64], ins["L0_attn_Wv"]), (wv[64:65], row(ins["L0_attn_bv"])),
                    (gwa[0:64], ins["L0_ffn_gate_w"]), (gwa[64:65], row(ins["L0_ffn_gate_b"])),
                    (gwb[0:64], ins["L1_ffn_gate_w"]), (gwb[64:65], row(ins["L1_ffn_gate_b"])),
                    (w1a[0:64].rearrange("d (e f) -> d e f", e=E1), ins["L0_ffn_w1"].rearrange("e d f -> d e f")),
                    (w1a[64:65], row(ins["L0_ffn_b1"].rearrange("e f -> (e f)"))),
                    (w2a.rearrange("p (e d) -> p e d", d=S), ins["L0_ffn_w2"].rearrange("e (h p) d -> p (e h) d", p=P)),
                    (w1b[0:64].rearrange("d (e f) -> d e f", e=E2), ins["L1_ffn_w1"].rearrange("e d f -> d e f")),
                    (w1b[64:65], row(ins["L1_ffn_b1"].rearrange("e f -> (e f)"))),
                    (w2b.rearrange("p (e d) -> p e d", d=S), ins["L1_ffn_w2"].rearrange("e p d -> p e d")),
                    (gamma, ins["L1_ffn_gamma"].partition_broadcast(P)), (beta, ins["L1_ffn_beta"].partition_broadcast(P)),
                ]
                for i in range(8):
                    dmas.append((b2a[E1 * i:E1 * i + E1, S * i:S * i + S], ins["L0_ffn_b2"]))
                    dmas.append((b2b[E2 * i:E2 * i + E2, S * i:S * i + S], ins["L1_ffn_b2"]))
                for i in range(2):
                    dmas.append((wg0[:, S * i:S * i + S], ins["L1_attn_W0"]))
                    dmas.append((wg1[:, S * i:S * i + S], ins["L1_attn_W1"]))
                    q = slice(64 * i, 64 * i + 64)
                    for n, b in enumerate(("L1_attn_b0", "L1_attn_b1")):
                        for part in range(2):
                            dmas.append((gbias[q, 2 * n + part:2 * n + part + 1], col(ins[b][S * part:S * part + S])))
                assert len(dmas) == N_PARAMS
                for dst, src in dmas:
                    sp.dma_start(dst, src).then_inc(s["par_loaded"], 16)

            load_first(0)
            with sp.Fori(0, NG - 1) as g:
                sp.wait_ge(s["s_full"], at("s_out", "first", 0, g, 2))
                load_first(g + 1)
                store("first", 0, g)
            store("first", 0, NG - 1)
            weights(0)

            with sp.Fori(0, LAYERS - 1) as L:
                conv_params(L)
                y_store(L)
                sp.wait_ge(s["stored"], at("stored", "mix", L, 0, 0) + 16)
                load_group(0)
                weights(L + 1)
                with sp.Fori(0, NG - 1) as g:
                    sp.wait_ge(s["acc_full"], at("acc", "mid", L, g, 8))
                    load_group(g + 1)
                    store("mid", L, g)
                store("mid", L, NG - 1)
            L = LAYERS - 1
            conv_params(L)
            y_store(L)
            token_params()
            sp.wait_ge(s["mlp_cleared"], 1)
            for j in range(4):
                sp.dma_start(fc1_pad[32 * j:32 * j + 32, j, :], ins["L0_tok_fc1_w"]).then_inc(s["mlp_loaded"], 16)
            sp.dma_start(fc1_b, ins["L0_tok_fc1_b"].rearrange("(p o) -> p o", o=1)).then_inc(s["mlp_loaded"], 16)
            sp.dma_start(fc2_w, ins["L0_tok_fc2_w"]).then_inc(s["mlp_loaded"], 16)
            for j in range(2):
                q = slice(64 * j, 64 * j + 64)
                sp.dma_start(fc2_b[q], ins["L0_tok_fc2_b"].rearrange("(p o) -> p o", o=1)).then_inc(s["mlp_loaded"], 16)
                sp.dma_start(fc3_w[q, j:j + 1], ins["L0_tok_fc3_w"]).then_inc(s["mlp_loaded"], 16)
            sp.dma_start(fc3_b, ins["L0_tok_fc3_b"].partition_broadcast(P)).then_inc(s["mlp_loaded"], 16)
            sp.wait_ge(s["stored"], at("stored", "last", L, 0, 0) + 16)
            load_group(0)
            with sp.Fori(0, NG - 1) as g:
                sp.wait_ge(s["acc_full"], at("acc", "last", L, g, 8))
                load_group(g + 1)
            sp.wait_ge(s["acc_done"], 1)
            sp.dma_start(out_ap.rearrange("(t b) y x -> (b y) t x", b=2), X.rearrange("p (t x) -> p t x", x=S)).then_inc(s["out_stored"], 16)
            sp.wait_ge(s["out_stored"], 16)

        @block.gpsimd
        def _(pool):
            def mix(L):
                pool.wait_ge(s["w_loaded"], at("w_loaded", "mix", L, 0, 256))
                pool.wait_ge(s["rstd_ok"], at("rstd", "mix", L, 0, 0))
                alone(pool)
                for w in range(2):
                    for k in range(2):
                        v = w_v[64 * k + 32:64 * k + 64, w, 0].rearrange("p o m -> p (o m)")
                        pool.tensor_scalar(v, v, -1.0, None, ALU.mult).then_inc(s["w_signed"], 1)
                        pool.wait_ge(s["w_signed"], at("w_signed", "mix", L, 0, 2 * w + k + 1))
                        alone(pool)
                if isinstance(L, int):
                    pool.wait_ge(s["s_full"], at("s_out", "mix", L, 0, 12))
                    pool.memset(w_sb[:, 0:1024], 0.0).then_inc(s["mlp_cleared"], 1)
                    pool.wait_ge(s["mlp_cleared"], 1)

                    pool.memset(spec[:, 0:at_col[0]], 0.0).then_inc(s["par_cleared"], 1)
                    pool.wait_ge(s["par_cleared"], 1)

            def group(ph, L, g):
                for m in range(4):
                    pool.wait_ge(s["summed"], at("summed", ph, L, g, 2 * m + 2))
                    alone(pool)
                    rsqrt(pool, rstd[m % 2], var[m % 2], newton, s["pool_chain"],
                          lambda k: at("pool_chain", ph, L, g, 13 * m + k), s["rstd_ok"], alone)

            phases(pool, mix, group)
            token_pool(pool)

        @block.tensor
        def _(pe):
            def ring_d(ph, L, g, k):
                pe.wait_ge(s["d_free"], at("d_out", ph, L, g, k + 1))
                return pD[k % 2]

            def ring_s(ph, L, g, k):
                pe.wait_ge(s["s_free"], at("s_out", ph, L, g, k + 1))
                return pS[k % 2]

            pe.wait_ge(s["cst_loaded"], 16)

            def mix(L):
                pe.wait_ge(s["w_signed"], at("w_signed", "mix", L, 0, 4))
                pe.wait_ge(s["d_free"], at("d_out", "mix", L, 0, 2))
                for q in range(6):
                    for half in range(2):
                        k0 = 2 * q + half
                        banks = [ring_d("mix", L, 0, k0), ring_s("mix", L, 0, k0)]
                        alone(pe)
                        for j in range(6):
                            for par in range(2):
                                for w in range(2):
                                    rows = slice(64 * par, 64 * par + 64)
                                    mm = pe.matmul(
                                        banks[par][64 * w:64 * w + B, 64 * j:64 * j + 64],
                                        spec_v[rows, q, 12 * w + 6 * half + j, :],
                                        w_v[rows, w, :, :, (6 * half + j) * M2 + 2 * q + par],
                                        start=True, stop=True)
                                    if j == 5 and w == 1:
                                        mm.then_inc(s["d_full" if par == 0 else "s_full"], 1)

            def group(ph, L, g):
                d = 0
                r = 0
                pe.wait_ge(s["in_loaded"], at("in_loaded", ph, L, g, 16 if ph == "first" else 48))
                if ph == "first":
                    for t in range(2):
                        bank = ring_s(ph, L, g, r)
                        alone(pe)
                        for xb in range(4):
                            mm = pe.transpose(bank[0:48, 128 * xb:128 * xb + 128], x_in[:, t, 48 * xb:48 * xb + 48], ident)
                        mm.then_inc(s["s_full"], 1)
                        r += 1
                    pe.wait_ge(s["fc0_chain"], 4)
                else:
                    for t in range(2):
                        for part in ("idft_y_re", "idft_y_im"):
                            if ph == "mid":
                                bank = ring_d(ph, L, g, d)
                                d += 1
                            else:
                                bank = ring_s(ph, L, g, r)
                                r += 1
                            mm = pe.matmul(bank[:, 0:384], const[part], y_in[:, 384 * t:384 * t + 384], start=True, stop=True)
                            mm.then_inc(s["d_full" if ph == "mid" else "s_full"], 1)
                    for t in range(2):
                        for half in range(2):
                            bank = ring_s(ph, L, g, r)
                            if half == 0:
                                if ph == "mid":
                                    pe.wait_ge(s["d_free"], at("d_out", ph, L, g, 2 * t + 2) + 2)
                                else:
                                    pe.wait_ge(s["s_free"], at("s_out", ph, L, g, 2 * t + 2) + 2)
                            for j in range(4):
                                o = 4 * half + j
                                mm = pe.transpose(bank[0:96, 128 * j:128 * j + 128], Z[t][:, 96 * o:96 * o + 96], ident)
                            mm.then_inc(s["s_full"], 1)
                            r += 1

                def accumulate(n):
                    t, xb = n // 4, n % 4
                    pe.wait_ge(s["squared"], at("squared", ph, L, g, n + 1))
                    bank = pA[n % 2]
                    if ph == "first":
                        if xb == 0:
                            pe.wait_ge(s["s_free"], at("s_out", ph, L, g, t + 1) + 2)
                        mm = pe.matmul(bank[:], xT[:, t, 128 * xb:128 * xb + 128],
                                       w_sb[0:65, 1024:1536], start=True, stop=True)
                    else:
                        if n == 0:
                            pe.wait_ge(s["conv_chain"], 2 * L + 2)
                        if xb == 0:
                            base = 2 * t + 2 if ph == "mid" else 4 + 2 * t + 2
                            pe.wait_ge(s["s_free"], at("s_out", ph, L, g, base) + 2)
                        out = bank[:].rearrange("p (x o) -> p o x", x=16)
                        for j in range(4):
                            pe.matmul(bank[:, 128 * j:128 * j + 128], hin_v[:, t, 4 * xb + j, :], conv_bd[:],
                                      start=(j == 0), stop=False, skip_group_check=True)
                        for o in range(8):
                            mm = pe.matmul(out[:, 4 * o:4 * o + 4, :],
                                           T[0:96, 1024 * t + 128 * o:1024 * t + 128 * o + 128],
                                           const["idft_x"][:, 64 * xb:64 * xb + 64],
                                           start=False, stop=(o == 7), skip_group_check=True)
                    mm.then_inc(s["acc_full"], 1)

                def turn(n):
                    pe.wait_ge(s["normed"], at("normed", ph, L, g, n + 1))
                    if n >= 2:
                        pe.wait_ge(s["h_new_ok"], at("h_new", ph, L, g, n - 1))
                    for j in range(4):
                        mm = pe.transpose(pT[n % 2][:, 128 * j:128 * j + 128], raw[n % 5][:, 128 * j:128 * j + 128], ident)
                    mm.then_inc(s["turned"], 1)

                def back(n):
                    nonlocal d
                    t, xb = n // 4, n % 4
                    pe.wait_ge(s["h_new_ok"], at("h_new", ph, L, g, n + 1))
                    bank = ring_d(ph, L, g, d)
                    for j in range(4):
                        mm = pe.transpose(bank[:, 128 * j:128 * j + 128], hnew_v[:, t, 4 * xb + j, :], ident)
                    mm.then_inc(s["d_full"], 1)
                    d += 1

                def fc12(n):
                    nonlocal r, d
                    t, xb = n // 4, n % 4
                    if n == 0:
                        pe.wait_ge(s["mlp_loaded"], 16 * 11)
                    pe.wait_ge(s["h_new_ok"], at("h_new", ph, L, g, n + 1))
                    for j in range(4):
                        bank = ring_s(ph, L, g, r)
                        mm = pe.matmul(bank[:], fc1_pad[:, j, :],
                                       hnew_v[:, t, 4 * xb:4 * xb + 4, :].rearrange("p a b -> p (a b)"), start=True, stop=True)
                        mm.then_inc(s["s_full"], 1)
                        r += 1
                    for jj in range(2):
                        bank = ring_d(ph, L, g, d)
                        pe.wait_ge(s["s_free"], at("s_out", ph, L, g, r - 2 + 2 * jj) + 2)
                        for j in range(2):
                            mm = pe.matmul(bank[64 * j:64 * j + 64, :], fc2_w, G1[2 * jj + j], start=True, stop=True)
                        mm.then_inc(s["d_full"], 1)
                        d += 1

                def fc3(t):
                    nonlocal r
                    bank = ring_s(ph, L, g, r)
                    pe.wait_ge(s["d_free"], at("d_out", ph, L, g, 8 * t + 8) + 2)
                    for xq in range(16):
                        for jj in range(2):
                            mm = pe.matmul(bank[:, 4 * xq + 2 * jj:4 * xq + 2 * jj + 2],
                                           G2[:, 2 * (xq // 4) + jj, 128 * (xq % 4):128 * (xq % 4) + 128],
                                           fc3_w, start=True, stop=True)
                    mm.then_inc(s["s_full"], 1)
                    r += 1

                use = back if ph != "last" else fc12
                for n in range(13):
                    if n < 8:
                        accumulate(n)
                    if 4 <= n <= 11:
                        turn(n - 4)
                    if n >= 5:
                        use(n - 5)
                        if ph == "last" and n in (8, 12):
                            fc3((n - 5) // 4)
                if ph == "last":
                    return
                for k in range(4):
                    bank = ring_s(ph, L, g, r)
                    pe.wait_ge(s["d_free"], at("d_out", ph, L, g, d - 3 + k) + 2)
                    for t in range(2):
                        mm = pe.matmul(bank[64 * t:64 * t + 64, :], const["dft_y"], hrow_v[:, t, 512 * k:512 * k + 512],
                                       start=True, stop=True)
                    mm.then_inc(s["s_full"], 1)
                    r += 1
                pe.wait_ge(s["s_free"], at("s_out", ph, L, g, r) + 2)
                for k in range(4):
                    bank = ring_d(ph, L, g, d)
                    for j in range(4):
                        c = 2 * (4 * k + j)
                        mm = pe.transpose(bank[:, 128 * j:128 * j + 128], V[:, S * c:S * c + 128], ident)
                    mm.then_inc(s["d_full"], 1)
                    d += 1
                for k in range(4):
                    bank = ring_s(ph, L, g, r)
                    pe.wait_ge(s["d_free"], at("d_out", ph, L, g, d - 3 + k) + 2)
                    for j in range(4):
                        mm = pe.matmul(bank[:, 96 * j:96 * j + 96], T[:, 128 * (4 * k + j):128 * (4 * k + j) + 128],
                                       const["dft_x"], start=True, stop=True)
                    mm.then_inc(s["s_full"], 1)
                    r += 1
                pe.wait_ge(s["s_free"], at("s_out", ph, L, g, r) + 2)
                for k in range(2):
                    bank = ring_d(ph, L, g, d)
                    for j in range(3):
                        q = 3 * k + j
                        o = bank[:, 96 * j:96 * j + 96]
                        pe.matmul(o, Xs[:, 256 * q:256 * q + 128], const["mix_cos"], start=True, stop=False)
                        mm = pe.matmul(o, Xs[:, 256 * q + 128:256 * q + 256], const["mix_sin"], start=False, stop=True)
                    mm.then_inc(s["d_full"], 1)
                    d += 1

            phases(pe, mix, group)
            token_pe(pe)

        @block.scalar
        def _(act):
            act.sem_inc(s["s_free"], 2)
            act.sem_inc(s["squared"], 2)
            act.sem_inc(s["stored"], 16)
            act.wait_ge(s["ln_loaded"], 16 * 4 * 2 * (LAYERS + 1))

            def take(ph, L, g, k):
                act.wait_ge(s["s_full"], at("s_out", ph, L, g, k + 1))
                return pS[k % 2]

            def mix(L):
                for k in range(12):
                    bank = take("mix", L, 0, k)
                    q, half = k // 2, k % 2
                    src = bank[:, 0:384].rearrange("p (k r o) -> p k r o", k=6, r=2)
                    act.copy(y_mix[:, 6 * half:6 * half + 6, :, 2 * q + 1, :], src).then_inc(s["s_free"], 1)

            def group(ph, L, g):
                r = 0
                if ph == "first":
                    for t in range(2):
                        bank = take(ph, L, g, r)
                        act.copy(xT[0:48, t, :], bank[0:48, :]).then_inc(s["s_free"], 1)
                        r += 1
                else:
                    if ph == "last":
                        for t in range(2):
                            for ri in range(2):
                                bank = take(ph, L, g, r)
                                act.copy(Z[t].rearrange("p (o r k) -> p r k o", o=C, r=2)[:, ri],
                                         bank[:, 0:384].rearrange("p (k o) -> p k o", o=C)).then_inc(s["s_free"], 1)
                                r += 1
                    for t in range(2):
                        for half in range(2):
                            bank = take(ph, L, g, r)
                            act.copy(T[0:96, 1024 * t + 512 * half:1024 * t + 512 * half + 512], bank[0:96, :]).then_inc(s["s_free"], 1)
                            r += 1

                def square(n):
                    act.wait_ge(s["acc_full"], at("acc", ph, L, g, n + 1))
                    act.copy(raw[n % 5], pA[n % 2][:])
                    if n >= 2:
                        act.wait_ge(s["summed"], at("summed", ph, L, g, n - 1))
                    act.activation(sq[n % 2], pA[n % 2][:], ACT.Square, scale=float(C) ** -0.5).then_inc(s["squared"], 1)

                def finish(n):
                    act.wait_ge(s["turned"], at("turned", ph, L, g, n + 1))
                    if n == 0 and ph != "last":
                        act.wait_ge(s["stored"], at("stored", ph, L, g, 0) + 16)
                    if n == 0 and ph == "last":
                        act.wait_ge(s["stored"], at("stored", ph, L, 0, 0) + 16)
                    alone(act)
                    col = 0 if ph == "first" else lay
                    act.activation(h_new[:, 512 * n:512 * n + 512], pT[n % 2][:], ACT.Gelu if ph == "mid" else ACT.Identity,
                                   bias=bet[:, col:col + 1] if ph != "mid" else bet[:, bass.ds(L + 1, 1)],
                                   scale=gam[:, col:col + 1] if ph != "mid" else gam[:, bass.ds(L + 1, 1)]).then_inc(s["h_new_ok"], 1)

                lay = LAYERS

                def gelus(n):
                    nonlocal r
                    for j in range(4):
                        bank = take(ph, L, g, r)
                        if n == 0 and j == 0:
                            act.wait_ge(s["mlp_loaded"], 16 * 11)
                        act.activation(G1[j], bank[:], ACT.Gelu, bias=fc1_b).then_inc(s["s_free"], 1)
                        r += 1
                    for jj in range(2):
                        k = 2 * n + jj
                        act.wait_ge(s["d_full"], at("d_out", ph, L, g, k + 1))
                        act.activation(G2[:, 2 * (n % 4) + jj, :], pD[k % 2][:], ACT.Gelu, bias=fc2_b).then_inc(s["d_free"], 1)

                for n in range(13):
                    if n < 8:
                        square(n)
                    if 4 <= n <= 11:
                        finish(n - 4)
                    if ph == "last" and n >= 5:
                        gelus(n - 5)
                        if n in (8, 12):
                            t = (n - 5) // 4
                            bank = take(ph, L, g, r)
                            act.activation(tok[:, bass.ds(g * 128 + 64 * t, 64)], bank[:, 0:64], ACT.Identity,
                                           bias=fc3_b).then_inc(s["s_free"], 1)
                            r += 1
                if ph == "last":
                    return
                for k in range(4):
                    bank = take(ph, L, g, r)
                    act.copy(V.rearrange("p (c x) -> p c x", x=S)[:, :, 16 * k:16 * k + 16],
                             bank[:].rearrange("p (x c) -> p c x", c=C)).then_inc(s["s_free"], 1)
                    r += 1
                for k in range(4):
                    bank = take(ph, L, g, r)
                    act.copy(Xs.rearrange("p (j c) -> p j c", c=C)[:, :, 8 * k:8 * k + 8],
                             bank[:, 0:384].rearrange("p (c j) -> p j c", j=48)).then_inc(s["s_free"], 1)
                    r += 1

            phases(act, mix, group)
            token_act(act)

        @block.vector
        def _(dve):
            dve.sem_inc(s["d_free"], 2)
            pass
            dve.memset(conv_bd[:], 0.0).then_inc(s["conv_cleared"], 1)
            dve.memset(w_sb[0:64, 0:2048], 0.0)
            dve.memset(w_sb[64:65, 0:1024], 1.0)
            dve.memset(w_sb[64:65, 1024:2048], 0.0).then_inc(s["fc0_chain"], 1)
            dve.wait_ge(s["fc0_loaded"], 16 * 17)
            dve.tensor_copy(fc0[64:65], fc0_row.rearrange("p (x o) -> p x o", x=1).broadcast_to([1, 16, C])).then_inc(s["fc0_chain"], 1)
            dve.wait_ge(s["fc0_chain"], 2)
            dve.reduce_sum(fc0_mean, fc0, axis=AX).then_inc(s["fc0_chain"], 1)
            dve.wait_ge(s["fc0_chain"], 3)
            dve.scalar_tensor_tensor(out=fc0, in0=fc0_mean.rearrange("p (x o) -> p x o", o=1).broadcast_to([65, 16, C]),
                                     scalar=-1.0 / C, in1=fc0, op0=ALU.mult, op1=ALU.add).then_inc(s["fc0_chain"], 1)

            def take(ph, L, g, k):
                dve.wait_ge(s["d_full"], at("d_out", ph, L, g, k + 1))
                return pD[k % 2]

            def mix(L):
                dve.wait_ge(s["conv_loaded"], 80 * L + 80)
                cv = conv_bd[:].rearrange("p (x o) -> p x o", x=4)
                cm = small[:, 64:68]
                dve.reduce_sum(cm, cv, axis=AX)
                dve.reduce_sum(small[0:B, 68:69], cbias[0:B, :], axis=AX).then_inc(s["conv_chain"], 1)
                dve.wait_ge(s["conv_chain"], 2 * L + 1)
                dve.scalar_tensor_tensor(out=cv, in0=cm.rearrange("p (x o) -> p x o", o=1).broadcast_to([P, 4, C]),
                                         scalar=-1.0 / C, in1=cv, op0=ALU.mult, op1=ALU.add)
                dve.scalar_tensor_tensor(out=cbias[0:B, :], in0=small[0:B, 68:69].broadcast_to([B, C]),
                                         scalar=-1.0 / C, in1=cbias[0:B, :], op0=ALU.mult, op1=ALU.add).then_inc(s["conv_chain"], 1)
                for k in range(12):
                    bank = take("mix", L, 0, k)
                    q, half = k // 2, k % 2
                    src = bank[:, 0:384].rearrange("p (k r o) -> p k r o", k=6, r=2)
                    dve.tensor_copy(y_mix[:, 6 * half:6 * half + 6, :, 2 * q, :], src).then_inc(s["d_free"], 1)
                dve.wait_ge(s["s_free"], at("s_out", "mix", L, 0, 12) + 2)
                dve.wait_ge(s["d_free"], at("d_out", "mix", L, 0, 12) + 2)
                yv = arena[:].rearrange("p (n o) -> p n o", o=C)
                dve.reduce_sum(y_mean, yv, axis=AX).then_inc(s["y_chain"], 1)
                dve.wait_ge(s["y_chain"], at("y_chain", "mix", L, 0, 1))
                dve.scalar_tensor_tensor(out=yv, in0=y_mean.rearrange("p (n o) -> p n o", o=1).broadcast_to([P, 288, C]),
                                         scalar=-1.0 / C, in1=yv, op0=ALU.mult, op1=ALU.add).then_inc(s["y_chain"], 1)
                dve.wait_ge(s["y_chain"], at("y_chain", "mix", L, 0, 2))
                dve.wait_ge(s["conv_chain"], 2 * L + 2)
                dve.scalar_tensor_tensor(out=arena[0:B, 0:C], in0=cbias[0:B, :], scalar=float(NPIX), in1=arena[0:B, 0:C],
                                         op0=ALU.mult, op1=ALU.add).then_inc(s["y_chain"], 2)

            def group(ph, L, g):
                d = 0
                if ph == "mid":
                    for t in range(2):
                        for ri in range(2):
                            bank = take(ph, L, g, d)
                            dve.tensor_copy(Z[t].rearrange("p (o r k) -> p r k o", o=C, r=2)[:, ri],
                                            bank[:, 0:384].rearrange("p (k o) -> p k o", o=C)).then_inc(s["d_free"], 1)
                            d += 1

                def sums(n):
                    dve.wait_ge(s["squared"], at("squared", ph, L, g, n + 1) + 2)
                    m = n // 2
                    dve.reduce_sum(var[m % 2][:, 16 * (n % 2):16 * (n % 2) + 16], sq[n % 2].rearrange("p (x o) -> p x o", x=16), axis=AX).then_inc(s["summed"], 1)

                def scale(n):
                    m = n // 2
                    dve.wait_ge(s["rstd_ok"], at("rstd", ph, L, g, m + 1))
                    z = raw[n % 5].rearrange("p (x o) -> p x o", x=16)
                    r = rstd[m % 2][:, 16 * (n % 2):16 * (n % 2) + 16].rearrange("p (x o) -> p x o", o=1)
                    dve.tensor_tensor(z, z, r.broadcast_to([P, 16, C]), ALU.mult).then_inc(s["normed"], 1)

                for n in range(13):
                    if n < 8:
                        sums(n)
                    if 3 <= n <= 10:
                        scale(n - 3)
                    if n >= 5 and ph != "last":
                        k = n - 5
                        bank = take(ph, L, g, d)
                        dve.tensor_copy(h_rows[:, 512 * k:512 * k + 512], bank[:]).then_inc(s["d_free"], 1)
                        d += 1
                if ph == "last":
                    return
                for k in range(4):
                    bank = take(ph, L, g, d)
                    dve.tensor_copy(T[:, 512 * k:512 * k + 512], bank[:]).then_inc(s["d_free"], 1)
                    d += 1
                for k in range(2):
                    bank = take(ph, L, g, d)
                    dve.tensor_copy(spec_v[:, 3 * k:3 * k + 3, :, bass.ds(GI * g, GI)],
                                    bank[:, 0:288].rearrange("p (q k b) -> p q k b", q=3, b=GI)).then_inc(s["d_free"], 1)
                    d += 1

            phases(dve, mix, group)
            token_dve(dve)


_INS = [
    "x", "L0_tok_fc0_w", "L0_tok_fc0_b", "L0_tok_ln0_g", "L0_tok_ln0_b", "L0_tok_w1r", "L0_tok_w1i", "L0_tok_w2r", "L0_tok_w2i",
    "L0_tok_conv_w", "L0_tok_conv_b", "L0_tok_ln_g", "L0_tok_ln_b", "L0_tok_fc1_w", "L0_tok_fc1_b", "L0_tok_fc2_w",
    "L0_tok_fc2_b", "L0_tok_fc3_w", "L0_tok_fc3_b", "L0_attn_Wq", "L0_attn_bq", "L0_attn_Wk", "L0_attn_bk", "L0_attn_Wv",
    "L0_attn_bv", "L0_ffn_gate_w", "L0_ffn_gate_b", "L0_ffn_w1", "L0_ffn_b1", "L0_ffn_w2", "L0_ffn_b2", "L1_attn_W0",
    "L1_attn_b0", "L1_attn_W1", "L1_attn_b1", "L1_ffn_gate_w", "L1_ffn_gate_b", "L1_ffn_w1", "L1_ffn_b1", "L1_ffn_w2",
    "L1_ffn_b2", "L1_ffn_gamma", "L1_ffn_beta",
]


def kernel(**inputs):
    import numpy as _np
    import concourse.bacc as _bacc
    from concourse import mybir as _mybir
    from concourse.bass_utils import run_bass_kernel_spmd as _run

    nc = _bacc.Bacc("TRN2", target_bir_lowering=False, num_devices=1)
    arrays, args = {}, {}
    for name in _INS + ["consts"]:
        a = CONSTS if name == "consts" else _np.ascontiguousarray(inputs[name])
        arrays[f"in_{name}_dram"] = a
        args[name] = nc.dram_tensor(f"in_{name}_dram", a.shape, _mybir.dt.from_np(a.dtype), kind="ExternalInput").ap()
    B = inputs["x"].shape[0]
    out = nc.dram_tensor("out_0_dram", (B, S, S), _mybir.dt.float32, kind="ExternalOutput").ap()
    build(nc, args, out, B)
    r = _run(nc, [arrays], core_ids=[0])
    return r.results[0]["out_0_dram"]
```

```python
from contextlib import ExitStack

import math

import numpy as np

import concourse.bass as bass
import concourse.mybir as mybir

F32 = mybir.dt.float32
ACT = mybir.ActivationFunctionType
ALU = mybir.AluOpType
AX = mybir.AxisListType.X

P = 128
S = 64
C = 32
LAYERS = 4
M1, M2 = 12, 12
KY, KX = 2 * M1, M2
NQ = 32
EPS = 1e-5
GI = 4
NPIX = S * S
E1, F1 = 8, 256
E2, F2 = 16, 128
CAPACITY = 1.25
N_PARAMS = 19 + 16 + 12
HUGE = 3.0e38
F32_MAX = float(np.finfo(np.float32).max)

CONST_COLS = {}


def constants():
    parts, at = [], 0

    def put(name, a):
        nonlocal at
        full = np.zeros((P, a.shape[1]), np.float32)
        full[:a.shape[0]] = a
        CONST_COLS[name] = (at, a.shape[0], a.shape[1])
        parts.append(full)
        at += a.shape[1]

    y = np.arange(S)
    ang = lambda k, t: 2 * np.pi * ((k * t) % S) / S
    kys = np.array(list(range(M1)) + list(range(-M1, 0)))
    put("ident", np.eye(P))
    f1 = np.zeros((2, S, 2, NQ))
    for b in range(2):
        for q in range(M1 + 1):
            f1[b, :, b, q] = np.cos(ang(q, y))
        for q in range(1, M1 + 1):
            f1[b, :, b, M1 + q] = np.sin(ang(q, y))
    put("dft_y", f1.reshape(P, 2 * NQ))
    f2 = np.zeros((2, S, 2, KX, 4))
    for c in range(2):
        for k in range(KX):
            f2[c, :, c, k, 0] = np.cos(ang(k, y))
            f2[c, :, c, k, 1] = -np.sin(ang(k, y))
            f2[c, :, c, k, 2] = -np.sin(ang(k, y))
            f2[c, :, c, k, 3] = -np.cos(ang(k, y))
    put("dft_x", f2.reshape(P, 2, KX // 2, 2, 2, 2).transpose(0, 1, 2, 4, 3, 5).reshape(P, 2 * KX * 4))
    mc = np.zeros((GI, NQ, KY, GI))
    ms = np.zeros((GI, NQ, KY, GI))
    for b in range(GI):
        for n, k in enumerate(kys):
            mc[b, abs(k), n, b] = 1
            if k:
                ms[b, M1 + abs(k), n, b] = np.sign(k)
    put("mix_cos", mc.reshape(P, KY * GI))
    put("mix_sin", ms.reshape(P, KY * GI))
    bre = np.zeros((2, KY, 2, 2, S))
    bim = np.zeros((2, KY, 2, 2, S))
    for b in range(2):
        for n, k in enumerate(kys):
            bre[b, n, 0, b], bre[b, n, 1, b] = np.cos(ang(k, y)), -np.sin(ang(k, y))
            bim[b, n, 0, b], bim[b, n, 1, b] = np.sin(ang(k, y)), np.cos(ang(k, y))
    put("idft_y_re", bre.reshape(96, P))
    put("idft_y_im", bim.reshape(96, P))
    i2 = np.zeros((4, 2, KX, 4, 4, 16))
    for o in range(4):
        for k in range(KX):
            w = (1 if k == 0 else 2) / NPIX
            i2[o, 0, k, :, o, :] = (w * np.cos(ang(k, y))).reshape(4, 16)
            i2[o, 1, k, :, o, :] = (-w * np.sin(ang(k, y))).reshape(4, 16)
    put("idft_x", i2.reshape(96, 256))
    CONST_COLS["late"] = (at, P, 0)
    put("upto", np.triu(np.ones((P, P))))
    put("ones", np.ones((P, P)))
    put("falling", np.tile(np.arange(E2, 0, -1), (P, 1)))
    return np.concatenate(parts, 1).astype(np.float32)


CONSTS = constants()
NC_COLS = CONSTS.shape[1]
NC_EARLY = CONST_COLS.pop("late")[0]


PER = {
    "d_out":         (14, 12, 18, 0),
    "s_out":         (10, 12, 12, 0),
    "acc":           (8, 0, 8, 8),
    "squared":       (8, 0, 8, 8),
    "summed":        (8, 0, 8, 8),
    "rstd":          (4, 0, 4, 4),
    "pool_chain":    (52, 0, 52, 52),
    "normed":        (8, 0, 8, 8),
    "turned":        (8, 0, 8, 8),
    "h_new":         (8, 0, 8, 8),
    "x_in":          (16, 0, 0, 0),
    "y_in":          (0, 0, 32, 32),
    "h_in":          (0, 0, 16, 16),
    "stored":        (16, 0, 16, 0),
    "y_stored":      (0, 64, 0, 0),
    "w_loaded":      (0, 16 * 16, 0, 0),
    "w_signed":      (0, 16, 0, 0),
    "y_chain":       (0, 24, 0, 0),
}


ORDER = {
    "first": {
        "PE": ("tr.0- xt.0 xt.1 tr.3- acc.0 acc.1 tr.2- acc.2 acc.3 tr.1- f2.2- f2.0- f2.3- f2.1- xx.0- turn.0 acc.4 "
               "turn.1 acc.5 acc.6 back.0 acc.7 turn.2 turn.3 back.2 back.1 back.3 xx.1- turn.4 turn.5 back.4 back.5 "
               "f1.0 f1.1 turn.6 turn.7 back.6 back.7 f1.2 f1.3"),
        "ACT": ("xt.0 xt.1 acc.0 acc.1 acc.2 acc.3 f2.2- f2.0- f2.3- f2.1- gelu.0 acc.4 acc.5 acc.6 acc.7 gelu.1 "
               "gelu.2 gelu.3 gelu.4 gelu.5 f1.0 f1.1 gelu.6 gelu.7 f1.2 f1.3"),
        "DVE": ("tr.0- tr.3- red.0 red.1 tr.2- red.2 red.3 tr.1- scale.0 scale.1 xx.0- red.4 red.5 scale.2 scale.3 "
               "red.6 red.7 back.0 back.2 back.1 scale.4 scale.5 back.3 xx.1- back.4 back.5 scale.6 scale.7 back.6 "
               "back.7"),
    },
    "mid": {
        "PE": ("i1.1 i1.0 turn.7- back.5- t2.1 t2.0 i1.3 acc.0 acc.1 acc.2 i1.2 acc.3 t2.3 t2.2 back.4- back.6- "
               "turn.0 acc.4 turn.1 back.7- acc.5 acc.6 acc.7 f1.0- turn.2 turn.3 f1.3- f1.2- back.2 f1.1- back.1 "
               "back.3 back.0 tr.2- tr.0- tr.3- tr.1- f2.0- f2.3- f2.1- f2.2- turn.4 turn.5 xx.0- xx.1- turn.6"),
        "ACT": ("gelu.6- gelu.7- t2.1 t2.0 acc.0 acc.1 acc.2 t2.3 t2.2 acc.3 gelu.0 acc.4 gelu.1 acc.5 acc.6 acc.7 "
               "f1.0- gelu.2 f1.3- f1.2- gelu.3 f1.1- f2.0- f2.3- f2.1- f2.2- gelu.4 gelu.5"),
        "DVE": ("i1.1 i1.0 back.5- i1.3 red.0 red.1 i1.2 red.2 scale.0 red.3 scale.1 back.4- back.6- red.4 back.7- "
               "scale.2 scale.3 red.5 red.6 red.7 back.2 back.1 back.3 back.0 tr.2- tr.0- tr.3- tr.1- scale.4 "
               "scale.5 xx.0- xx.1- scale.6 scale.7"),
    },
    "last": {
        "PE": ("i1.1 i1.0 t2.0 t2.1 fin.1- acc.0 acc.1 acc.2 acc.3 i1.3 i1.2 t2.2 t2.3 turn.0 acc.4 turn.1 fc1.2 "
               "fc1.3 fc1.0 acc.5 fc1.1 fc2.1 fc2.0 fc1.4 fc1.7 fc1.5 fc1.6 acc.6 turn.2 fc2.3 fc2.2 fc1.8 fc1.10 "
               "fc1.11 acc.7 fc1.9 turn.3 turn.4 fc2.4 fc2.5 fc1.14 fc1.13 fc1.12 fc1.15 fc2.6 fc2.7 fc1.17 fc1.19 "
               "fc3.0 fc1.18 fc1.16 turn.5 fin.0 fc2.8 fc2.9 fc1.22 fc1.23 fc1.21 fc1.20 turn.6 turn.7 fc2.10 fc2.11 "
               "fc1.25 fc1.24 fc1.27 fc1.26 fc2.12 fc2.13 fc1.28 fc1.29 fc1.30 fc1.31 fc2.14 fc2.15 fc3.1"),
        "ACT": ("i1.1 i1.0 t2.0 t2.1 fin.1- acc.0 acc.1 acc.2 i1.3 i1.2 acc.3 t2.2 t2.3 gelu.0 gelu.1 fc1.2 fc1.3 "
               "fc1.0 acc.4 fc1.1 fc2.1 fc2.0 fc1.4 fc1.7 acc.5 fc1.5 fc1.6 gelu.2 fc2.3 fc2.2 fc1.8 fc1.10 fc1.11 "
               "acc.6 fc1.9 gelu.3 gelu.4 fc2.4 fc2.5 fc1.14 fc1.13 fc1.12 fc1.15 acc.7 fc2.6 fc2.7 fc1.17 fc1.19 "
               "fc3.0 fc1.18 fc1.16 gelu.5 fin.0 fc2.8 fc2.9 fc1.22 fc1.23 fc1.21 fc1.20 gelu.6 gelu.7 fc2.10 fc2.11 "
               "fc1.25 fc1.24 fc1.27 fc1.26 fc2.12 fc2.13 fc1.28 fc1.29 fc1.30 fc1.31 fc2.14 fc2.15 fc3.1"),
        "DVE": ("red.0 red.1 red.2 scale.0 red.3 scale.1 scale.2 scale.3 red.4 red.5 scale.4 scale.5 red.6 red.7 "
               "scale.6 scale.7"),
    },
}
RING = {
    "first": dict(xt="s", back="d", f1="s", tr="d", f2="s", xx="d"),
    "mid": dict(i1="d", t2="s", back="d", f1="s", tr="d", f2="s", xx="d"),
    "last": dict(i1="s", t2="s", fc1="s", fc2="d", fc3="s", fin="s"),
}


def parse(text):
    out = []
    for word in text.split():
        op, n = word.rstrip("-").split(".")
        out.append((op, int(n), word.endswith("-")))
    return out


def rsqrt(eng, out, var, tmp, chain, value, done, alone):
    k = 0

    def after(ins):
        nonlocal k
        k += 1
        ins.then_inc(chain, 1)
        eng.wait_ge(chain, value(k))
        alone(eng)

    v, a, b = tmp[0][:, 0:var.shape[1]], tmp[1][:, 0:var.shape[1]], tmp[2][:, 0:var.shape[1]]
    after(eng.tensor_scalar(v, var, EPS, None, ALU.add))
    after(eng.tensor_scalar(out.bitcast(mybir.dt.int32), v.bitcast(mybir.dt.int32), -0.5, float(0x5F3759DF), ALU.mult, ALU.add))
    for step in range(2):
        after(eng.tensor_tensor(a, out, out, ALU.mult))
        after(eng.tensor_tensor(a, a, v, ALU.mult))
        after(eng.tensor_scalar(b, a, 0.375, -1.25, ALU.mult, ALU.add))
        after(eng.tensor_tensor(a, a, b, ALU.mult))
        after(eng.tensor_scalar(a, a, 1.875, None, ALU.add))
        if step == 0:
            after(eng.tensor_tensor(out, out, a, ALU.mult))
        else:
            eng.tensor_tensor(out, out, a, ALU.mult).then_inc(done, 1)


def build(nc, ins, out_ap, B, debug=None, stop=None):
    NG = B // GI
    NT = B // 2
    TOKENS = B * S
    CAP = max(1, math.ceil(CAPACITY * TOKENS / E1))
    PER["s_out"] = (10, 12, 12, 4 + 4 + 2 * 16 + 4)
    PER["d_out"] = (14, 12, 18, 16)

    def at(name, ph, L, g, n):
        f, x, m, l = PER[name]
        per_layer = x + NG * m
        if ph == "first":
            return g * f + n
        if ph == "mix":
            return NG * f + L * per_layer + n
        if ph == "mid":
            return NG * f + x + L * per_layer + g * m + n
        return NG * f + 3 * per_layer + x + g * l + n

    ctx = ExitStack()
    with ctx:
        sb = lambda name, shape: ctx.enter_context(nc.sbuf_tensor(name, shape, F32))
        pb = lambda name: ctx.enter_context(nc.psum_tensor(name, [P, 512], F32))
        sem = lambda name: ctx.enter_context(nc.semaphore(name))

        h_dram = nc.dram_tensor("h_scratch", [NG, P, 2 * 16 * P], F32, kind="Internal").ap()
        y_dram = nc.dram_tensor("y_scratch", [B, KY * 2 * KX * C], F32, kind="Internal").ap()

        cst = sb("cst", [P, NC_EARLY])
        const = {k: cst[0:r, a:a + n] for k, (a, r, n) in CONST_COLS.items() if a < NC_EARLY}
        ident = const["ident"]
        spec = sb("spec", [P, 6 * KY * B])
        spec_v = spec[:].rearrange("p (q k b) -> p q k b", q=6, b=B)
        w_sb = sb("w_sb", [P, 2 * 2 * C * M1 * M2])
        w_v = w_sb[:].rearrange("p (w s o m) -> p w s o m", w=2, s=2, o=C)
        arena = sb("arena", [P, 9216])
        y_mix = arena[:].rearrange("p (k r x o) -> p k r x o", k=M1, r=2, x=KX)
        raw_more = sb("raw_more", [P, 3 * 512])
        raw = [arena[:, 0:512], arena[:, 512:1024]] + [raw_more[:, 512 * i:512 * i + 512] for i in range(3)] + [arena[:, 7424:7936]]
        V = arena[:, 1024:3072]
        T2 = arena[:, 3072:5120]
        TA = [V[:, 512 * k:512 * k + 512] for k in range(4)]
        Xs = arena[:, 5120:6656]
        Z = arena[:, 6656:7424]
        sq = [arena[:, 8192 + 512 * i:8192 + 512 * (i + 1)] for i in range(2)]
        h_in = sb("h_in", [P, 4096])
        h_new = sb("h_new", [P, 4096])
        h_rows = sb("h_rows", [P, 4096])
        y_in = sb("y_in", [96, 768])
        conv_bd = sb("conv_bd", [P, P])
        gam = sb("gam", [P, LAYERS + 1])
        bet = sb("bet", [P, LAYERS + 1])
        small = sb("small", [P, 224])
        var = [small[:, 32 * i:32 * i + 32] for i in range(2)]
        rstd = [small[:, 64 + 32 * i:96 + 32 * i] for i in range(2)]
        newton = [small[:, 128 + 32 * i:160 + 32 * i] for i in range(3)]
        y_mean = h_rows[:, 0:288]
        cbias = small[:, 0:32]
        x_in = h_in[:, 0:384].rearrange("p (t n) -> p t n", t=2)
        xT = T2[:, 0:1024].rearrange("p (t n) -> p t n", t=2)
        fc0 = T2[:, 1024:1536].rearrange("p (x o) -> p x o", x=16)
        fc0_mean = T2[:, 1536:1552]
        fc0_row = T2[64:65, 1600:1632]
        fc1_pad = w_sb[:, 0:512].rearrange("p (j f) -> p j f", j=4)
        fc1_b = w_sb[:, 512:513]
        fc2_w = w_sb[:, 513:577]
        fc2_b = w_sb[:, 577:578]
        fc3_pad = w_sb[:, 584:648].rearrange("p (k m) -> p k m", k=2)
        fc3_b = w_sb[:, 580:581]
        G1 = [w_sb[:, 1024 + 512 * i:1536 + 512 * i] for i in range(4)]
        G3 = w_sb[:, 3072:3584]
        G2 = w_sb[:, 4096:8192].rearrange("p (n c) -> p n c", n=8)
        tok = sb("tok", [P, NT * S]) if False else w_sb[:, 8192:8192 + NT * S]

        at_col = [0]

        def param(rows, cols):
            a = at_col[0]
            at_col[0] += cols
            return spec[0:rows, a:a + cols]

        w1a, w2a = param(P, E1 * F1), param(P, E1 * F1 // P * S)
        w1b, w2b = param(P, E2 * F2), param(P, E2 * F2 // P * S)
        b2a, b2b = param(8 * E1, 512), param(8 * E2, 512)
        wq, wk, wv = param(P, S), param(P, S), param(P, S)
        gwa, gwb = param(P, E1), param(P, E2)
        wg0, wg1 = param(P, P), param(P, P)
        wg0T, wg1T = param(P, P), param(P, P)
        gbias = param(P, 4)
        ngbias = param(P, 2)
        gamma, beta = param(P, S), param(P, S)
        late = param(P, NC_COLS - NC_EARLY)
        const |= {k: late[0:r, a - NC_EARLY:a - NC_EARLY + n] for k, (a, r, n) in CONST_COLS.items() if a >= NC_EARLY}
        XT = h_rows[:, 0:TOKENS]
        QT, KT = arena[0:64, 0:4096], arena[0:64, 4096:8192]
        VB = h_in[0:64, :]
        Sx = h_new[:, 0:2048]
        PT = w_sb[0:64, 10240:14336]
        hid = [w_sb[:, 14336 + 512 * i:14848 + 512 * i] for i in range(8)]
        X = tok
        Y = h_new[:, 2048:4096]
        Z2 = w_sb[:, 0:2048]
        Z3 = w_sb[:, 2048:4096]
        tiny = w_sb[:, 4096:4096 + 16 * 512]
        tiny = [w_sb[:, 4096 + 512 * i:4608 + 512 * i] for i in range(8)]
        gates = arena[:, 8192:8704]
        GT = arena[:, 8704:9216]
        GA, GZ = arena[:, 0:2048], arena[:, 2048:4096]
        GS, GV = arena[:, 4096:6144], arena[:, 6144:8192]
        OUT0, OUT1 = h_in[:, 0:2048], h_in[:, 2048:4096]

        pA = [pb("pA0"), pb("pA1")]
        pT = [pb("pT0"), pb("pT1")]
        pD = [pb("pD0"), pb("pD1")]
        pS = [pb("pS0"), pb("pS1")]

        names = ["d_full", "d_free", "s_full", "s_free", "acc_full", "squared", "summed", "rstd_ok",
                 "turned", "h_new_ok", "x_loaded", "y_loaded", "h_loaded0", "h_loaded1", "stored0", "stored1", "fc0_clear", "y_stored", "w_loaded",
                 "w_signed", "conv_cleared", "conv_loaded", "conv_chain", "cst_loaded", "ln_loaded",
                 "fc0_loaded", "fc0_chain", "mlp_cleared", "mlp_loaded", "y_chain", "normed", "pool_chain"]
        names += ["td_full", "td_free", "ts_full", "ts_free", "par_cleared", "par_loaded", "tok_ready", "v_chain", "shifted",
                  "exped", "e_subbed", "e_exped", "gated", "part_done", "part_used", "acc_done", "out_stored", "wg_scaled",
                  "scored", "gru_a", "gru_act", "gru_out", "ones_set", "passed"]
        s = {n: sem(n) for n in names}
        TD = [pD[0], pD[1], pA[0], pA[1]]
        TS = [pS[0], pS[1], pT[0], pT[1]]
        ctx.enter_context(nc.allow_non_contiguous_dma(reason="small parameters, once per layer"))
        block = ctx.enter_context(nc.Block())
        h_v = lambda t: t[:].rearrange("p (t q n) -> p t q n", t=2, q=16)
        hin_v, hnew_v = h_v(h_in), h_v(h_new)
        hrow_v = h_rows[:].rearrange("p (t n) -> p t n", t=2)

        LAYER1 = dict(E=E1, H=F1 // P, w1=w1a, w2=w2a, gw=gwa, b2=b2a, tiles=8)
        LAYER2 = dict(E=E2, H=F2 // P, w1=w1b, w2=w2b, gw=gwb, b2=b2b, tiles=8)

        def token_pe(pe):
            n = {"d": 0, "s": 0}
            ring = {"d": TD, "s": TS}

            def bank(which):
                pe.wait_ge(s[f"t{which}_free"], n[which] + 1)
                return ring[which][n[which] % 4]

            def sent(which, mm):
                mm.then_inc(s[f"t{which}_full"], 1)
                n[which] += 1

            def taken(which, back=0):
                pe.wait_ge(s[f"t{which}_free"], n[which] + 4 - back)

            def turn_x(stage):
                pe.wait_ge(s["tok_ready"], stage)
                for j in range(8):
                    b = bank("s")
                    for i in range(4):
                        t = 4 * j + i
                        mm = pe.transpose(b[0:64, 128 * i:128 * i + 128], X[:, S * t:S * t + S], ident)
                    sent("s", mm)
                taken("s")

            pe.wait_ge(s["par_loaded"], 16 * N_PARAMS)
            turn_x(1)
            pe.wait_ge(s["ones_set"], 2)
            for j in range(8):
                for which, w in (("d", wq), ("s", wk)):
                    b = bank(which)
                    sent(which, pe.matmul(b[0:64, :], w, XT[:, 512 * j:512 * j + 512], start=True, stop=True))
            for j in range(8):
                b = bank("d")
                for i in range(8):
                    mm = pe.matmul(b[0:64, S * i:S * i + S], XT[:, S * (8 * j + i):S * (8 * j + i + 1)], wv, start=True, stop=True)
                sent("d", mm)
            taken("d")
            taken("s")
            for j in range(4):
                b = bank("d")
                for i in range(8):
                    for h in range(2):
                        c = 128 * (8 * j + i) + 64 * h
                        mm = pe.matmul(b[64 * h:64 * h + 64, S * i:S * i + S], QT[:, c:c + 64], KT[:, c:c + 64], start=True, stop=True)
                sent("d", mm)
            for j in range(8):
                pe.wait_ge(s["exped"], j // 2 + 1)
                b = bank("s")
                for i in range(4):
                    t = 4 * j + i
                    mm = pe.transpose(b[0:64, 128 * i:128 * i + 128], Sx[:, S * t:S * t + S], ident)
                sent("s", mm)
            taken("s")
            for j in range(4):
                b = bank("d")
                for i in range(8):
                    for h in range(2):
                        c = 128 * (8 * j + i) + 64 * h
                        mm = pe.matmul(b[64 * h:64 * h + 64, S * i:S * i + S], PT[:, c:c + 64],
                                       VB[:, c:c + 64], start=True, stop=True)
                sent("d", mm)

            def experts(stage, E, H, w1, w2, gw, b2, tiles):
                turn_x(stage)
                b = bank("d")
                for t in range(NT):
                    mm = pe.matmul(b[:, E * t:E * t + E], XT[:, 128 * t:128 * t + 128], gw, start=True, stop=True)
                sent("d", mm)
                if E == E1:
                    pe.wait_ge(s["scored"], 1)
                    for lhs in ("upto", "ones"):
                        b = bank("d")
                        sent("d", pe.matmul(b[:, 0:E * NT], const[lhs], gates[:, 0:E * NT], start=True, stop=True))

                def hidden(e, k):
                    for h in range(H):
                        b = bank("s")
                        c = (e * H + h) * P
                        sent("s", pe.matmul(b[:], w1[:, c:c + P], XT[:, 512 * k:512 * k + 512], start=True, stop=True))

                def output(e, k, b):
                    for i in range(4):
                        for h in range(H):
                            slot = ((e * 8 + k) * H + h) % 8
                            mm = pe.matmul(b[:, S * (4 * (k % 2) + i):S * (4 * (k % 2) + i) + S],
                                           hid[slot][:, 128 * i:128 * i + 128], w2[:, (e * H + h) * S:(e * H + h) * S + S],
                                           start=(h == 0), stop=(h == H - 1))
                    return mm

                todo = [(e, k) for e in range(E) for k in range(8)]
                hidden(*todo[0])
                for i, (e, k) in enumerate(todo):
                    if i + 1 < len(todo):
                        hidden(*todo[i + 1])
                    taken("s", H if i + 1 < len(todo) else 0)
                    if k % 2 == 0:
                        b = bank("d")
                    mm = output(e, k, b)
                    if k % 2:
                        sent("d", mm)
                pe.wait_ge(s["gated"], 1 if E == E1 else 2)
                b = bank("s")
                for j in range(NT // 8):
                    mm = pe.transpose(b[0:8 * E, 128 * j:128 * j + 128], gates[:, 8 * E * j:8 * E * j + 8 * E], ident)
                sent("s", mm)
                taken("s")
                for j in range(NT // 8):
                    b = bank("d")
                    sent("d", pe.matmul(b[:], GT[0:8 * E, 128 * j:128 * j + 128], b2[0:8 * E, :], start=True, stop=True))

            experts(2, **LAYER1)

            b = bank("s")
            pe.transpose(b[:, 0:P], wg0, ident)
            sent("s", pe.transpose(b[:, P:2 * P], wg1, ident))
            turn_x(3)
            for n_layer in range(2):
                if n_layer == 1:
                    pe.wait_ge(s["gru_out"], 1)
                for part in range(2):
                    for j in range(4):
                        b = bank("s" if part == 0 else "d")
                        for h in range(2):
                            if n_layer == 0:
                                mm = pe.matmul(b[64 * h:64 * h + 64, :], wg0T[0:64, 64 * part:64 * part + 64],
                                               XT[0:64, 2048 * h + 512 * j:2048 * h + 512 * j + 512], start=True, stop=True)
                            else:
                                q = slice(64 * h, 64 * h + 64)
                                mm = pe.matmul(b[q, :], wg1T[q, 64 * part:64 * part + 64], OUT0[q, 512 * j:512 * j + 512],
                                               start=True, stop=True)
                        sent("s" if part == 0 else "d", mm)
            pe.wait_ge(s["gru_out"], 2)
            for j in range(4):
                b = bank("d")
                for i in range(4):
                    t = 4 * j + i
                    mm = pe.transpose(b[:, 128 * i:128 * i + 128], OUT1[:, 128 * t:128 * t + 128], ident)
                sent("d", mm)

            experts(4, **LAYER2)

        def token_act(act):
            n = [0]
            act.sem_inc(s["ts_free"], 4)

            def take():
                n[0] += 1
                act.wait_ge(s["ts_full"], n[0])
                return TS[(n[0] - 1) % 4]

            act.wait_ge(s["s_free"], at("s_out", "last", LAYERS - 1, NG, 0) + 2)
            act.sem_inc(s["tok_ready"], 1)

            def turn_x():
                for j in range(8):
                    act.copy(XT[0:64, 512 * j:512 * j + 512], take()[0:64, :]).then_inc(s["ts_free"], 1)

            turn_x()
            for j in range(8):
                act.copy(KT[:, 512 * j:512 * j + 512], take()[0:64, :]).then_inc(s["ts_free"], 1)
            for j in range(4):
                act.wait_ge(s["shifted"], j + 1)
                act.activation(Sx[:, 512 * j:512 * j + 512], Sx[:, 512 * j:512 * j + 512], ACT.Exp, scale=S ** -0.5).then_inc(s["exped"], 1)
            for j in range(8):
                act.copy(PT[:, 512 * j:512 * j + 512], take()[0:64, :]).then_inc(s["ts_free"], 1)

            def experts(E, H, **_):
                turn_x()
                act.wait_ge(s["e_subbed"], 1 if E == E1 else 2)
                m = E * NT if E == E1 else NT
                act.activation(tiny[1][:, 0:m], tiny[0][:, 0:m], ACT.Exp).then_inc(s["e_exped"], 1)
                for i in range(E * 8 * H):
                    act.activation(hid[i % 8], take()[:], ACT.Relu).then_inc(s["ts_free"], 1)
                act.copy(GT[0:8 * E, :], take()[0:8 * E, :]).then_inc(s["ts_free"], 1)

            experts(**LAYER1)
            b = take()
            act.copy(wg0T, b[:, 0:P])
            act.copy(wg1T, b[:, P:2 * P]).then_inc(s["ts_free"], 1)
            turn_x()
            act.wait_ge(s["wg_scaled"], 1)
            for layer in range(2):
                for j in range(4):
                    c = slice(512 * j, 512 * j + 512)
                    b = take()
                    act.activation(GZ[:, c], b[:], ACT.Sigmoid, bias=gbias[:, 2 * layer:2 * layer + 1])
                    act.activation(GA[:, c], b[:], ACT.Sigmoid, bias=ngbias[:, layer:layer + 1], scale=-1.0).then_inc(s["ts_free"], 1)
                for j in range(4):
                    c = slice(512 * j, 512 * j + 512)
                    act.wait_ge(s["td_full"], GRU_D[layer] + j + 1)
                    act.activation(GS[:, c], TD[(GRU_D[layer] + j) % 4][:], ACT.Sigmoid,
                                   bias=gbias[:, 2 * layer + 1:2 * layer + 2]).then_inc(s["gru_act"], 1)
            experts(**LAYER2)

        d_attn = 8 + 8 + 4 + 4
        d_ffn = 1 + 2 + E1 * 4 + NT // 8
        GRU_D = [d_attn + d_ffn, d_attn + d_ffn + 4]

        def token_dve(dve):
            n = [0]
            chain = [0]
            dve.sem_inc(s["td_free"], 4)

            def take():
                n[0] += 1
                dve.wait_ge(s["td_full"], n[0])
                return TD[(n[0] - 1) % 4]

            def link(ins):
                chain[0] += 1
                ins.then_inc(s["v_chain"], 1)
                dve.wait_ge(s["v_chain"], chain[0])

            by_tile = lambda a, w=S: a.rearrange("p (t x) -> p t x", x=w)
            wide = lambda a, w=S, m=NT: a.rearrange("p (t x) -> p t x", x=1).broadcast_to([P, m, w])

            def rsqrt_here(out, var):
                v, a, b = tiny[5][:, 0:NT], tiny[6][:, 0:NT], tiny[7][:, 0:NT]
                link(dve.tensor_scalar(v, var, EPS, None, ALU.add))
                link(dve.tensor_scalar(out.bitcast(mybir.dt.int32), v.bitcast(mybir.dt.int32), -0.5, float(0x5F3759DF), ALU.mult, ALU.add))
                for _ in range(2):
                    link(dve.tensor_tensor(a, out, out, ALU.mult))
                    link(dve.tensor_tensor(a, a, v, ALU.mult))
                    link(dve.tensor_scalar(b, a, 0.375, -1.25, ALU.mult, ALU.add))
                    link(dve.tensor_tensor(a, a, b, ALU.mult))
                    link(dve.scalar_tensor_tensor(out=out, in0=a, scalar=1.875, in1=out, op0=ALU.add, op1=ALU.mult))

            def layer_norm(x):
                mean, var, r = tiny[4][:, 0:NT], tiny[4][:, 64:64 + NT], tiny[4][:, 128:128 + NT]
                link(dve.reduce_sum(mean, by_tile(x), axis=AX))
                link(dve.scalar_tensor_tensor(out=by_tile(x), in0=wide(mean), scalar=-1.0 / S, in1=by_tile(x), op0=ALU.mult, op1=ALU.add))
                link(dve.tensor_tensor(Z2, x, x, ALU.mult))
                link(dve.reduce_sum(var, by_tile(Z2), axis=AX))
                link(dve.tensor_scalar(var, var, 1.0 / S, None, ALU.mult))
                rsqrt_here(r, var)
                link(dve.tensor_tensor(by_tile(x), by_tile(x), wide(r), ALU.mult))

            dve.wait_ge(s["par_loaded"], 16 * N_PARAMS)
            
            link(dve.tensor_scalar(ngbias, gbias.rearrange("p (l g) -> p g l", g=2)[:, 0, :], -1.0, None, ALU.mult))
            for j in range(8):
                dve.tensor_copy(QT[:, 512 * j:512 * j + 512], take()[0:64, :]).then_inc(s["td_free"], 1)
            for j in range(8):
                dve.tensor_copy(VB[:, 512 * j:512 * j + 512], take()[0:64, :]).then_inc(s["td_free"], 1)
            top, den = tiny[0][:, 0:NT], tiny[1][:, 0:NT]
            for j in range(4):
                b = take()
                m = top[:, 8 * j:8 * j + 8]
                link(dve.reduce_max(m, by_tile(b[:]), axis=AX))
                dve.tensor_tensor(by_tile(Sx[:, 512 * j:512 * j + 512]), by_tile(b[:]), wide(m, m=8), ALU.subtract).then_inc(s["shifted"], 1)
                dve.wait_ge(s["shifted"], j + 1)
                dve.sem_inc(s["td_free"], 1)
            for j in range(4):
                dve.wait_ge(s["exped"], j + 1)
                dve.reduce_sum(den[:, 8 * j:8 * j + 8], by_tile(Sx[:, 512 * j:512 * j + 512]), axis=AX)
            link(dve.memset(tiny[2][:, 0:1], 0.0))
            link(dve.reciprocal(den, den))
            for j in range(4):
                b = take()
                c = slice(512 * j, 512 * j + 512)
                dve.tensor_tensor(by_tile(Y[:, c]), by_tile(b[:]), wide(den[:, 8 * j:8 * j + 8], m=8), ALU.mult).then_inc(s["td_free"], 1)
            dve.wait_ge(s["td_free"], n[0] + 4)
            link(dve.tensor_tensor(X, X, Y, ALU.add))
            layer_norm(X)
            dve.sem_inc(s["tok_ready"], 1)

            def combine(E, tiles_y):
                for e in range(E):
                    for j in range(4):
                        b = take()
                        c = slice(512 * j, 512 * j + 512)
                        g = gates.rearrange("p (t e) -> p e t", e=E)[:, e, 8 * j:8 * j + 8] if False else None
                        gv = gates[:, 8 * E * j:8 * E * j + 8 * E].rearrange("p (t e) -> p t e", e=E)[:, :, e:e + 1].broadcast_to([P, 8, S])
                        if e == 0:
                            dve.tensor_tensor(by_tile(Y[:, c]), by_tile(b[:]), gv, ALU.mult).then_inc(s["td_free"], 1)
                        else:
                            dve.tensor_tensor(by_tile(Z3[:, c]), by_tile(b[:]), gv, ALU.mult).then_inc(s["td_free"], 1)
                            dve.wait_ge(s["td_free"], n[0] + 4)
                            dve.tensor_tensor(Y[:, c], Y[:, c], Z3[:, c], ALU.add)
                link(dve.memset(tiny[2][:, 0:1], 0.0))
                for j in range(4):
                    b = take()
                    c = slice(512 * j, 512 * j + 512)
                    dve.tensor_tensor(Y[:, c], Y[:, c], b[:], ALU.add).then_inc(s["td_free"], 1)
                dve.wait_ge(s["td_free"], n[0] + 4)

            def first_best(out, value, best, E):
                fall = const["falling"][:, E2 - E:E2].rearrange("p (t e) -> p t e", t=1).broadcast_to([P, NT, E])
                a, m = tiny[2][:, 0:E * NT], tiny[3][:, 0:NT]
                link(dve.tensor_tensor(by_tile(a, E), by_tile(value, E), wide(best, E), ALU.is_equal))
                link(dve.tensor_tensor(by_tile(a, E), by_tile(a, E), fall, ALU.mult))
                link(dve.reduce_max(m, by_tile(a, E), axis=AX))
                link(dve.tensor_tensor(by_tile(out, E), by_tile(a, E), wide(m, E), ALU.is_equal))

            E = E1
            m = E * NT
            logits, best, shifted = tiny[0][:, m:2 * m], tiny[4][:, 256:256 + NT], tiny[0][:, 0:m]
            link(dve.tensor_copy(logits, take()[:, 0:m]))
            dve.sem_inc(s["td_free"], 1)
            link(dve.reduce_max(best, by_tile(logits, E), axis=AX))
            dve.tensor_tensor(by_tile(shifted, E), by_tile(logits, E), wide(best, E), ALU.subtract).then_inc(s["e_subbed"], 1)
            first_best(gates[:, 0:m], logits, best, E)
            dve.sem_inc(s["scored"], 1)
            inclusive, totals, running, rank = tiny[5][:, 0:m], tiny[5][:, m:2 * m], tiny[6][:, 0:m], tiny[3][:, 64:64 + NT]
            link(dve.tensor_copy(inclusive, take()[:, 0:m]))
            dve.sem_inc(s["td_free"], 1)
            link(dve.tensor_copy(totals, take()[:, 0:m]))
            dve.sem_inc(s["td_free"], 1)
            for e in range(E):
                by_e = lambda a: a.rearrange("p (t e) -> p e t", e=E)[:, e, :]
                dve.tensor_tensor_scan(by_e(running), const["ones"][:, 0:NT], by_e(totals), 0.0, ALU.mult, ALU.add)
            link(dve.memset(tiny[7][:, 0:1], 0.0))
            link(dve.tensor_tensor(running, running, totals, ALU.subtract))
            link(dve.tensor_tensor(running, running, inclusive, ALU.add))
            link(dve.tensor_tensor(running, running, gates[:, 0:m], ALU.mult))
            link(dve.reduce_sum(rank, by_tile(running, E), axis=AX))
            keep, total = tiny[3][:, 128:128 + NT], tiny[3][:, 192:192 + NT]
            link(dve.tensor_scalar(keep, rank, float(CAP), None, ALU.is_le))
            dve.wait_ge(s["e_exped"], 1)
            link(dve.reduce_sum(total, by_tile(tiny[1][:, 0:m], E), axis=AX))
            link(dve.reciprocal(total, total))
            link(dve.tensor_tensor(keep, keep, total, ALU.mult))
            link(dve.tensor_tensor(by_tile(gates[:, 0:m], E), by_tile(gates[:, 0:m], E), wide(keep, E), ALU.mult))
            dve.sem_inc(s["gated"], 1)
            combine(E1, NT)
            I32 = mybir.dt.int32
            link(dve.memset(Z2, 0.0))
            link(dve.tensor_tensor(Z3.bitcast(I32), Y, Y, ALU.not_equal))
            link(dve.copy_predicated(Y, Z3.bitcast(I32), Z2))
            link(dve.memset(Z2, 1.0e4))
            link(dve.tensor_scalar(Z3.bitcast(I32), Y, F32_MAX, None, ALU.is_gt))
            link(dve.copy_predicated(Y, Z3.bitcast(I32), Z2))
            link(dve.memset(Z2, -1.0e4))
            link(dve.tensor_scalar(Z3.bitcast(I32), Y, -F32_MAX, None, ALU.is_lt))
            link(dve.copy_predicated(Y, Z3.bitcast(I32), Z2))
            link(dve.tensor_tensor(X, X, Y, ALU.add))
            layer_norm(X)
            dve.sem_inc(s["wg_scaled"], 1)
            dve.sem_inc(s["tok_ready"], 1)

            for layer in range(2):
                for j in range(4):
                    c = slice(512 * j, 512 * j + 512)
                    b = take()
                    dve.wait_ge(s["gru_act"], 4 * layer + j + 1)
                    link(dve.tensor_scalar(GV[:, c], b[:], gbias[:, 2 * layer + 1:2 * layer + 2], 0.5, ALU.add, ALU.add))
                    dve.sem_inc(s["td_free"], 1)
                    link(dve.tensor_tensor(GV[:, c], GV[:, c], GS[:, c], ALU.max))
                    link(dve.tensor_tensor(GV[:, c], GV[:, c], GZ[:, c], ALU.mult))
                head = lambda a: a.rearrange("p (b t) -> p b t", t=S)[:, :, 0]
                link(dve.scalar_tensor_tensor(out=head(GV), in0=head(GA), scalar=0.5, in1=head(GV), op0=ALU.mult, op1=ALU.add))
                link(dve.memset(head(GA), 0.0))
                dve.tensor_tensor_scan((OUT0, OUT1)[layer], GA, GV, 0.0, ALU.mult, ALU.add).then_inc(s["gru_out"], 1)
            xv = X.rearrange("p (h t x) -> p t h x", h=2, x=S)
            for j in range(4):
                b = take()
                dve.tensor_tensor(xv[:, 4 * j:4 * j + 4], xv[:, 4 * j:4 * j + 4],
                                  b[:].rearrange("p (t h x) -> p t h x", h=2, x=S), ALU.add).then_inc(s["td_free"], 1)
            dve.wait_ge(s["td_free"], n[0] + 4)
            layer_norm(X)
            dve.sem_inc(s["tok_ready"], 1)

            E = E2
            m = E * NT
            logits, best, second = tiny[2][:, 0:m], tiny[4][:, 256:256 + NT], tiny[4][:, 320:320 + NT]
            logits = Z2[:, 0:m]
            rest = Z2[:, m:2 * m]
            pick1, pick2 = Z2[:, 2 * m:3 * m], Z2[:, 3 * m:4 * m]
            link(dve.tensor_copy(logits, take()[:, 0:m]))
            dve.sem_inc(s["td_free"], 1)
            link(dve.reduce_max(best, by_tile(logits, E), axis=AX))
            first_best(pick1, logits, best, E)
            link(dve.scalar_tensor_tensor(out=rest, in0=pick1, scalar=-HUGE, in1=logits, op0=ALU.mult, op1=ALU.add))
            link(dve.reduce_max(second, by_tile(rest, E), axis=AX))
            dve.tensor_tensor(tiny[0][:, 0:NT], second, best, ALU.subtract).then_inc(s["e_subbed"], 1)
            first_best(pick2, rest, second, E)
            dve.wait_ge(s["e_exped"], 2)
            ex, inv = tiny[1][:, 0:NT], tiny[3][:, 64:64 + NT]
            link(dve.tensor_scalar(inv, ex, 1.0, None, ALU.add))
            link(dve.reciprocal(inv, inv))
            link(dve.tensor_tensor(by_tile(pick1, E), by_tile(pick1, E), wide(inv, E), ALU.mult))
            link(dve.tensor_tensor(inv, inv, ex, ALU.mult))
            link(dve.tensor_tensor(by_tile(pick2, E), by_tile(pick2, E), wide(inv, E), ALU.mult))
            link(dve.tensor_tensor(gates[:, 0:m], pick1, pick2, ALU.add))
            dve.sem_inc(s["gated"], 1)
            combine(E2, NT)
            link(dve.tensor_tensor(Y, Y, X, ALU.add))
            layer_norm(Y)
            g_t = lambda a: a.rearrange("p (t x) -> p t x", t=1).broadcast_to([P, NT, S])
            link(dve.tensor_tensor(by_tile(Y), by_tile(Y), g_t(gamma), ALU.mult))
            link(dve.tensor_tensor(by_tile(Y), by_tile(Y), g_t(beta), ALU.add))
            link(dve.tensor_tensor(X, X, Y, ALU.add))
            layer_norm(X)
            dve.sem_inc(s["acc_done"], 1)

        def token_pool(pool):
            pass

        raw_of = lambda n: raw[(0, 1, 2, 3, 0, 1, 4, 5)[n]]
        first_group = lambda g: isinstance(g, int) and g == 0

        def alone(eng):
            eng.sem_inc(s["passed"], 1)

        class Phase:

            def __init__(self, ph, L):
                self.ph, self.L = ph, L
                self.order = {e: parse(t) for e, t in ORDER[ph].items()}
                self.place = {}
                for ring in "ds":
                    sent = [(op, n, late) for op, n, late in self.order["PE"] if RING[ph].get(op) == ring]
                    heads = sum(not late for _, _, late in sent)
                    for i, (op, n, late) in enumerate(sent):
                        before = sum(not x for _, _, x in sent[:i])
                        self.place[op, n] = (ring, late, i, before, heads)

            def product(self, op, n, g):
                ring, late, i, before, heads = self.place[op, n]
                banks, name = (pD if ring == "d" else pS), ring + "_out"
                if not late and isinstance(g, int) and g == 0:
                    return ring, banks[before % 2], at(name, self.ph, self.L, 0, before + 1)
                if late and isinstance(g, int) and g == NG - 1:
                    i -= before
                return ring, banks[(heads + i) % 2], at(name, self.ph, self.L, g if late else g - 1, heads + i + 1)

            def ends(self, op):
                ns = [n for late in (False, True) for o, n, l in self.order["PE"] if o == op and l == late]
                return ns[0], ns[-1]

            def sent(self, eng, op, n, g):
                ring, bank, v = self.product(op, n, g)
                eng.wait_ge(s[ring + "_full"], v)
                return bank

            def taken(self, eng, *keys, g):
                last = max(keys, key=lambda k: self.place[k][1:3])
                ring, _, v = self.product(*last, g)
                eng.wait_ge(s[ring + "_free"], v + 2)

        def phases(eng, name, mix, steps):
            def phase(ph, L):
                p = Phase(ph, L)
                do = steps(p)

                def body(b):
                    for op, n, late in p.order[name]:
                        if isinstance(b, int) and (b == 0 and late or b == NG and not late):
                            continue
                        do[op](n, b - 1 if late else b)

                body(0)
                body(1)
                with eng.Fori(2, NG) as b:
                    body(b)
                body(NG)

            phase("first", 0)
            with eng.Fori(0, LAYERS - 1) as L:
                mix(L)
                phase("mid", L)
            mix(LAYERS - 1)
            phase("last", LAYERS - 1)

        @block.sync
        def _(sp):
            sp.dma_start(cst[:], ins["consts"][:, 0:NC_EARLY]).then_inc(s["cst_loaded"], 16)
            for j in range(4):
                q = slice(32 * j, 32 * j + 32)
                sp.dma_start(gam[q, 0:1], ins["L0_tok_ln0_g"].rearrange("(p o) -> p o", o=1)).then_inc(s["ln_loaded"], 16)
                sp.dma_start(bet[q, 0:1], ins["L0_tok_ln0_b"].rearrange("(p o) -> p o", o=1)).then_inc(s["ln_loaded"], 16)
                for L in range(LAYERS):
                    sp.dma_start(gam[q, L + 1:L + 2], ins["L0_tok_ln_g"][L].rearrange("(p o) -> p o", o=1)).then_inc(s["ln_loaded"], 16)
                    sp.dma_start(bet[q, L + 1:L + 2], ins["L0_tok_ln_b"][L].rearrange("(p o) -> p o", o=1)).then_inc(s["ln_loaded"], 16)
            sp.wait_ge(s["fc0_chain"], 1)
            for x in range(16):
                sp.dma_start(fc0[3 * x:3 * x + 3, x, :], ins["L0_tok_fc0_w"]).then_inc(s["fc0_loaded"], 16)
            sp.dma_start(fc0_row, ins["L0_tok_fc0_b"].rearrange("(p o) -> p o", p=1)).then_inc(s["fc0_loaded"], 16)

            def load_x(g):
                src = ins["x"].rearrange("(g t b) y x c -> g (b y) t (x c)", t=2, b=2)
                sp.dma_start(x_in, src[g]).then_inc(s["x_loaded"], 16)

            def load_y(g):
                src = y_dram.rearrange("(g t b) (k n) -> g t (b k) n", t=2, b=2, k=2 * KY)
                for t in range(2):
                    sp.dma_start(y_in[:, 384 * t:384 * t + 384], src[g, t]).then_inc(s["y_loaded"], 16)

            def load_h(g, t):
                c = slice(2048 * t, 2048 * t + 2048)
                sp.dma_start(h_in[:, c], h_dram[g][:, c]).then_inc(s[f"h_loaded{t}"], 16)

            def store_h(ph, L, g, t):
                c = slice(2048 * t, 2048 * t + 2048)
                sp.wait_ge(s["h_new_ok"], at("h_new", ph, L, g, 4 * t + 4))
                sp.dma_start(h_dram[g][:, c], h_new[:, c]).then_inc(s[f"stored{t}"], 16)

            def weights(L):
                for w, (wr, wi) in enumerate((("L0_tok_w1r", "L0_tok_w1i"), ("L0_tok_w2r", "L0_tok_w2i"))):
                    for k in range(2):
                        for r in range(2):
                            q = slice(64 * k + 32 * r, 64 * k + 32 * r + 32)
                            for slot in range(2):
                                name = wr if slot == r else wi
                                sp.dma_start(w_v[q, w, slot].rearrange("p o m -> p (o m)"),
                                             ins[name][L].rearrange("i o x y -> i (o x y)")).then_inc(s["w_loaded"], 16)

            def conv_params(L):
                sp.wait_ge(s["conv_cleared"], 1)
                sp.wait_ge(s["acc_full"], at("acc", "mix", L, 0, 0))
                for j in range(4):
                    sp.dma_start(conv_bd[32 * j:32 * j + 32, 32 * j:32 * j + 32],
                                 ins["L0_tok_conv_w"][L].rearrange("o c -> c o")).then_inc(s["conv_loaded"], 16)
                sp.wait_ge(s["rstd_ok"], at("rstd", "mix", L, 0, 0))
                sp.dma_start(cbias[0:B, :], ins["L0_tok_conv_b"][L].partition_broadcast(B)).then_inc(s["conv_loaded"], 16)

            def y_store(L):
                for half in range(2):
                    sp.wait_ge(s["y_chain"], at("y_chain", "mix", L, 0, 12 * half + 12))
                    n = slice(4608 * half, 4608 * half + 4608)
                    for w in range(2):
                        dst = y_dram.rearrange("b (w n) -> w b n", w=2)[w]
                        sp.dma_start(dst[:, n], arena[64 * w:64 * w + B, n]).then_inc(s["y_stored"], 16)

            def y_is_stored(L):
                sp.wait_ge(s["y_stored"], at("y_stored", "mix", L, 0, 64))

            def token_params():
                sp.wait_ge(s["par_cleared"], 1)
                col = lambda a: a.rearrange("(p o) -> p o", o=1)
                row = lambda a: a.rearrange("(o n) -> o n", o=1)
                dmas = [
                    (late, ins["consts"][:, NC_EARLY:]),
                    (wq[0:64], ins["L0_attn_Wq"]), (wq[64:65], row(ins["L0_attn_bq"])),
                    (wk[0:64], ins["L0_attn_Wk"]), (wk[64:65], row(ins["L0_attn_bk"])),
                    (wv[0:64], ins["L0_attn_Wv"]), (wv[64:65], row(ins["L0_attn_bv"])),
                    (gwa[0:64], ins["L0_ffn_gate_w"]), (gwa[64:65], row(ins["L0_ffn_gate_b"])),
                    (gwb[0:64], ins["L1_ffn_gate_w"]), (gwb[64:65], row(ins["L1_ffn_gate_b"])),
                    (w1a[0:64].rearrange("d (e f) -> d e f", e=E1), ins["L0_ffn_w1"].rearrange("e d f -> d e f")),
                    (w1a[64:65], row(ins["L0_ffn_b1"].rearrange("e f -> (e f)"))),
                    (w2a.rearrange("p (e d) -> p e d", d=S), ins["L0_ffn_w2"].rearrange("e (h p) d -> p (e h) d", p=P)),
                    (w1b[0:64].rearrange("d (e f) -> d e f", e=E2), ins["L1_ffn_w1"].rearrange("e d f -> d e f")),
                    (w1b[64:65], row(ins["L1_ffn_b1"].rearrange("e f -> (e f)"))),
                    (w2b.rearrange("p (e d) -> p e d", d=S), ins["L1_ffn_w2"].rearrange("e p d -> p e d")),
                    (gamma, ins["L1_ffn_gamma"].partition_broadcast(P)), (beta, ins["L1_ffn_beta"].partition_broadcast(P)),
                ]
                for i in range(8):
                    dmas.append((b2a[E1 * i:E1 * i + E1, S * i:S * i + S], ins["L0_ffn_b2"]))
                    dmas.append((b2b[E2 * i:E2 * i + E2, S * i:S * i + S], ins["L1_ffn_b2"]))
                for i in range(2):
                    dmas.append((wg0[:, S * i:S * i + S], ins["L1_attn_W0"]))
                    dmas.append((wg1[:, S * i:S * i + S], ins["L1_attn_W1"]))
                    q = slice(64 * i, 64 * i + 64)
                    for n, b in enumerate(("L1_attn_b0", "L1_attn_b1")):
                        for part in range(2):
                            dmas.append((gbias[q, 2 * n + part:2 * n + part + 1], col(ins[b][S * part:S * part + S])))
                assert len(dmas) == N_PARAMS
                for dst, src in dmas:
                    sp.dma_start(dst, src).then_inc(s["par_loaded"], 16)

            def loads(ph, L):
                p = Phase(ph, L)

                def group(g, more):
                    if more:
                        op = "xt" if ph == "first" else "i1"
                        p.sent(sp, op, p.ends(op)[1], g)
                        load_x(g + 1) if ph == "first" else load_y(g + 1)
                    if more and ph != "first":
                        for t in range(2):
                            sp.wait_ge(s["acc_full"], at("acc", ph, L, g, 4 * t + 4))
                            load_h(g + 1, t)
                    if ph != "last":
                        store_h(ph, L, g, 0)
                        store_h(ph, L, g, 1)

                if ph == "first":
                    load_x(0)
                    weights(0)
                else:
                    load_y(0)
                if ph == "mid":
                    weights(L + 1)
                group(0, True)
                if ph == "last":
                    token_params()
                with sp.Fori(1, NG - 1) as g:
                    group(g, True)
                group(NG - 1, False)

            def first_h(ph, L):
                for t in range(2):
                    sp.wait_ge(s[f"stored{t}"], at("stored", ph, L, 0, 0) + 16)
                for t in range(2):
                    load_h(0, t)

            loads("first", 0)
            with sp.Fori(0, LAYERS - 1) as L:
                conv_params(L)
                first_h("mid", L)
                y_store(L)
                y_is_stored(L)
                loads("mid", L)
            L = LAYERS - 1
            conv_params(L)
            first_h("last", L)
            y_store(L)
            sp.wait_ge(s["mlp_cleared"], 1)
            for j in range(4):
                sp.dma_start(fc1_pad[32 * j:32 * j + 32, j, :], ins["L0_tok_fc1_w"]).then_inc(s["mlp_loaded"], 16)
            sp.dma_start(fc1_b, ins["L0_tok_fc1_b"].rearrange("(p o) -> p o", o=1)).then_inc(s["mlp_loaded"], 16)
            sp.dma_start(fc2_w, ins["L0_tok_fc2_w"]).then_inc(s["mlp_loaded"], 16)
            for j in range(2):
                q = slice(64 * j, 64 * j + 64)
                sp.dma_start(fc2_b[q], ins["L0_tok_fc2_b"].rearrange("(p o) -> p o", o=1)).then_inc(s["mlp_loaded"], 16)
                for k in range(2):
                    sp.dma_start(fc3_pad[q, k, 2 * k + j:2 * k + j + 1], ins["L0_tok_fc3_w"]).then_inc(s["mlp_loaded"], 16)
            sp.dma_start(fc3_b, ins["L0_tok_fc3_b"].partition_broadcast(P)).then_inc(s["mlp_loaded"], 16)
            y_is_stored(L)
            loads("last", L)
            sp.wait_ge(s["acc_done"], 1)
            sp.dma_start(out_ap.rearrange("(t b) y x -> (b y) t x", b=2), X.rearrange("p (t x) -> p t x", x=S)).then_inc(s["out_stored"], 16)
            sp.wait_ge(s["out_stored"], 16)

        @block.gpsimd
        def _(pool):
            def flip(L, j, m):
                w, k, n = m // 2, m % 2, C // 4
                v = w_v[64 * k + 32:64 * k + 64, w, 0, n * j:n * j + n].rearrange("p o m -> p (o m)")
                pool.tensor_scalar(v, v, -1.0, None, ALU.mult).then_inc(s["w_signed"], 1)
                pool.wait_ge(s["w_signed"], at("w_signed", "mix", L, 0, 4 * j + m + 1))
                alone(pool)

            def group(ph, L, g, and_then=None):
                for m in range(4):
                    pool.wait_ge(s["summed"], at("summed", ph, L, g, 2 * m + 2))
                    alone(pool)
                    rsqrt(pool, rstd[m % 2], var[m % 2], newton, s["pool_chain"],
                          lambda k: at("pool_chain", ph, L, g, 13 * m + k), s["rstd_ok"], alone)
                    if and_then:
                        pool.wait_ge(s["rstd_ok"], at("rstd", ph, L, g, m + 1))
                        alone(pool)
                        and_then(m)

            def groups(ph, L, layer_loaded):
                for j in range(4):
                    g = (j + 1) * (NG // 4) - 1
                    with pool.Fori(g + 1 - NG // 4, g) as b:
                        group(ph, L, b)
                    if j == 0:
                        pool.wait_ge(s["w_loaded"], 256 * layer_loaded + 256)
                        alone(pool)
                    group(ph, L, g, lambda m: flip(layer_loaded, j, m))

            groups("first", 0, 0)
            with pool.Fori(0, LAYERS - 1) as L:
                groups("mid", L, L + 1)
            L = LAYERS - 1
            pool.wait_ge(s["s_full"], at("s_out", "mix", L, 0, 12))
            pool.wait_ge(s["d_full"], at("d_out", "mix", L, 0, 12))
            pool.memset(w_sb[:, 0:1024], 0.0).then_inc(s["mlp_cleared"], 1)
            pool.wait_ge(s["mlp_cleared"], 1)
            pool.memset(spec[:, 0:at_col[0]], 0.0).then_inc(s["par_cleared"], 1)
            pool.wait_ge(s["par_cleared"], 1)
            pool.wait_ge(s["y_chain"], at("y_chain", "mix", L, 0, 24))
            pool.memset(XT[64:128, :], 0.0).then_inc(s["ones_set"], 1)
            pool.wait_ge(s["ones_set"], 1)
            pool.memset(XT[64:65, :], 1.0).then_inc(s["ones_set"], 1)
            pool.wait_ge(s["ones_set"], 2)
            with pool.Fori(0, NG) as g:
                group("last", L, g)

        @block.tensor
        def _(pe):
            pe.wait_ge(s["cst_loaded"], 16)

            def mix(L):
                pe.wait_ge(s["w_signed"], at("w_signed", "mix", L, 0, 16))
                pe.wait_ge(s["d_free"], at("d_out", "mix", L, 0, 2))
                for half in range(2):
                    for q in range(6):
                        k0 = 6 * half + q
                        pe.wait_ge(s["d_free"], at("d_out", "mix", L, 0, k0 + 1))
                        pe.wait_ge(s["s_free"], at("s_out", "mix", L, 0, k0 + 1))
                        alone(pe)
                        banks = [pD[k0 % 2], pS[k0 % 2]]
                        for j in range(6):
                            for par in range(2):
                                for w in range(2):
                                    rows = slice(64 * par, 64 * par + 64)
                                    mm = pe.matmul(
                                        banks[par][64 * w:64 * w + B, 64 * j:64 * j + 64],
                                        spec_v[rows, q, 12 * w + 6 * half + j, :],
                                        w_v[rows, w, :, :, (6 * half + j) * M2 + 2 * q + par],
                                        start=True, stop=True)
                                    if j == 5 and w == 1:
                                        mm.then_inc(s["d_full" if par == 0 else "s_full"], 1)

            def steps(p):
                ph, L = p.ph, p.L

                def bank_of(op, n, g):
                    ring, bank, v = p.product(op, n, g)
                    pe.wait_ge(s[ring + "_free"], v)
                    return bank

                def send(mm, op, n, g):
                    mm.then_inc(s[p.product(op, n, g)[0] + "_full"], 1)

                def xt(t, g):
                    if t == p.ends("xt")[0]:
                        pe.wait_ge(s["x_loaded"], at("x_in", ph, L, g, 16))
                    bank = bank_of("xt", t, g)
                    alone(pe)
                    for xb in range(4):
                        mm = pe.transpose(bank[0:48, 128 * xb:128 * xb + 128], x_in[:, t, 48 * xb:48 * xb + 48], ident)
                    send(mm, "xt", t, g)

                def i1(n, g):
                    if n == p.ends("i1")[0]:
                        pe.wait_ge(s["y_loaded"], at("y_in", ph, L, g, 32))
                    bank, t = bank_of("i1", n, g), n // 2
                    send(pe.matmul(bank[:, 0:384], const[("idft_y_re", "idft_y_im")[n % 2]], y_in[:, 384 * t:384 * t + 384],
                                   start=True, stop=True), "i1", n, g)

                def t2(n, g):
                    t, half = n // 2, n % 2
                    p.taken(pe, ("i1", 2 * t), ("i1", 2 * t + 1), g=g)
                    bank = bank_of("t2", n, g)
                    for j in range(4):
                        o = 4 * half + j
                        mm = pe.transpose(bank[0:96, 128 * j:128 * j + 128], Z[:, 96 * o:96 * o + 96], ident)
                    send(mm, "t2", n, g)

                def acc(n, g):
                    t, xb = n // 4, n % 4
                    pe.wait_ge(s["squared"], at("squared", ph, L, g, n + 1))
                    bank = pA[n % 2]
                    if ph == "first":
                        if n == 0:
                            pe.wait_ge(s["fc0_chain"], 4)
                        if xb == 0:
                            p.taken(pe, ("xt", t), g=g)
                        mm = pe.matmul(bank[:], xT[:, t, 128 * xb:128 * xb + 128],
                                       fc0.rearrange("p x o -> p (x o)"), start=True, stop=True)
                    else:
                        if n == 0:
                            pe.wait_ge(s["conv_chain"], 2 * L + 2)
                        if xb == 0:
                            pe.wait_ge(s[f"h_loaded{t}"], at("h_in", ph, L, g, 16))
                        out = bank[:].rearrange("p (x o) -> p o x", x=16)
                        for j in range(4):
                            pe.matmul(bank[:, 128 * j:128 * j + 128], hin_v[:, t, 4 * xb + j, :], conv_bd[:],
                                      start=(j == 0), stop=False, skip_group_check=True)
                        if xb == 0:
                            p.taken(pe, ("t2", 2 * t), ("t2", 2 * t + 1), g=g)
                        for o in range(8):
                            mm = pe.matmul(out[:, 4 * o:4 * o + 4, :],
                                           T2[0:96, 1024 * t + 128 * o:1024 * t + 128 * o + 128],
                                           const["idft_x"][:, 64 * xb:64 * xb + 64],
                                           start=False, stop=(o == 7), skip_group_check=True)
                    mm.then_inc(s["acc_full"], 1)

                def turn(n, g):
                    pe.wait_ge(s["normed"], at("normed", ph, L, g, n + 1))
                    if n >= 2 or not first_group(g):
                        pe.wait_ge(s["h_new_ok"], at("h_new", ph, L, g, n - 1))
                    for j in range(4):
                        mm = pe.transpose(pT[n % 2][:, 128 * j:128 * j + 128], raw_of(n)[:, 128 * j:128 * j + 128], ident)
                    mm.then_inc(s["turned"], 1)

                def back(n, g):
                    t, xb = n // 4, n % 4
                    pe.wait_ge(s["h_new_ok"], at("h_new", ph, L, g, n + 1))
                    bank = bank_of("back", n, g)
                    for j in range(4):
                        mm = pe.transpose(bank[:, 128 * j:128 * j + 128], hnew_v[:, t, 4 * xb + j, :], ident)
                    send(mm, "back", n, g)

                def f1(k, g):
                    p.taken(pe, ("back", k), ("back", 4 + k), g=g)
                    bank = bank_of("f1", k, g)
                    for t in range(2):
                        mm = pe.matmul(bank[64 * t:64 * t + 64, :], const["dft_y"], hrow_v[:, t, 512 * k:512 * k + 512],
                                       start=True, stop=True)
                    send(mm, "f1", k, g)

                def tr(k, g):
                    p.taken(pe, *[("f1", i) for i in range(4)], g=g)
                    bank = bank_of("tr", k, g)
                    for j in range(4):
                        c = 2 * (4 * k + j)
                        mm = pe.transpose(bank[:, 128 * j:128 * j + 128], V[:, S * c:S * c + 128], ident)
                    send(mm, "tr", k, g)

                def f2(k, g):
                    p.taken(pe, ("tr", k), g=g)
                    bank = bank_of("f2", k, g)
                    for j in range(4):
                        mm = pe.matmul(bank[:, 96 * j:96 * j + 96], TA[k][:, 128 * j:128 * j + 128],
                                       const["dft_x"], start=True, stop=True)
                    send(mm, "f2", k, g)

                def xx(k, g):
                    p.taken(pe, *[("f2", i) for i in range(4)], g=g)
                    bank = bank_of("xx", k, g)
                    for j in range(3):
                        q = 3 * k + j
                        o = bank[:, 96 * j:96 * j + 96]
                        pe.matmul(o, Xs[:, 256 * q:256 * q + 128], const["mix_cos"], start=True, stop=False)
                        mm = pe.matmul(o, Xs[:, 256 * q + 128:256 * q + 256], const["mix_sin"], start=False, stop=True)
                    send(mm, "xx", k, g)

                def fc1(m, g):
                    n, j = m // 4, m % 4
                    if m == p.ends("fc1")[0]:
                        pe.wait_ge(s["mlp_loaded"], 16 * 13)
                    pe.wait_ge(s["h_new_ok"], at("h_new", ph, L, g, n + 1))
                    bank, t, xb = bank_of("fc1", m, g), n // 4, n % 4
                    send(pe.matmul(bank[:], fc1_pad[:, j, :], hnew_v[:, t, 4 * xb:4 * xb + 4, :].rearrange("p a b -> p (a b)"),
                                   start=True, stop=True), "fc1", m, g)

                def fc2(m, g):
                    p.taken(pe, ("fc1", 2 * m), ("fc1", 2 * m + 1), g=g)
                    bank = bank_of("fc2", m, g)
                    for j in range(2):
                        mm = pe.matmul(bank[64 * j:64 * j + 64, :], fc2_w, G1[2 * (m % 2) + j], start=True, stop=True)
                    send(mm, "fc2", m, g)

                def fc3(t, g):
                    p.taken(pe, *[("fc2", 8 * t + i) for i in range(8)], g=g)
                    bank = bank_of("fc3", t, g)
                    for k in range(2):
                        for xb in range(4):
                            mm = pe.matmul(bank[32 * xb:32 * xb + 32, :], fc3_pad[:, k, :], G2[:, 2 * xb + k, :],
                                           start=(k == 0), stop=(k == 1), skip_group_check=True)
                    send(mm, "fc3", t, g)

                def fin(t, g):
                    p.taken(pe, ("fc3", t), g=g)
                    bank = bank_of("fin", t, g)
                    for j in range(4):
                        mm = pe.transpose(bank[:, 128 * j:128 * j + 128], G3[:, 128 * j:128 * j + 128], ident)
                    send(mm, "fin", t, g)

                return dict(xt=xt, i1=i1, t2=t2, acc=acc, turn=turn, back=back, f1=f1, tr=tr, f2=f2, xx=xx,
                            fc1=fc1, fc2=fc2, fc3=fc3, fin=fin)

            phases(pe, "PE", mix, steps)
            token_pe(pe)

        @block.scalar
        def _(act):
            act.sem_inc(s["s_free"], 2)
            act.sem_inc(s["squared"], 2)
            act.sem_inc(s["stored0"], 16)
            act.sem_inc(s["stored1"], 16)
            act.wait_ge(s["ln_loaded"], 16 * 4 * 2 * (LAYERS + 1))

            def mix(L):
                for k in range(12):
                    act.wait_ge(s["s_full"], at("s_out", "mix", L, 0, k + 1))
                    half, q = k // 6, k % 6
                    src = pS[k % 2][:, 0:384].rearrange("p (k r o) -> p k r o", k=6, r=2)
                    act.copy(y_mix[:, 6 * half:6 * half + 6, :, 2 * q + 1, :], src).then_inc(s["s_free"], 1)

            def steps(p):
                ph, L = p.ph, p.L
                take = lambda op, n, g: p.sent(act, op, n, g)

                def xt(t, g):
                    act.copy(xT[0:48, t, :], take("xt", t, g)[0:48, :]).then_inc(s["s_free"], 1)

                def i1(n, g):
                    act.copy(Z.rearrange("p (o r k) -> p r k o", o=C, r=2)[:, n % 2],
                             take("i1", n, g)[:, 0:384].rearrange("p (k o) -> p k o", o=C)).then_inc(s["s_free"], 1)

                def t2(n, g):
                    act.copy(T2[0:96, 512 * n:512 * n + 512], take("t2", n, g)[0:96, :]).then_inc(s["s_free"], 1)

                def acc(n, g):
                    act.wait_ge(s["acc_full"], at("acc", ph, L, g, n + 1))
                    act.copy(raw_of(n), pA[n % 2][:])
                    if n >= 2 or not first_group(g):
                        act.wait_ge(s["summed"], at("summed", ph, L, g, n - 1))
                    act.activation(sq[n % 2], pA[n % 2][:], ACT.Square, scale=float(C) ** -0.5).then_inc(s["squared"], 1)

                def gelu(n, g):
                    act.wait_ge(s["turned"], at("turned", ph, L, g, n + 1))
                    if n % 4 == 0 and ph != "last":
                        act.wait_ge(s[f"stored{n // 4}"], at("stored", ph, L, g, 0) + 16)
                    alone(act)
                    col = {"first": slice(0, 1), "mid": bass.ds(L + 1, 1), "last": slice(LAYERS, LAYERS + 1)}[ph]
                    act.activation(h_new[:, 512 * n:512 * n + 512], pT[n % 2][:], ACT.Gelu if ph == "mid" else ACT.Identity,
                                   bias=bet[:, col], scale=gam[:, col]).then_inc(s["h_new_ok"], 1)

                def f1(k, g):
                    act.copy(V.rearrange("p (c x) -> p c x", x=S)[:, :, 16 * k:16 * k + 16],
                             take("f1", k, g)[:].rearrange("p (x c) -> p c x", c=C)).then_inc(s["s_free"], 1)

                def f2(k, g):
                    act.copy(Xs.rearrange("p (j c) -> p j c", c=C)[:, :, 8 * k:8 * k + 8],
                             take("f2", k, g)[:, 0:384].rearrange("p (c j) -> p j c", j=48)).then_inc(s["s_free"], 1)

                def fc1(m, g):
                    bank = take("fc1", m, g)
                    if m == p.ends("fc1")[0]:
                        act.wait_ge(s["mlp_loaded"], 16 * 13)
                    act.activation(G1[m % 4], bank[:], ACT.Gelu, bias=fc1_b).then_inc(s["s_free"], 1)

                def fc2(m, g):
                    act.activation(G2[:, m % 8, :], take("fc2", m, g)[:], ACT.Gelu, bias=fc2_b).then_inc(s["d_free"], 1)

                def fc3(t, g):
                    act.copy(G3, take("fc3", t, g)[:]).then_inc(s["s_free"], 1)

                def fin(t, g):
                    bank = take("fin", t, g)
                    alone(act)
                    act.activation(tok[:, bass.ds(g * 128 + 64 * t, 64)].rearrange("p (b q m) -> p b q m", b=4, q=4),
                                   bank[:].rearrange("p (q b r) -> p b q r", q=4, b=4)[:, :, :, 0:4],
                                   ACT.Identity, bias=fc3_b).then_inc(s["s_free"], 1)

                return dict(xt=xt, i1=i1, t2=t2, acc=acc, gelu=gelu, f1=f1, f2=f2, fc1=fc1, fc2=fc2, fc3=fc3, fin=fin)

            phases(act, "ACT", mix, steps)
            token_act(act)

        @block.vector
        def _(dve):
            dve.sem_inc(s["d_free"], 2)
            dve.memset(conv_bd[:], 0.0).then_inc(s["conv_cleared"], 1)
            dve.memset(T2[:, 0:1536], 0.0).then_inc(s["fc0_clear"], 1)
            dve.wait_ge(s["fc0_clear"], 1)
            dve.memset(T2[64:65, 0:1024], 1.0).then_inc(s["fc0_chain"], 1)
            dve.wait_ge(s["fc0_loaded"], 16 * 17)
            dve.tensor_copy(fc0[64:65], fc0_row.rearrange("p (x o) -> p x o", x=1).broadcast_to([1, 16, C])).then_inc(s["fc0_chain"], 1)
            dve.wait_ge(s["fc0_chain"], 2)
            dve.reduce_sum(fc0_mean, fc0, axis=AX).then_inc(s["fc0_chain"], 1)
            dve.wait_ge(s["fc0_chain"], 3)
            dve.scalar_tensor_tensor(out=fc0, in0=fc0_mean.rearrange("p (x o) -> p x o", o=1).broadcast_to([P, 16, C]),
                                     scalar=-1.0 / C, in1=fc0, op0=ALU.mult, op1=ALU.add).then_inc(s["fc0_chain"], 1)

            def mix(L):
                dve.wait_ge(s["conv_loaded"], 80 * L + 80)
                cv = conv_bd[:].rearrange("p (x o) -> p x o", x=4)
                cm = small[:, 64:68]
                dve.reduce_sum(cm, cv, axis=AX)
                dve.reduce_sum(small[0:B, 68:69], cbias[0:B, :], axis=AX).then_inc(s["conv_chain"], 1)
                dve.wait_ge(s["conv_chain"], 2 * L + 1)
                dve.scalar_tensor_tensor(out=cv, in0=cm.rearrange("p (x o) -> p x o", o=1).broadcast_to([P, 4, C]),
                                         scalar=-1.0 / C, in1=cv, op0=ALU.mult, op1=ALU.add)
                dve.scalar_tensor_tensor(out=cbias[0:B, :], in0=small[0:B, 68:69].broadcast_to([B, C]),
                                         scalar=-1.0 / C, in1=cbias[0:B, :], op0=ALU.mult, op1=ALU.add).then_inc(s["conv_chain"], 1)
                yv = arena[:].rearrange("p (n x o) -> p n x o", x=KX, o=C)
                chain = lambda k: at("y_chain", "mix", L, 0, k)

                def centre(k):
                    half, q = k // 6, k % 6
                    v = yv[:, 12 * half:12 * half + 12, 2 * q:2 * q + 2, :]
                    mean = y_mean[:, 24 * k:24 * k + 24].rearrange("p (n x) -> p n x", x=2)
                    dve.wait_ge(s["s_free"], at("s_out", "mix", L, 0, k + 1) + 2)
                    dve.wait_ge(s["d_free"], at("d_out", "mix", L, 0, k + 1) + 2)
                    dve.reduce_sum(mean, v, axis=AX).then_inc(s["y_chain"], 1)
                    dve.wait_ge(s["y_chain"], chain(2 * k + 1))
                    for x in range(2):
                        ins = dve.scalar_tensor_tensor(out=v[:, :, x, :], in0=mean[:, :, x:x + 1].broadcast_to([P, 12, C]),
                                                       scalar=-1.0 / C, in1=v[:, :, x, :], op0=ALU.mult, op1=ALU.add)
                    ins.then_inc(s["y_chain"], 1)

                for k in range(12):
                    dve.wait_ge(s["d_full"], at("d_out", "mix", L, 0, k + 1))
                    half, q = k // 6, k % 6
                    dve.tensor_copy(y_mix[:, 6 * half:6 * half + 6, :, 2 * q, :],
                                    pD[k % 2][:, 0:384].rearrange("p (k r o) -> p k r o", k=6, r=2)).then_inc(s["d_free"], 1)
                    if k:
                        centre(k - 1)
                    if k == 1:
                        dve.wait_ge(s["y_chain"], chain(2))
                        dve.wait_ge(s["conv_chain"], 2 * L + 2)
                        dve.scalar_tensor_tensor(out=arena[0:B, 0:C], in0=cbias[0:B, :], scalar=float(NPIX), in1=arena[0:B, 0:C],
                                                 op0=ALU.mult, op1=ALU.add)
                centre(11)

            def steps(p):
                ph, L = p.ph, p.L
                take = lambda op, n, g: p.sent(dve, op, n, g)

                def i1(n, g):
                    dve.tensor_copy(Z.rearrange("p (o r k) -> p r k o", o=C, r=2)[:, n % 2],
                                    take("i1", n, g)[:, 0:384].rearrange("p (k o) -> p k o", o=C)).then_inc(s["d_free"], 1)

                def red(n, g):
                    m = n // 2
                    dve.wait_ge(s["squared"], at("squared", ph, L, g, n + 1) + 2)
                    dve.reduce_sum(var[m % 2][:, 16 * (n % 2):16 * (n % 2) + 16],
                                   sq[n % 2].rearrange("p (x o) -> p x o", x=16), axis=AX).then_inc(s["summed"], 1)

                def scale(n, g):
                    m = n // 2
                    dve.wait_ge(s["rstd_ok"], at("rstd", ph, L, g, m + 1))
                    z = raw_of(n).rearrange("p (x o) -> p x o", x=16)
                    r = rstd[m % 2][:, 16 * (n % 2):16 * (n % 2) + 16].rearrange("p (x o) -> p x o", o=1)
                    dve.tensor_tensor(z, z, r.broadcast_to([P, 16, C]), ALU.mult).then_inc(s["normed"], 1)

                def back(n, g):
                    dve.tensor_copy(h_rows[:, 512 * n:512 * n + 512], take("back", n, g)[:]).then_inc(s["d_free"], 1)

                def tr(k, g):
                    dve.tensor_copy(TA[k], take("tr", k, g)[:]).then_inc(s["d_free"], 1)

                def xx(k, g):
                    bank = take("xx", k, g)
                    dve.tensor_copy(spec_v[:, 3 * k:3 * k + 3, :, bass.ds(GI * g, GI)],
                                    bank[:, 0:288].rearrange("p (q k b) -> p q k b", q=3, b=GI)).then_inc(s["d_free"], 1)

                return dict(i1=i1, red=red, scale=scale, back=back, tr=tr, xx=xx)

            phases(dve, "DVE", mix, steps)
            token_dve(dve)


_INS = [
    "x", "L0_tok_fc0_w", "L0_tok_fc0_b", "L0_tok_ln0_g", "L0_tok_ln0_b", "L0_tok_w1r", "L0_tok_w1i", "L0_tok_w2r", "L0_tok_w2i",
    "L0_tok_conv_w", "L0_tok_conv_b", "L0_tok_ln_g", "L0_tok_ln_b", "L0_tok_fc1_w", "L0_tok_fc1_b", "L0_tok_fc2_w",
    "L0_tok_fc2_b", "L0_tok_fc3_w", "L0_tok_fc3_b", "L0_attn_Wq", "L0_attn_bq", "L0_attn_Wk", "L0_attn_bk", "L0_attn_Wv",
    "L0_attn_bv", "L0_ffn_gate_w", "L0_ffn_gate_b", "L0_ffn_w1", "L0_ffn_b1", "L0_ffn_w2", "L0_ffn_b2", "L1_attn_W0",
    "L1_attn_b0", "L1_attn_W1", "L1_attn_b1", "L1_ffn_gate_w", "L1_ffn_gate_b", "L1_ffn_w1", "L1_ffn_b1", "L1_ffn_w2",
    "L1_ffn_b2", "L1_ffn_gamma", "L1_ffn_beta",
]


def kernel(**inputs):
    import numpy as _np
    import concourse.bacc as _bacc
    from concourse import mybir as _mybir
    from concourse.bass_utils import run_bass_kernel_spmd as _run

    nc = _bacc.Bacc("TRN2", target_bir_lowering=False, num_devices=1)
    arrays, args = {}, {}
    for name in _INS + ["consts"]:
        a = CONSTS if name == "consts" else _np.ascontiguousarray(inputs[name])
        arrays[f"in_{name}_dram"] = a
        args[name] = nc.dram_tensor(f"in_{name}_dram", a.shape, _mybir.dt.from_np(a.dtype), kind="ExternalInput").ap()
    B = inputs["x"].shape[0]
    out = nc.dram_tensor("out_0_dram", (B, S, S), _mybir.dt.float32, kind="ExternalOutput").ap()
    build(nc, args, out, B)
    r = _run(nc, [arrays], core_ids=[0])
    return r.results[0]["out_0_dram"]
```

```python
from contextlib import ExitStack

import math

import numpy as np

import concourse.bass as bass
import concourse.mybir as mybir

F32 = mybir.dt.float32
F32R = mybir.dt.float32r
ACT = mybir.ActivationFunctionType
ALU = mybir.AluOpType
AX = mybir.AxisListType.X

P = 128
S = 64
C = 32
LAYERS = 4
M1, M2 = 12, 12
KY, KX = 2 * M1, M2
NQ = 32
EPS = 1e-5
GI = 4
NPIX = S * S
E1, F1 = 8, 256
E2, F2 = 16, 128
CAPACITY = 1.25
N_PARAMS = 23 + 16 + 12
HUGE = 3.0e38
F32_MAX = float(np.finfo(np.float32).max)

CONST_COLS = {}


def constants():
    parts, at = [], 0

    def put(name, a):
        nonlocal at
        full = np.zeros((P, a.shape[1]), np.float32)
        full[:a.shape[0]] = a
        CONST_COLS[name] = (at, a.shape[0], a.shape[1])
        parts.append(full)
        at += a.shape[1]

    y = np.arange(S)
    ang = lambda k, t: 2 * np.pi * ((k * t) % S) / S
    kys = np.array(list(range(M1)) + list(range(-M1, 0)))
    put("ident", np.eye(P))
    f1 = np.zeros((2, S, 2, NQ))
    for b in range(2):
        for q in range(M1 + 1):
            f1[b, :, b, q] = np.cos(ang(q, y))
        for q in range(1, M1 + 1):
            f1[b, :, b, M1 + q] = np.sin(ang(q, y))
    put("dft_y", f1.reshape(P, 2 * NQ))
    f2 = np.zeros((2, S, 2, KX, 4))
    for c in range(2):
        for k in range(KX):
            f2[c, :, c, k, 0] = np.cos(ang(k, y))
            f2[c, :, c, k, 1] = -np.sin(ang(k, y))
            f2[c, :, c, k, 2] = -np.sin(ang(k, y))
            f2[c, :, c, k, 3] = -np.cos(ang(k, y))
    put("dft_x", f2.reshape(P, 2, KX // 2, 2, 2, 2).transpose(0, 1, 2, 4, 3, 5).reshape(P, 2 * KX * 4))
    mc = np.zeros((GI, NQ, KY, GI))
    ms = np.zeros((GI, NQ, KY, GI))
    for b in range(GI):
        for n, k in enumerate(kys):
            mc[b, abs(k), n, b] = 1
            if k:
                ms[b, M1 + abs(k), n, b] = np.sign(k)
    put("mix_cos", mc.reshape(P, KY * GI))
    put("mix_sin", ms.reshape(P, KY * GI))
    bre = np.zeros((2, KY, 2, 2, S))
    bim = np.zeros((2, KY, 2, 2, S))
    for b in range(2):
        for n, k in enumerate(kys):
            bre[b, n, 0, b], bre[b, n, 1, b] = np.cos(ang(k, y)), -np.sin(ang(k, y))
            bim[b, n, 0, b], bim[b, n, 1, b] = np.sin(ang(k, y)), np.cos(ang(k, y))
    put("idft_y_re", bre.reshape(96, P))
    put("idft_y_im", bim.reshape(96, P))
    i2 = np.zeros((4, 2, KX, 4, 4, 16))
    for o in range(4):
        for k in range(KX):
            w = (1 if k == 0 else 2) / NPIX
            i2[o, 0, k, :, o, :] = (w * np.cos(ang(k, y))).reshape(4, 16)
            i2[o, 1, k, :, o, :] = (-w * np.sin(ang(k, y))).reshape(4, 16)
    put("idft_x", i2.reshape(96, 256))
    CONST_COLS["late"] = (at, P, 0)
    put("upto", np.triu(np.ones((P, P))))
    put("ones", np.ones((P, P)))
    put("falling", np.tile(np.arange(E2, 0, -1), (P, 1)))
    return np.concatenate(parts, 1).astype(np.float32)


CONSTS = constants()
NC_COLS = CONSTS.shape[1]
NC_EARLY = CONST_COLS.pop("late")[0]


PER = {
    "d_out":         (14, 12, 18, 16),
    "s_out":         (10, 12, 12, 44),
    "acc":           (8, 0, 8, 8),
    "squared":       (8, 0, 8, 8),
    "summed":        (8, 0, 8, 8),
    "rstd":          (4, 0, 4, 4),
    "pool_chain":    (52, 0, 52, 52),
    "normed":        (8, 0, 8, 24),
    "turned":        (8, 0, 8, 16),
    "h_new":         (8, 0, 8, 16),
    "x_in":          (16, 0, 0, 0),
    "y_in":          (0, 0, 32, 32),
    "h_in":          (0, 0, 16, 16),
    "stored":        (16, 0, 16, 0),
    "y_stored":      (0, 64, 0, 0),
    "w_loaded":      (0, 16 * 16, 0, 0),
    "w_signed":      (0, 16, 0, 0),
    "y_chain":       (0, 24, 0, 0),
}


ORDER = {
    "first": {
        "PE": ("xt.0 tr.0- acc.0 acc.1 f2.0- acc.2 tr.2- xt.1 tr.3- f2.2- acc.3 f2.3- tr.1- turn.0 acc.4 turn.1 "
               "acc.5 acc.6 back.0 f2.1- turn.2 back.1 acc.7 back.2 xx.1- turn.3 xx.0- turn.4 turn.5 back.3 back.4 "
               "back.5 f1.0 f1.1 turn.6 turn.7 back.6 back.7 f1.2 f1.3"),
        "ACT": ("xt.0 acc.0 acc.1 f2.0- acc.2 xt.1 f2.2- acc.3 gelu.0 f2.3- acc.4 acc.5 gelu.1 acc.6 f2.1- gelu.2 "
               "acc.7 gelu.3 gelu.4 gelu.5 gelu.6 gelu.7 f1.0 f1.1 f1.2 f1.3"),
        "DVE": ("tr.0- red.0 red.1 tr.2- red.2 tr.3- red.3 scale.0 tr.1- scale.1 red.4 red.5 scale.2 back.0 scale.3 "
               "red.6 back.1 red.7 back.2 scale.4 scale.5 xx.1- xx.0- back.3 back.4 back.5 scale.6 scale.7 back.6 "
               "back.7"),
    },
    "mid": {
        "PE": ("i1.0 i1.1 tr.3- t2.0 t2.1 i1.3 acc.0 acc.1 tr.1- i1.2 acc.2 t2.3 t2.2 acc.3 tr.0- tr.2- turn.0 acc.4 "
               "turn.1 acc.5 acc.6 acc.7 turn.2 f2.1- back.1 turn.3 back.0 f2.2- turn.4 back.2 turn.5 back.3 f2.3- "
               "back.5 back.4 f2.0- f1.1 turn.6 turn.7 xx.1- back.6 f1.0 back.7 f1.2 xx.0- f1.3"),
        "ACT": ("t2.0 t2.1 acc.0 acc.1 acc.2 t2.3 acc.3 t2.2 acc.4 acc.5 acc.6 gelu.0 gelu.1 acc.7 gelu.2 gelu.3 "
               "f2.1- gelu.4 gelu.5 f2.2- f2.3- f2.0- gelu.6 f1.1 gelu.7 f1.0 f1.2 f1.3"),
        "DVE": ("i1.0 i1.1 tr.3- i1.3 red.0 red.1 tr.1- i1.2 scale.0 red.2 red.3 scale.1 red.4 red.5 tr.0- scale.2 "
               "red.6 scale.3 tr.2- red.7 back.1 scale.4 scale.5 back.0 back.2 back.3 back.5 scale.6 scale.7 back.4 "
               "xx.1- back.6 back.7 xx.0-"),
    },
    "last": {
        "PE": ("i1.0 i1.1 t2.0 t2.1 acc.0 acc.1 acc.2 i1.3 i1.2 t2.2 t2.3 acc.3 turn.0 turn.1 acc.4 fc1.2 turn.2 "
               "turn.3 fc1.3 fc1.0 acc.5 fc1.1 fc2.1 acc.6 fc1.6 fc1.7 fc2.0 fc1.4 fc1.5 acc.7 turn.4 fc2.3 fc2.2 "
               "fc1.8 turn.5 turn.6 fc1.11 turn.7 fc1.10 fc1.9 turn.8 fc2.5 fc1.15 fc1.14 fc2.4 fc1.13 fc1.12 turn.9 "
               "fc2.7 fc2.6 fc1.16 turn.10 fc3.0 fc1.17 turn.11 turn.12 fc1.18 fc1.19 fc2.8 fin.0 fc2.9 fc1.22 "
               "turn.13 fc1.23 turn.14 fc1.21 fc1.20 fc2.11 fc2.10 fc1.27 fc1.26 turn.15 fc1.25 fc1.24 fc2.13 fc2.12 "
               "fc1.29 fc1.28 fc1.31 fc1.30 fc2.14 fc2.15 fc3.1 fin.1"),
        "ACT": ("i1.0 i1.1 t2.0 t2.1 acc.0 acc.1 acc.2 i1.3 i1.2 t2.2 t2.3 gelu.0 gelu.1 acc.3 fc1.2 fc1.3 fc1.0 "
               "gelu.2 gelu.3 acc.4 acc.5 fc1.1 fc1.6 fc1.7 fc2.1 fc2.0 acc.6 fc1.4 fc1.5 gelu.4 fc2.3 fc2.2 fc1.8 "
               "gelu.5 acc.7 fc1.11 gelu.6 fc1.10 gelu.7 fc1.9 fc2.5 fc1.15 fc1.14 fc2.4 fc1.13 fc1.12 gelu.8 fc2.7 "
               "fc2.6 gelu.9 fc1.16 gelu.10 fc3.0 fc1.17 gelu.11 fc1.18 fc1.19 gelu.12 fc2.8 fin.0 fc2.9 fc1.22 "
               "fc1.23 fc1.21 fc1.20 gelu.13 fc2.11 fc2.10 fc1.27 fc1.26 fc1.25 fc1.24 gelu.14 fc2.13 gelu.15 fc1.29 "
               "fc1.28 fc2.12 fc1.31 fc1.30 fc2.14 fc2.15 fc3.1 fin.1"),
        "DVE": ("red.0 red.1 scale.0 scale.1 red.2 red.3 scale.2 scale.3 red.4 red.5 scale.4 scale.5 red.6 red.7 "
               "scale.6 scale.7"),
    },
}
RING = {
    "first": dict(xt="s", back="d", f1="s", tr="d", f2="s", xx="d"),
    "mid": dict(i1="d", t2="s", back="d", f1="s", tr="d", f2="s", xx="d"),
    "last": dict(i1="s", t2="s", fc1="s", fc2="d", fc3="s", fin="s"),
}


def parse(text):
    out = []
    for word in text.split():
        op, n = word.rstrip("-").split(".")
        out.append((op, int(n), word.endswith("-")))
    return out


def rsqrt(eng, out, var, tmp, chain, value, done, alone):
    k = 0

    def after(ins):
        nonlocal k
        k += 1
        ins.then_inc(chain, 1)
        eng.wait_ge(chain, value(k))
        alone(eng)

    v, a, b = tmp[0][:, 0:var.shape[1]], tmp[1][:, 0:var.shape[1]], tmp[2][:, 0:var.shape[1]]
    after(eng.tensor_scalar(v, var, EPS, None, ALU.add))
    after(eng.tensor_scalar(out.bitcast(mybir.dt.int32), v.bitcast(mybir.dt.int32), -0.5, float(0x5F3759DF), ALU.mult, ALU.add))
    for step in range(2):
        after(eng.tensor_tensor(a, out, out, ALU.mult))
        after(eng.tensor_tensor(a, a, v, ALU.mult))
        after(eng.tensor_scalar(b, a, 0.375, -1.25, ALU.mult, ALU.add))
        after(eng.tensor_tensor(a, a, b, ALU.mult))
        after(eng.tensor_scalar(a, a, 1.875, None, ALU.add))
        if step == 0:
            after(eng.tensor_tensor(out, out, a, ALU.mult))
        else:
            eng.tensor_tensor(out, out, a, ALU.mult).then_inc(done, 1)


def build(nc, ins, out_ap, B):
    NG = B // GI
    NT = B // 2
    TOKENS = B * S
    CAP = max(1, math.ceil(CAPACITY * TOKENS / E1))

    def at(name, ph, L, g, n):
        f, x, m, l = PER[name]
        per_layer = x + NG * m
        if ph == "first":
            return g * f + n
        if ph == "mix":
            return NG * f + L * per_layer + n
        if ph == "mid":
            return NG * f + x + L * per_layer + g * m + n
        return NG * f + 3 * per_layer + x + g * l + n

    ctx = ExitStack()
    with ctx:
        start = {}

        def sb(name, shape):
            t = ctx.enter_context(nc.sbuf_tensor(name, shape, F32))
            start[name] = nc.sbuf_base - 4 * shape[1]
            return t

        def rounded(name, where, col, cols):
            return nc.alloc_sbuf_tensor_at(name, [P, cols], F32, offset=start[where] + 4 * col)

        pb = lambda name: ctx.enter_context(nc.psum_tensor(name, [P, 512], F32))
        sem = lambda name: ctx.enter_context(nc.semaphore(name))

        h_dram = nc.dram_tensor("h_scratch", [NG, P, 2 * 16 * P], F32, kind="Internal").ap()
        y_dram = nc.dram_tensor("y_scratch", [B, KY * 2 * KX * C], F32, kind="Internal").ap()

        cst = sb("cst", [P, NC_EARLY])
        const = {k: cst[0:r, a:a + n] for k, (a, r, n) in CONST_COLS.items() if a < NC_EARLY}
        ident = const["ident"]
        spec = sb("spec", [P, 6 * KY * B])
        spec_v = spec[:].rearrange("p (q k b) -> p q k b", q=6, b=B)
        w_sb = sb("w_sb", [P, 2 * 2 * C * M1 * M2])
        w_v = w_sb[:].rearrange("p (w s o m) -> p w s o m", w=2, s=2, o=C)
        arena = sb("arena", [P, 9216])
        y_mix = arena[:].rearrange("p (k r x o) -> p k r x o", k=M1, r=2, x=KX)
        raw_more = sb("raw_more", [P, 3 * 512])
        raw = [arena[:, 0:512], arena[:, 512:1024]] + [raw_more[:, 512 * i:512 * i + 512] for i in range(3)] + [arena[:, 7424:7936]]
        V = arena[:, 1024:3072]
        T2 = arena[:, 3072:5120]
        TA = [V[:, 512 * k:512 * k + 512] for k in range(4)]
        Xs = arena[:, 5120:6656]
        Z = arena[:, 6656:7424]
        sq = [arena[:, 8192 + 512 * i:8192 + 512 * (i + 1)] for i in range(2)]
        h_in = sb("h_in", [P, 4096])
        h_new = sb("h_new", [P, 4096])
        h_rows = sb("h_rows", [P, 4096])
        y_in = sb("y_in", [96, 768])
        conv_bd = sb("conv_bd", [P, P])
        gam = sb("gam", [P, LAYERS + 1])
        bet = sb("bet", [P, LAYERS + 1])
        small = sb("small", [P, 224])
        var = [small[:, 32 * i:32 * i + 32] for i in range(2)]
        rstd = [small[:, 64 + 32 * i:96 + 32 * i] for i in range(2)]
        newton = [small[:, 128 + 32 * i:160 + 32 * i] for i in range(3)]
        y_mean = h_rows[:, 0:288]
        cbias = small[:, 0:32]
        x_in = h_in[:, 0:384].rearrange("p (t n) -> p t n", t=2)
        xT = T2[:, 0:1024].rearrange("p (t n) -> p t n", t=2)
        fc0 = T2[:, 1024:1536].rearrange("p (x o) -> p x o", x=16)
        fc0_mean = T2[:, 1536:1552]
        fc0_row = T2[64:65, 1600:1632]
        fc1_raw = w_sb[:, 0:256]
        fc1_hi, fc1_lo = rounded("fc1_hi", "w_sb", 256, 256)[:], rounded("fc1_lo", "w_sb", 768, 256)[:]
        h_split = rounded("h_split", "h_new", 0, 4096)
        fc1_b = w_sb[:, 512:513]
        fc2_w = w_sb[:, 513:577]
        fc2_b = w_sb[:, 577:578]
        fc3_pad = w_sb[:, 584:648].rearrange("p (k m) -> p k m", k=2)
        fc3_b = w_sb[:, 580:581]
        G1 = [w_sb[:, 1024 + 512 * i:1536 + 512 * i] for i in range(4)]
        split = [V[:, 1024 * i:1024 * i + 1024].rearrange("p (x a c) -> p x a c", a=2, c=C) for i in range(2)]
        G3 = w_sb[:, 3072:3584]
        G2 = w_sb[:, 4096:8192].rearrange("p (n c) -> p n c", n=8)
        tok = w_sb[:, 8192:8192 + NT * S]

        at_col = [0]

        def param(rows, cols):
            a = at_col[0]
            at_col[0] += cols
            return spec[0:rows, a:a + cols]

        w1a, w2a = param(P, E1 * F1), param(P, E1 * F1 // P * S)
        w1b, w2b = param(P, E2 * F2), param(P, E2 * F2 // P * S)
        b2a, b2b = param(8 * E1, 512), param(8 * E2, 512)
        wq, wk, wv = param(P, S), param(P, S), param(P, S)
        gwa, gwb = param(P, E1), param(P, E2)
        gba, gbb = param(P, E1), param(P, E2)
        b1a, b1b = param(P, E1 * F1 // P), param(P, E2 * F2 // P)
        wg0, wg1 = param(P, P), param(P, P)
        wg0T, wg1T = param(P, P), param(P, P)
        gbias = param(P, 4)
        ngbias = param(P, 2)
        gamma, beta = param(P, S), param(P, S)
        late = param(P, NC_COLS - NC_EARLY)
        const |= {k: late[0:r, a - NC_EARLY:a - NC_EARLY + n] for k, (a, r, n) in CONST_COLS.items() if a >= NC_EARLY}
        XT = h_rows[:, 0:TOKENS]
        XT_split = rounded("XT_split", "h_rows", 0, TOKENS)
        w1a_hi = rounded("w1a_hi", "w_sb", 10240, E1 * F1)[:]
        w1b_hi = rounded("w1b_hi", "w_sb", 10240 + E1 * F1, E2 * F2)[:]
        w1a_lo = rounded("w1a_lo", "spec", 0, E1 * F1)[:]
        w1b_lo = rounded("w1b_lo", "spec", E1 * F1 + E1 * F1 // P * S, E2 * F2)[:]
        QT, KT = arena[0:64, 0:4096], arena[0:64, 4096:8192]
        VB = h_in[0:64, :]
        Sx = h_new[:, 0:2048]
        PT = w_sb[0:64, 10240:14336]
        hid = [w_sb[:, 14336 + 512 * i:14848 + 512 * i] for i in range(8)]
        X = tok
        Y = h_new[:, 2048:4096]
        Z2 = w_sb[:, 0:2048]
        Z3 = w_sb[:, 2048:4096]
        tiny = [w_sb[:, 4096 + 512 * i:4608 + 512 * i] for i in range(8)]
        gates = arena[:, 8192:8704]
        GT = arena[:, 8704:9216]
        GA, GZ = arena[:, 0:2048], arena[:, 2048:4096]
        GS, GV = arena[:, 4096:6144], arena[:, 6144:8192]
        OUT0, OUT1 = h_in[:, 0:2048], h_in[:, 2048:4096]

        pA = [pb("pA0"), pb("pA1")]
        pT = [pb("pT0"), pb("pT1")]
        pD = [pb("pD0"), pb("pD1")]
        pS = [pb("pS0"), pb("pS1")]

        names = ["d_full", "d_free", "s_full", "s_free", "acc_full", "squared", "summed", "rstd_ok",
                 "turned", "h_new_ok", "x_loaded", "y_loaded", "h_loaded0", "h_loaded1", "stored0", "stored1", "fc0_clear", "y_stored", "w_loaded",
                 "w_signed", "conv_cleared", "conv_loaded", "conv_chain", "cst_loaded", "ln_loaded",
                 "fc0_loaded", "fc0_chain", "mlp_cleared", "mlp_loaded", "y_chain", "normed", "pool_chain"]
        names += ["td_full", "td_free", "ts_full", "ts_free", "par_cleared", "par_loaded", "tok_ready", "v_chain", "shifted",
                  "exped", "e_subbed", "fc1_bias", "mlp_ready", "w1_split", "upper", "e_exped", "gated", "acc_done", "out_stored", "wg_scaled",
                  "scored", "gru_act", "gru_out", "ones_set", "passed"]
        s = {n: sem(n) for n in names}
        TD = [pD[0], pD[1], pA[0], pA[1]]
        TS = [pS[0], pS[1], pT[0], pT[1]]
        ctx.enter_context(nc.allow_non_contiguous_dma(reason="small parameters, once per layer"))
        block = ctx.enter_context(nc.Block())
        h_v = lambda t: t[:].rearrange("p (t q n) -> p t q n", t=2, q=16)
        hin_v, hnew_v = h_v(h_in), h_v(h_new)
        hrow_v = h_rows[:].rearrange("p (t n) -> p t n", t=2)

        LAYER1 = dict(E=E1, H=F1 // P, w1=(w1a_hi, w1a_lo), w2=w2a, gw=gwa, b1=b1a, b2=b2a)
        LAYER2 = dict(E=E2, H=F2 // P, w1=(w1b_hi, w1b_lo), w2=w2b, gw=gwb, b1=b1b, b2=b2b)

        def token_pe(pe):
            n = {"d": 0, "s": 0}
            ring = {"d": TD, "s": TS}

            def bank(which):
                pe.wait_ge(s[f"t{which}_free"], n[which] + 1)
                return ring[which][n[which] % 4]

            def sent(which, mm):
                mm.then_inc(s[f"t{which}_full"], 1)
                n[which] += 1

            def taken(which, back=0):
                pe.wait_ge(s[f"t{which}_free"], n[which] + 4 - back)

            def turn_x(stage):
                pe.wait_ge(s["tok_ready"], stage)
                for j in range(8):
                    b = bank("s")
                    for i in range(4):
                        t = 4 * j + i
                        if stage in (2, 4):
                            for h in range(2):
                                mm = pe.matmul(b[64 * h:64 * h + 64, 128 * i:128 * i + 128], X[:, S * t:S * t + S], ident,
                                               start=True, stop=True)
                        else:
                            mm = pe.transpose(b[0:64, 128 * i:128 * i + 128], X[:, S * t:S * t + S], ident)
                    sent("s", mm)
                taken("s")

            pe.wait_ge(s["par_loaded"], 16 * N_PARAMS)
            turn_x(1)
            pe.wait_ge(s["ones_set"], 2)
            for j in range(8):
                for which, w in (("d", wq), ("s", wk)):
                    b = bank(which)
                    sent(which, pe.matmul(b[0:64, :], w, XT[:, 512 * j:512 * j + 512], start=True, stop=True))
            for j in range(8):
                b = bank("d")
                for i in range(8):
                    mm = pe.matmul(b[0:64, S * i:S * i + S], XT[:, S * (8 * j + i):S * (8 * j + i + 1)], wv, start=True, stop=True)
                sent("d", mm)
            taken("d")
            taken("s")
            for j in range(4):
                b = bank("d")
                for i in range(8):
                    for h in range(2):
                        c = 128 * (8 * j + i) + 64 * h
                        mm = pe.matmul(b[64 * h:64 * h + 64, S * i:S * i + S], QT[:, c:c + 64], KT[:, c:c + 64], start=True, stop=True)
                sent("d", mm)
            for j in range(8):
                pe.wait_ge(s["exped"], j // 2 + 1)
                b = bank("s")
                for i in range(4):
                    t = 4 * j + i
                    mm = pe.transpose(b[0:64, 128 * i:128 * i + 128], Sx[:, S * t:S * t + S], ident)
                sent("s", mm)
            taken("s")
            for j in range(4):
                b = bank("d")
                for i in range(8):
                    for h in range(2):
                        c = 128 * (8 * j + i) + 64 * h
                        mm = pe.matmul(b[64 * h:64 * h + 64, S * i:S * i + S], PT[:, c:c + 64],
                                       VB[:, c:c + 64], start=True, stop=True)
                sent("d", mm)

            def experts(stage, E, H, w1, w2, gw, b2, **_):
                turn_x(stage)
                b = bank("d")
                for t in range(NT):
                    mm = pe.matmul(b[:, E * t:E * t + E], XT_split[:, 128 * t:128 * t + 128], gw, start=True, stop=True)
                sent("d", mm)
                def hidden(e, k):
                    for h in range(H):
                        b = bank("s")
                        c = (e * H + h) * P
                        for w in w1:
                            mm = pe.matmul(b[:], w[:, c:c + P].bitcast(F32R), XT_split[:, 512 * k:512 * k + 512].bitcast(F32R),
                                           start=(w is w1[0]), stop=(w is w1[1]))
                        sent("s", mm)

                def output(e, k, b):
                    for i in range(4):
                        for h in range(H):
                            slot = ((e * 8 + k) * H + h) % 8
                            mm = pe.matmul(b[:, S * (4 * (k % 2) + i):S * (4 * (k % 2) + i) + S],
                                           hid[slot][:, 128 * i:128 * i + 128], w2[:, (e * H + h) * S:(e * H + h) * S + S],
                                           start=(h == 0), stop=(h == H - 1))
                    return mm

                pe.wait_ge(s["w1_split"], 2 if E == E1 else 4)
                todo = [(e, k) for e in range(E) for k in range(8)]
                ahead = 8 // H - 1
                for block in todo[:ahead]:
                    hidden(*block)
                if E == E1:
                    pe.wait_ge(s["scored"], 1)
                    for lhs in ("upto", "ones"):
                        b = bank("d")
                        sent("d", pe.matmul(b[:, 0:E * NT], const[lhs], gates[:, 0:E * NT], start=True, stop=True))
                for i, (e, k) in enumerate(todo):
                    if i + ahead < len(todo):
                        hidden(*todo[i + ahead])
                    taken("s", H * min(ahead, len(todo) - 1 - i))
                    if k % 2 == 0:
                        b = bank("d")
                    mm = output(e, k, b)
                    if k % 2:
                        sent("d", mm)
                pe.wait_ge(s["gated"], 1 if E == E1 else 2)
                b = bank("s")
                for j in range(NT // 8):
                    mm = pe.transpose(b[0:8 * E, 128 * j:128 * j + 128], gates[:, 8 * E * j:8 * E * j + 8 * E], ident)
                sent("s", mm)
                taken("s")
                for j in range(NT // 8):
                    b = bank("d")
                    sent("d", pe.matmul(b[:], GT[0:8 * E, 128 * j:128 * j + 128], b2[0:8 * E, :], start=True, stop=True))

            experts(2, **LAYER1)

            b = bank("s")
            pe.transpose(b[:, 0:P], wg0, ident)
            sent("s", pe.transpose(b[:, P:2 * P], wg1, ident))
            turn_x(3)
            for n_layer in range(2):
                if n_layer == 1:
                    pe.wait_ge(s["gru_out"], 1)
                for part in range(2):
                    for j in range(4):
                        b = bank("s" if part == 0 else "d")
                        for h in range(2):
                            if n_layer == 0:
                                mm = pe.matmul(b[64 * h:64 * h + 64, :], wg0T[0:64, 64 * part:64 * part + 64],
                                               XT[0:64, 2048 * h + 512 * j:2048 * h + 512 * j + 512], start=True, stop=True)
                            else:
                                q = slice(64 * h, 64 * h + 64)
                                mm = pe.matmul(b[q, :], wg1T[q, 64 * part:64 * part + 64], OUT0[q, 512 * j:512 * j + 512],
                                               start=True, stop=True)
                        sent("s" if part == 0 else "d", mm)
            pe.wait_ge(s["gru_out"], 2)
            for j in range(4):
                b = bank("d")
                for i in range(4):
                    t = 4 * j + i
                    mm = pe.transpose(b[:, 128 * i:128 * i + 128], OUT1[:, 128 * t:128 * t + 128], ident)
                sent("d", mm)

            experts(4, **LAYER2)

        def token_act(act):
            n = [0]
            act.sem_inc(s["ts_free"], 4)

            def take():
                n[0] += 1
                act.wait_ge(s["ts_full"], n[0])
                return TS[(n[0] - 1) % 4]

            act.wait_ge(s["s_free"], at("s_out", "last", LAYERS - 1, NG, 0) + 2)
            act.sem_inc(s["tok_ready"], 1)

            def turn_x():
                for j in range(8):
                    act.copy(XT[0:64, 512 * j:512 * j + 512], take()[0:64, :]).then_inc(s["ts_free"], 1)

            turn_x()
            for j in range(8):
                act.copy(KT[:, 512 * j:512 * j + 512], take()[0:64, :]).then_inc(s["ts_free"], 1)
            for j in range(4):
                act.wait_ge(s["shifted"], j + 1)
                act.activation(Sx[:, 512 * j:512 * j + 512], Sx[:, 512 * j:512 * j + 512], ACT.Exp, scale=S ** -0.5).then_inc(s["exped"], 1)
            for j in range(8):
                act.copy(PT[:, 512 * j:512 * j + 512], take()[0:64, :]).then_inc(s["ts_free"], 1)

            def experts(E, H, b1, **_):
                for j in range(8):
                    b = take()
                    act.copy(XT_split[:, 512 * j:512 * j + 512].bitcast(F32R), b[:]).then_inc(s["upper"], 1)
                act.wait_ge(s["e_subbed"], 1 if E == E1 else 2)
                m = E * NT if E == E1 else NT
                act.activation(tiny[1][:, 0:m], tiny[0][:, 0:m], ACT.Exp).then_inc(s["e_exped"], 1)
                for i in range(E * 8 * H):
                    c = i // (8 * H) * H + i % H
                    act.activation(hid[i % 8], take()[:], ACT.Relu, bias=b1[:, c:c + 1]).then_inc(s["ts_free"], 1)
                act.copy(GT[0:8 * E, :], take()[0:8 * E, :]).then_inc(s["ts_free"], 1)

            experts(**LAYER1)
            b = take()
            act.copy(wg0T, b[:, 0:P])
            act.copy(wg1T, b[:, P:2 * P]).then_inc(s["ts_free"], 1)
            turn_x()
            act.wait_ge(s["wg_scaled"], 1)
            for layer in range(2):
                for j in range(4):
                    c = slice(512 * j, 512 * j + 512)
                    b = take()
                    act.activation(GZ[:, c], b[:], ACT.Sigmoid, bias=gbias[:, 2 * layer:2 * layer + 1])
                    act.activation(GA[:, c], b[:], ACT.Sigmoid, bias=ngbias[:, layer:layer + 1], scale=-1.0).then_inc(s["ts_free"], 1)
                for j in range(4):
                    c = slice(512 * j, 512 * j + 512)
                    act.wait_ge(s["td_full"], GRU_D[layer] + j + 1)
                    act.activation(GS[:, c], TD[(GRU_D[layer] + j) % 4][:], ACT.Sigmoid,
                                   bias=gbias[:, 2 * layer + 1:2 * layer + 2]).then_inc(s["gru_act"], 1)
            experts(**LAYER2)

        d_attn = 8 + 8 + 4 + 4
        d_ffn = 1 + 2 + E1 * 4 + NT // 8
        GRU_D = [d_attn + d_ffn, d_attn + d_ffn + 4]
        s_attn = 8 + 8 + 8
        s_ffn = 8 + E1 * 8 * (F1 // P) + 1
        S_TURNED = [s_attn, s_attn + s_ffn + 1 + 8 + 8]

        def token_dve(dve):
            n = [0]
            chain = [0]
            dve.sem_inc(s["td_free"], 4)

            def take():
                n[0] += 1
                dve.wait_ge(s["td_full"], n[0])
                return TD[(n[0] - 1) % 4]

            def link(ins):
                chain[0] += 1
                ins.then_inc(s["v_chain"], 1)
                dve.wait_ge(s["v_chain"], chain[0])

            by_tile = lambda a, w=S: a.rearrange("p (t x) -> p t x", x=w)
            wide = lambda a, w=S, m=NT: a.rearrange("p (t x) -> p t x", x=1).broadcast_to([P, m, w])

            def rsqrt_here(out, var):
                v, a, b = tiny[5][:, 0:NT], tiny[6][:, 0:NT], tiny[7][:, 0:NT]
                link(dve.tensor_scalar(v, var, EPS, None, ALU.add))
                link(dve.tensor_scalar(out.bitcast(mybir.dt.int32), v.bitcast(mybir.dt.int32), -0.5, float(0x5F3759DF), ALU.mult, ALU.add))
                for _ in range(2):
                    link(dve.tensor_tensor(a, out, out, ALU.mult))
                    link(dve.tensor_tensor(a, a, v, ALU.mult))
                    link(dve.tensor_scalar(b, a, 0.375, -1.25, ALU.mult, ALU.add))
                    link(dve.tensor_tensor(a, a, b, ALU.mult))
                    link(dve.scalar_tensor_tensor(out=out, in0=a, scalar=1.875, in1=out, op0=ALU.add, op1=ALU.mult))

            def layer_norm(x):
                mean, var, r = tiny[4][:, 0:NT], tiny[4][:, 64:64 + NT], tiny[4][:, 128:128 + NT]
                link(dve.reduce_sum(mean, by_tile(x), axis=AX))
                link(dve.scalar_tensor_tensor(out=by_tile(x), in0=wide(mean), scalar=-1.0 / S, in1=by_tile(x), op0=ALU.mult, op1=ALU.add))
                link(dve.tensor_tensor(Z2, x, x, ALU.mult))
                link(dve.reduce_sum(var, by_tile(Z2), axis=AX))
                link(dve.tensor_scalar(var, var, 1.0 / S, None, ALU.mult))
                rsqrt_here(r, var)
                link(dve.tensor_tensor(by_tile(x), by_tile(x), wide(r), ALU.mult))

            dve.wait_ge(s["par_loaded"], 16 * N_PARAMS)
            
            link(dve.tensor_scalar(ngbias, gbias.rearrange("p (l g) -> p g l", g=2)[:, 0, :], -1.0, None, ALU.mult))
            for j in range(8):
                dve.tensor_copy(QT[:, 512 * j:512 * j + 512], take()[0:64, :]).then_inc(s["td_free"], 1)
            for j in range(8):
                dve.tensor_copy(VB[:, 512 * j:512 * j + 512], take()[0:64, :]).then_inc(s["td_free"], 1)
            top, den = tiny[0][:, 0:NT], tiny[1][:, 0:NT]
            for j in range(4):
                b = take()
                m = top[:, 8 * j:8 * j + 8]
                link(dve.reduce_max(m, by_tile(b[:]), axis=AX))
                dve.tensor_tensor(by_tile(Sx[:, 512 * j:512 * j + 512]), by_tile(b[:]), wide(m, m=8), ALU.subtract).then_inc(s["shifted"], 1)
                dve.wait_ge(s["shifted"], j + 1)
                dve.sem_inc(s["td_free"], 1)
            for j in range(4):
                dve.wait_ge(s["exped"], j + 1)
                dve.reduce_sum(den[:, 8 * j:8 * j + 8], by_tile(Sx[:, 512 * j:512 * j + 512]), axis=AX)
            link(dve.memset(tiny[2][:, 0:1], 0.0))
            link(dve.reciprocal(den, den))
            for j in range(4):
                b = take()
                c = slice(512 * j, 512 * j + 512)
                dve.tensor_tensor(by_tile(Y[:, c]), by_tile(b[:]), wide(den[:, 8 * j:8 * j + 8], m=8), ALU.mult).then_inc(s["td_free"], 1)
            dve.wait_ge(s["td_free"], n[0] + 4)
            link(dve.tensor_tensor(X, X, Y, ALU.add))
            layer_norm(X)
            dve.sem_inc(s["tok_ready"], 1)

            def lower_bits(stage):
                for j in range(8):
                    c = slice(512 * j, 512 * j + 512)
                    dve.wait_ge(s["upper"], 8 * stage + j + 1)
                    b = TS[(S_TURNED[stage] + j) % 4]
                    dve.tensor_tensor(XT_split[64:128, c].bitcast(F32R), b[64:128, :], XT_split[64:128, c], ALU.subtract).then_inc(s["ts_free"], 1)

            def combine(E):
                for e in range(E):
                    for j in range(4):
                        b = take()
                        c = slice(512 * j, 512 * j + 512)
                        gv = gates[:, 8 * E * j:8 * E * j + 8 * E].rearrange("p (t e) -> p t e", e=E)[:, :, e:e + 1].broadcast_to([P, 8, S])
                        if e == 0:
                            dve.tensor_tensor(by_tile(Y[:, c]), by_tile(b[:]), gv, ALU.mult).then_inc(s["td_free"], 1)
                        else:
                            dve.tensor_tensor(by_tile(Z3[:, c]), by_tile(b[:]), gv, ALU.mult).then_inc(s["td_free"], 1)
                            dve.wait_ge(s["td_free"], n[0] + 4)
                            dve.tensor_tensor(Y[:, c], Y[:, c], Z3[:, c], ALU.add)
                link(dve.memset(tiny[2][:, 0:1], 0.0))
                for j in range(4):
                    b = take()
                    c = slice(512 * j, 512 * j + 512)
                    dve.tensor_tensor(Y[:, c], Y[:, c], b[:], ALU.add).then_inc(s["td_free"], 1)
                dve.wait_ge(s["td_free"], n[0] + 4)

            def first_best(out, value, best, E):
                fall = const["falling"][:, E2 - E:E2].rearrange("p (t e) -> p t e", t=1).broadcast_to([P, NT, E])
                a, m = tiny[2][:, 0:E * NT], tiny[3][:, 0:NT]
                link(dve.tensor_tensor(by_tile(a, E), by_tile(value, E), wide(best, E), ALU.is_equal))
                link(dve.tensor_tensor(by_tile(a, E), by_tile(a, E), fall, ALU.mult))
                link(dve.reduce_max(m, by_tile(a, E), axis=AX))
                link(dve.tensor_tensor(by_tile(out, E), by_tile(a, E), wide(m, E), ALU.is_equal))

            lower_bits(0)
            gate_bias = lambda E: (gba if E == E1 else gbb).rearrange("p (t e) -> p t e", t=1).broadcast_to([P, NT, E])
            E = E1
            m = E * NT
            logits, best, shifted = tiny[0][:, m:2 * m], tiny[4][:, 256:256 + NT], tiny[0][:, 0:m]
            link(dve.tensor_tensor(by_tile(logits, E), by_tile(take()[:, 0:m], E), gate_bias(E), ALU.add))
            dve.sem_inc(s["td_free"], 1)
            link(dve.reduce_max(best, by_tile(logits, E), axis=AX))
            dve.tensor_tensor(by_tile(shifted, E), by_tile(logits, E), wide(best, E), ALU.subtract).then_inc(s["e_subbed"], 1)
            first_best(gates[:, 0:m], logits, best, E)
            dve.sem_inc(s["scored"], 1)
            inclusive, totals, running, rank = tiny[5][:, 0:m], tiny[5][:, m:2 * m], tiny[6][:, 0:m], tiny[3][:, 64:64 + NT]
            link(dve.tensor_copy(inclusive, take()[:, 0:m]))
            dve.sem_inc(s["td_free"], 1)
            link(dve.tensor_copy(totals, take()[:, 0:m]))
            dve.sem_inc(s["td_free"], 1)
            for e in range(E):
                by_e = lambda a: a.rearrange("p (t e) -> p e t", e=E)[:, e, :]
                dve.tensor_tensor_scan(by_e(running), const["ones"][:, 0:NT], by_e(totals), 0.0, ALU.mult, ALU.add)
            link(dve.memset(tiny[7][:, 0:1], 0.0))
            link(dve.tensor_tensor(running, running, totals, ALU.subtract))
            link(dve.tensor_tensor(running, running, inclusive, ALU.add))
            link(dve.tensor_tensor(running, running, gates[:, 0:m], ALU.mult))
            link(dve.reduce_sum(rank, by_tile(running, E), axis=AX))
            keep, total = tiny[3][:, 128:128 + NT], tiny[3][:, 192:192 + NT]
            link(dve.tensor_scalar(keep, rank, float(CAP), None, ALU.is_le))
            dve.wait_ge(s["e_exped"], 1)
            link(dve.reduce_sum(total, by_tile(tiny[1][:, 0:m], E), axis=AX))
            link(dve.reciprocal(total, total))
            link(dve.tensor_tensor(keep, keep, total, ALU.mult))
            link(dve.tensor_tensor(by_tile(gates[:, 0:m], E), by_tile(gates[:, 0:m], E), wide(keep, E), ALU.mult))
            dve.sem_inc(s["gated"], 1)
            combine(E1)
            I32 = mybir.dt.int32
            for i, value in enumerate((0.0, 1.0e4, -1.0e4)):
                link(dve.memset(Z2[:, i:i + 1], value))
            fill = lambda i: Z2[:, i:i + 1].broadcast_to([P, NT * S])
            link(dve.tensor_tensor(Z3.bitcast(I32), Y, Y, ALU.not_equal))
            link(dve.copy_predicated(Y, Z3.bitcast(I32), fill(0)))
            link(dve.tensor_scalar(Z3.bitcast(I32), Y, F32_MAX, None, ALU.is_gt))
            link(dve.copy_predicated(Y, Z3.bitcast(I32), fill(1)))
            link(dve.tensor_scalar(Z3.bitcast(I32), Y, -F32_MAX, None, ALU.is_lt))
            link(dve.copy_predicated(Y, Z3.bitcast(I32), fill(2)))
            link(dve.tensor_tensor(X, X, Y, ALU.add))
            layer_norm(X)
            dve.sem_inc(s["wg_scaled"], 1)
            dve.sem_inc(s["tok_ready"], 1)

            for layer in range(2):
                for j in range(4):
                    c = slice(512 * j, 512 * j + 512)
                    b = take()
                    dve.wait_ge(s["gru_act"], 4 * layer + j + 1)
                    link(dve.tensor_scalar(GV[:, c], b[:], gbias[:, 2 * layer + 1:2 * layer + 2], 0.5, ALU.add, ALU.add))
                    dve.sem_inc(s["td_free"], 1)
                    link(dve.tensor_tensor(GV[:, c], GV[:, c], GS[:, c], ALU.max))
                    link(dve.tensor_tensor(GV[:, c], GV[:, c], GZ[:, c], ALU.mult))
                head = lambda a: a.rearrange("p (b t) -> p b t", t=S)[:, :, 0]
                link(dve.scalar_tensor_tensor(out=head(GV), in0=head(GA), scalar=0.5, in1=head(GV), op0=ALU.mult, op1=ALU.add))
                link(dve.memset(head(GA), 0.0))
                dve.tensor_tensor_scan((OUT0, OUT1)[layer], GA, GV, 0.0, ALU.mult, ALU.add).then_inc(s["gru_out"], 1)
            xv = X.rearrange("p (h t x) -> p t h x", h=2, x=S)
            for j in range(4):
                b = take()
                dve.tensor_tensor(xv[:, 4 * j:4 * j + 4], xv[:, 4 * j:4 * j + 4],
                                  b[:].rearrange("p (t h x) -> p t h x", h=2, x=S), ALU.add).then_inc(s["td_free"], 1)
            dve.wait_ge(s["td_free"], n[0] + 4)
            layer_norm(X)
            dve.sem_inc(s["tok_ready"], 1)

            lower_bits(1)
            E = E2
            m = E * NT
            logits, best, second = Z2[:, 0:m], tiny[4][:, 256:256 + NT], tiny[4][:, 320:320 + NT]
            rest = Z2[:, m:2 * m]
            pick1, pick2 = Z2[:, 2 * m:3 * m], Z2[:, 3 * m:4 * m]
            link(dve.tensor_tensor(by_tile(logits, E), by_tile(take()[:, 0:m], E), gate_bias(E), ALU.add))
            dve.sem_inc(s["td_free"], 1)
            link(dve.reduce_max(best, by_tile(logits, E), axis=AX))
            first_best(pick1, logits, best, E)
            link(dve.scalar_tensor_tensor(out=rest, in0=pick1, scalar=-HUGE, in1=logits, op0=ALU.mult, op1=ALU.add))
            link(dve.reduce_max(second, by_tile(rest, E), axis=AX))
            dve.tensor_tensor(tiny[0][:, 0:NT], second, best, ALU.subtract).then_inc(s["e_subbed"], 1)
            first_best(pick2, rest, second, E)
            dve.wait_ge(s["e_exped"], 2)
            ex, inv = tiny[1][:, 0:NT], tiny[3][:, 64:64 + NT]
            link(dve.tensor_scalar(inv, ex, 1.0, None, ALU.add))
            link(dve.reciprocal(inv, inv))
            link(dve.tensor_tensor(by_tile(pick1, E), by_tile(pick1, E), wide(inv, E), ALU.mult))
            link(dve.tensor_tensor(inv, inv, ex, ALU.mult))
            link(dve.tensor_tensor(by_tile(pick2, E), by_tile(pick2, E), wide(inv, E), ALU.mult))
            link(dve.tensor_tensor(gates[:, 0:m], pick1, pick2, ALU.add))
            dve.sem_inc(s["gated"], 1)
            combine(E2)
            link(dve.tensor_tensor(Y, Y, X, ALU.add))
            layer_norm(Y)
            g_t = lambda a: a.rearrange("p (t x) -> p t x", t=1).broadcast_to([P, NT, S])
            link(dve.tensor_tensor(by_tile(Y), by_tile(Y), g_t(gamma), ALU.mult))
            link(dve.tensor_tensor(by_tile(Y), by_tile(Y), g_t(beta), ALU.add))
            link(dve.tensor_tensor(X, X, Y, ALU.add))
            layer_norm(X)
            dve.sem_inc(s["acc_done"], 1)

        def token_pool(pool):
            pool.wait_ge(s["par_loaded"], 16 * N_PARAMS)
            pool.wait_ge(s["tok_ready"], 2)
            for n, (hi, lo, w) in enumerate(((w1a_hi, w1a_lo, w1a), (w1b_hi, w1b_lo, w1b))):
                pool.tensor_copy(hi.bitcast(F32R), w).then_inc(s["w1_split"], 1)
                pool.wait_ge(s["w1_split"], 2 * n + 1)
                pool.tensor_tensor(lo.bitcast(F32R), w, hi, ALU.subtract).then_inc(s["w1_split"], 1)

        raw_of = lambda n: raw[(0, 1, 2, 3, 0, 1, 4, 5)[n]]
        first_group = lambda g: isinstance(g, int) and g == 0

        def alone(eng):
            eng.sem_inc(s["passed"], 1)

        class Phase:

            def __init__(self, ph, L):
                self.ph, self.L = ph, L
                self.order = {e: parse(t) for e, t in ORDER[ph].items()}
                self.place = {}
                for ring in "ds":
                    sent = [(op, n, late) for op, n, late in self.order["PE"] if RING[ph].get(op) == ring]
                    heads = sum(not late for _, _, late in sent)
                    for i, (op, n, late) in enumerate(sent):
                        before = sum(not x for _, _, x in sent[:i])
                        self.place[op, n] = (ring, late, i, before, heads)

            def product(self, op, n, g):
                ring, late, i, before, heads = self.place[op, n]
                banks, name = (pD if ring == "d" else pS), ring + "_out"
                if not late and isinstance(g, int) and g == 0:
                    return ring, banks[before % 2], at(name, self.ph, self.L, 0, before + 1)
                if late and isinstance(g, int) and g == NG - 1:
                    i -= before
                return ring, banks[(heads + i) % 2], at(name, self.ph, self.L, g if late else g - 1, heads + i + 1)

            def ends(self, op):
                ns = [n for late in (False, True) for o, n, l in self.order["PE"] if o == op and l == late]
                return ns[0], ns[-1]

            def sent(self, eng, op, n, g):
                ring, bank, v = self.product(op, n, g)
                eng.wait_ge(s[ring + "_full"], v)
                return bank

            def taken(self, eng, *keys, g):
                last = max(keys, key=lambda k: self.place[k][1:3])
                ring, _, v = self.product(*last, g)
                eng.wait_ge(s[ring + "_free"], v + 2)

        def phases(eng, name, mix, steps, before_last=None):
            def phase(ph, L):
                p = Phase(ph, L)
                do = steps(p)

                def body(b):
                    for op, n, late in p.order[name]:
                        if isinstance(b, int) and (b == 0 and late or b == NG and not late):
                            continue
                        do[op](n, b - 1 if late else b)

                body(0)
                body(1)
                with eng.Fori(2, NG) as b:
                    body(b)
                body(NG)

            phase("first", 0)
            with eng.Fori(0, LAYERS - 1) as L:
                mix(L)
                phase("mid", L)
            mix(LAYERS - 1)
            if before_last:
                before_last()
            phase("last", LAYERS - 1)

        @block.sync
        def _(sp):
            def load_x(g):
                src = ins["x"].rearrange("(g t b) y x c -> g (b y) t (x c)", t=2, b=2)
                sp.dma_start(x_in, src[g]).then_inc(s["x_loaded"], 16)

            sp.dma_start(cst[:], ins["consts"][:, 0:NC_EARLY]).then_inc(s["cst_loaded"], 16)
            load_x(0)
            sp.wait_ge(s["fc0_chain"], 1)
            for x in range(16):
                sp.dma_start(fc0[3 * x:3 * x + 3, x, :], ins["L0_tok_fc0_w"]).then_inc(s["fc0_loaded"], 16)
            sp.dma_start(fc0_row, ins["L0_tok_fc0_b"].rearrange("(p o) -> p o", p=1)).then_inc(s["fc0_loaded"], 16)
            for j in range(4):
                q = slice(32 * j, 32 * j + 32)
                for t, first, layers in ((gam, "L0_tok_ln0_g", "L0_tok_ln_g"), (bet, "L0_tok_ln0_b", "L0_tok_ln_b")):
                    sp.dma_start(t[q, 0:1], ins[first].rearrange("(p o) -> p o", o=1)).then_inc(s["ln_loaded"], 16)
                    sp.dma_start(t[q, 1:LAYERS + 1], ins[layers].rearrange("l c -> c l")).then_inc(s["ln_loaded"], 16)


            def load_y(g):
                src = y_dram.rearrange("(g t b) (k n) -> g t (b k) n", t=2, b=2, k=2 * KY)
                for t in range(2):
                    sp.dma_start(y_in[:, 384 * t:384 * t + 384], src[g, t]).then_inc(s["y_loaded"], 16)

            def load_h(g, t):
                c = slice(2048 * t, 2048 * t + 2048)
                sp.dma_start(h_in[:, c], h_dram[g][:, c]).then_inc(s[f"h_loaded{t}"], 16)

            def store_h(ph, L, g, t):
                c = slice(2048 * t, 2048 * t + 2048)
                sp.wait_ge(s["h_new_ok"], at("h_new", ph, L, g, 4 * t + 4))
                sp.dma_start(h_dram[g][:, c], h_new[:, c]).then_inc(s[f"stored{t}"], 16)

            def weights(L):
                for w, (wr, wi) in enumerate((("L0_tok_w1r", "L0_tok_w1i"), ("L0_tok_w2r", "L0_tok_w2i"))):
                    for k in range(2):
                        for r in range(2):
                            q = slice(64 * k + 32 * r, 64 * k + 32 * r + 32)
                            for slot in range(2):
                                name = wr if slot == r else wi
                                sp.dma_start(w_v[q, w, slot].rearrange("p o m -> p (o m)"),
                                             ins[name][L].rearrange("i o x y -> i (o x y)")).then_inc(s["w_loaded"], 16)

            def conv_params(L):
                sp.wait_ge(s["conv_cleared"], 1)
                sp.wait_ge(s["acc_full"], at("acc", "mix", L, 0, 0))
                for j in range(4):
                    sp.dma_start(conv_bd[32 * j:32 * j + 32, 32 * j:32 * j + 32],
                                 ins["L0_tok_conv_w"][L].rearrange("o c -> c o")).then_inc(s["conv_loaded"], 16)
                sp.wait_ge(s["rstd_ok"], at("rstd", "mix", L, 0, 0))
                sp.dma_start(cbias[0:B, :], ins["L0_tok_conv_b"][L].partition_broadcast(B)).then_inc(s["conv_loaded"], 16)

            def y_store(L):
                for half in range(2):
                    sp.wait_ge(s["y_chain"], at("y_chain", "mix", L, 0, 12 * half + 12))
                    n = slice(4608 * half, 4608 * half + 4608)
                    for w in range(2):
                        dst = y_dram.rearrange("b (w n) -> w b n", w=2)[w]
                        sp.dma_start(dst[:, n], arena[64 * w:64 * w + B, n]).then_inc(s["y_stored"], 16)

            def y_is_stored(L):
                sp.wait_ge(s["y_stored"], at("y_stored", "mix", L, 0, 64))

            def token_params():
                sp.wait_ge(s["par_cleared"], 1)
                col = lambda a: a.rearrange("(p o) -> p o", o=1)
                row = lambda a: a.rearrange("(o n) -> o n", o=1)
                dmas = [
                    (late, ins["consts"][:, NC_EARLY:]),
                    (wq[0:64], ins["L0_attn_Wq"]), (wq[64:65], row(ins["L0_attn_bq"])),
                    (wk[0:64], ins["L0_attn_Wk"]), (wk[64:65], row(ins["L0_attn_bk"])),
                    (wv[0:64], ins["L0_attn_Wv"]), (wv[64:65], row(ins["L0_attn_bv"])),
                    (gba, ins["L0_ffn_gate_b"].partition_broadcast(P)), (gbb, ins["L1_ffn_gate_b"].partition_broadcast(P)),
                    (b1a.rearrange("p (e h) -> p e h", e=E1), ins["L0_ffn_b1"].rearrange("e (h p) -> p e h", p=P)),
                    (b1b, ins["L1_ffn_b1"].rearrange("e p -> p e")),
                    (w2a.rearrange("p (e d) -> p e d", d=S), ins["L0_ffn_w2"].rearrange("e (h p) d -> p (e h) d", p=P)),
                    (w2b.rearrange("p (e d) -> p e d", d=S), ins["L1_ffn_w2"].rearrange("e p d -> p e d")),
                    (gamma, ins["L1_ffn_gamma"].partition_broadcast(P)), (beta, ins["L1_ffn_beta"].partition_broadcast(P)),
                ]
                for i in range(8):
                    dmas.append((b2a[E1 * i:E1 * i + E1, S * i:S * i + S], ins["L0_ffn_b2"]))
                    dmas.append((b2b[E2 * i:E2 * i + E2, S * i:S * i + S], ins["L1_ffn_b2"]))
                for i in range(2):
                    dmas.append((wg0[:, S * i:S * i + S], ins["L1_attn_W0"]))
                    dmas.append((wg1[:, S * i:S * i + S], ins["L1_attn_W1"]))
                    q = slice(64 * i, 64 * i + 64)
                    dmas.append((gwa[q], ins["L0_ffn_gate_w"]))
                    dmas.append((gwb[q], ins["L1_ffn_gate_w"]))
                    dmas.append((w1a[q].rearrange("d (e f) -> d e f", e=E1), ins["L0_ffn_w1"].rearrange("e d f -> d e f")))
                    dmas.append((w1b[q].rearrange("d (e f) -> d e f", e=E2), ins["L1_ffn_w1"].rearrange("e d f -> d e f")))
                    for n, b in enumerate(("L1_attn_b0", "L1_attn_b1")):
                        for part in range(2):
                            dmas.append((gbias[q, 2 * n + part:2 * n + part + 1], col(ins[b][S * part:S * part + S])))
                assert len(dmas) == N_PARAMS
                for dst, src in dmas:
                    sp.dma_start(dst, src).then_inc(s["par_loaded"], 16)

            def loads(ph, L):
                p = Phase(ph, L)

                def group(g, more):
                    if more:
                        op = "xt" if ph == "first" else "i1"
                        p.sent(sp, op, p.ends(op)[1], g)
                        load_x(g + 1) if ph == "first" else load_y(g + 1)
                    if more and ph != "first":
                        for t in range(2):
                            sp.wait_ge(s["acc_full"], at("acc", ph, L, g, 4 * t + 4))
                            load_h(g + 1, t)
                    if ph != "last":
                        store_h(ph, L, g, 0)
                        store_h(ph, L, g, 1)

                if ph == "first":
                    weights(0)
                else:
                    load_y(0)
                if ph == "mid":
                    weights(L + 1)
                group(0, True)
                if ph == "last":
                    token_params()
                with sp.Fori(1, NG - 1) as g:
                    group(g, True)
                group(NG - 1, False)

            def first_h(ph, L):
                for t in range(2):
                    sp.wait_ge(s[f"stored{t}"], at("stored", ph, L, 0, 0) + 16)
                for t in range(2):
                    load_h(0, t)

            loads("first", 0)
            with sp.Fori(0, LAYERS - 1) as L:
                conv_params(L)
                first_h("mid", L)
                y_store(L)
                y_is_stored(L)
                loads("mid", L)
            L = LAYERS - 1
            conv_params(L)
            first_h("last", L)
            y_store(L)
            sp.wait_ge(s["mlp_cleared"], 1)
            for j in range(4):
                sp.dma_start(fc1_raw[32 * j:32 * j + 32, 128 * (j // 2):128 * (j // 2) + 128],
                             ins["L0_tok_fc1_w"]).then_inc(s["mlp_loaded"], 16)
            sp.dma_start(fc1_b, ins["L0_tok_fc1_b"].rearrange("(p o) -> p o", o=1)).then_inc(s["mlp_loaded"], 16)
            sp.dma_start(fc2_w, ins["L0_tok_fc2_w"]).then_inc(s["mlp_loaded"], 16)
            for j in range(2):
                q = slice(64 * j, 64 * j + 64)
                sp.dma_start(fc2_b[q], ins["L0_tok_fc2_b"].rearrange("(p o) -> p o", o=1)).then_inc(s["mlp_loaded"], 16)
                for k in range(2):
                    sp.dma_start(fc3_pad[q, k, 2 * k + j:2 * k + j + 1], ins["L0_tok_fc3_w"]).then_inc(s["mlp_loaded"], 16)
            sp.dma_start(fc3_b, ins["L0_tok_fc3_b"].partition_broadcast(P)).then_inc(s["mlp_loaded"], 16)
            y_is_stored(L)
            loads("last", L)
            sp.wait_ge(s["acc_done"], 1)
            sp.dma_start(out_ap.rearrange("(t b) y x -> (b y) t x", b=2), X.rearrange("p (t x) -> p t x", x=S)).then_inc(s["out_stored"], 16)
            sp.wait_ge(s["out_stored"], 16)

        @block.gpsimd
        def _(pool):
            def flip(L, j, m):
                w, k, n = m // 2, m % 2, C // 4
                v = w_v[64 * k + 32:64 * k + 64, w, 0, n * j:n * j + n].rearrange("p o m -> p (o m)")
                pool.tensor_scalar(v, v, -1.0, None, ALU.mult).then_inc(s["w_signed"], 1)
                pool.wait_ge(s["w_signed"], at("w_signed", "mix", L, 0, 4 * j + m + 1))
                alone(pool)

            def group(ph, L, g, and_then=None):
                for m in range(4):
                    pool.wait_ge(s["summed"], at("summed", ph, L, g, 2 * m + 2))
                    alone(pool)
                    rsqrt(pool, rstd[m % 2], var[m % 2], newton, s["pool_chain"],
                          lambda k: at("pool_chain", ph, L, g, 13 * m + k), s["rstd_ok"], alone)
                    if and_then:
                        pool.wait_ge(s["rstd_ok"], at("rstd", ph, L, g, m + 1))
                        alone(pool)
                        and_then(m)

            def groups(ph, L, layer_loaded):
                for j in range(4):
                    g = (j + 1) * (NG // 4) - 1
                    with pool.Fori(g + 1 - NG // 4, g) as b:
                        group(ph, L, b)
                    if j == 0:
                        pool.wait_ge(s["w_loaded"], 256 * layer_loaded + 256)
                        alone(pool)
                    group(ph, L, g, lambda m: flip(layer_loaded, j, m))

            groups("first", 0, 0)
            with pool.Fori(0, LAYERS - 1) as L:
                groups("mid", L, L + 1)
            L = LAYERS - 1
            pool.wait_ge(s["s_full"], at("s_out", "mix", L, 0, 12))
            pool.wait_ge(s["d_full"], at("d_out", "mix", L, 0, 12))
            pool.memset(w_sb[:, 0:1024], 0.0).then_inc(s["mlp_cleared"], 1)
            pool.wait_ge(s["mlp_cleared"], 1)
            pool.memset(spec[:, 0:at_col[0]], 0.0).then_inc(s["par_cleared"], 1)
            pool.wait_ge(s["par_cleared"], 1)
            pool.wait_ge(s["y_chain"], at("y_chain", "mix", L, 0, 24))
            pool.memset(XT[64:128, :], 0.0).then_inc(s["ones_set"], 1)
            pool.wait_ge(s["ones_set"], 1)
            pool.memset(XT[64:65, :], 1.0).then_inc(s["ones_set"], 1)
            pool.wait_ge(s["ones_set"], 2)
            with pool.Fori(0, NG) as g:
                group("last", L, g)
            token_pool(pool)

        @block.tensor
        def _(pe):
            pe.wait_ge(s["cst_loaded"], 16)

            def mix(L):
                pe.wait_ge(s["w_signed"], at("w_signed", "mix", L, 0, 16))
                pe.wait_ge(s["d_free"], at("d_out", "mix", L, 0, 2))
                for half in range(2):
                    for q in range(6):
                        k0 = 6 * half + q
                        pe.wait_ge(s["d_free"], at("d_out", "mix", L, 0, k0 + 1))
                        pe.wait_ge(s["s_free"], at("s_out", "mix", L, 0, k0 + 1))
                        alone(pe)
                        banks = [pD[k0 % 2], pS[k0 % 2]]
                        for j in range(6):
                            for par in range(2):
                                for w in range(2):
                                    rows = slice(64 * par, 64 * par + 64)
                                    mm = pe.matmul(
                                        banks[par][64 * w:64 * w + B, 64 * j:64 * j + 64],
                                        spec_v[rows, q, 12 * w + 6 * half + j, :],
                                        w_v[rows, w, :, :, (6 * half + j) * M2 + 2 * q + par],
                                        start=True, stop=True)
                                    if j == 5 and w == 1:
                                        mm.then_inc(s["d_full" if par == 0 else "s_full"], 1)

            def steps(p):
                ph, L = p.ph, p.L

                def bank_of(op, n, g):
                    ring, bank, v = p.product(op, n, g)
                    pe.wait_ge(s[ring + "_free"], v)
                    return bank

                def send(mm, op, n, g):
                    mm.then_inc(s[p.product(op, n, g)[0] + "_full"], 1)

                def xt(t, g):
                    if t == p.ends("xt")[0]:
                        pe.wait_ge(s["x_loaded"], at("x_in", ph, L, g, 16))
                    bank = bank_of("xt", t, g)
                    alone(pe)
                    for xb in range(4):
                        mm = pe.transpose(bank[0:48, 128 * xb:128 * xb + 128], x_in[:, t, 48 * xb:48 * xb + 48], ident)
                    send(mm, "xt", t, g)

                def i1(n, g):
                    if n == p.ends("i1")[0]:
                        pe.wait_ge(s["y_loaded"], at("y_in", ph, L, g, 32))
                    bank, t = bank_of("i1", n, g), n // 2
                    send(pe.matmul(bank[:, 0:384], const[("idft_y_re", "idft_y_im")[n % 2]], y_in[:, 384 * t:384 * t + 384],
                                   start=True, stop=True), "i1", n, g)

                def t2(n, g):
                    t, half = n // 2, n % 2
                    p.taken(pe, ("i1", 2 * t), ("i1", 2 * t + 1), g=g)
                    bank = bank_of("t2", n, g)
                    for j in range(4):
                        o = 4 * half + j
                        mm = pe.transpose(bank[0:96, 128 * j:128 * j + 128], Z[:, 96 * o:96 * o + 96], ident)
                    send(mm, "t2", n, g)

                def acc(n, g):
                    t, xb = n // 4, n % 4
                    pe.wait_ge(s["squared"], at("squared", ph, L, g, n + 1))
                    bank = pA[n % 2]
                    if ph == "first":
                        if n == 0:
                            pe.wait_ge(s["fc0_chain"], 4)
                        if xb == 0:
                            p.taken(pe, ("xt", t), g=g)
                        mm = pe.matmul(bank[:], xT[:, t, 128 * xb:128 * xb + 128],
                                       fc0.rearrange("p x o -> p (x o)"), start=True, stop=True)
                    else:
                        if n == 0:
                            pe.wait_ge(s["conv_chain"], 2 * L + 2)
                        if xb == 0:
                            pe.wait_ge(s[f"h_loaded{t}"], at("h_in", ph, L, g, 16))
                        out = bank[:].rearrange("p (x o) -> p o x", x=16)
                        for j in range(4):
                            pe.matmul(bank[:, 128 * j:128 * j + 128], hin_v[:, t, 4 * xb + j, :], conv_bd[:],
                                      start=(j == 0), stop=False, skip_group_check=True)
                        if xb == 0:
                            p.taken(pe, ("t2", 2 * t), ("t2", 2 * t + 1), g=g)
                        for o in range(8):
                            mm = pe.matmul(out[:, 4 * o:4 * o + 4, :],
                                           T2[0:96, 1024 * t + 128 * o:1024 * t + 128 * o + 128],
                                           const["idft_x"][:, 64 * xb:64 * xb + 64],
                                           start=False, stop=(o == 7), skip_group_check=True)
                    mm.then_inc(s["acc_full"], 1)

                def turn(n, g):
                    pe.wait_ge(s["normed"], at("normed", ph, L, g, 3 * (n // 2) + 3 if ph == "last" else n + 1))
                    if n >= 2 or not first_group(g):
                        pe.wait_ge(s["h_new_ok"], at("h_new", ph, L, g, n - 1))
                    if ph == "last":
                        rows = split[n // 2 % 2][:, 8 * (n % 2):8 * (n % 2) + 8].rearrange("p x a c -> p (x a c)")
                    else:
                        rows = raw_of(n)
                    for j in range(4):
                        mm = pe.transpose(pT[n % 2][:, 128 * j:128 * j + 128], rows[:, 128 * j:128 * j + 128], ident)
                    mm.then_inc(s["turned"], 1)

                def back(n, g):
                    t, xb = n // 4, n % 4
                    pe.wait_ge(s["h_new_ok"], at("h_new", ph, L, g, n + 1))
                    bank = bank_of("back", n, g)
                    for j in range(4):
                        mm = pe.transpose(bank[:, 128 * j:128 * j + 128], hnew_v[:, t, 4 * xb + j, :], ident)
                    send(mm, "back", n, g)

                def f1(k, g):
                    p.taken(pe, ("back", k), ("back", 4 + k), g=g)
                    bank = bank_of("f1", k, g)
                    for t in range(2):
                        mm = pe.matmul(bank[64 * t:64 * t + 64, :], const["dft_y"], hrow_v[:, t, 512 * k:512 * k + 512],
                                       start=True, stop=True)
                    send(mm, "f1", k, g)

                def tr(k, g):
                    p.taken(pe, *[("f1", i) for i in range(4)], g=g)
                    bank = bank_of("tr", k, g)
                    for j in range(4):
                        c = 2 * (4 * k + j)
                        mm = pe.transpose(bank[:, 128 * j:128 * j + 128], V[:, S * c:S * c + 128], ident)
                    send(mm, "tr", k, g)

                def f2(k, g):
                    p.taken(pe, ("tr", k), g=g)
                    bank = bank_of("f2", k, g)
                    for j in range(4):
                        mm = pe.matmul(bank[:, 96 * j:96 * j + 96], TA[k][:, 128 * j:128 * j + 128],
                                       const["dft_x"], start=True, stop=True)
                    send(mm, "f2", k, g)

                def xx(k, g):
                    p.taken(pe, *[("f2", i) for i in range(4)], g=g)
                    bank = bank_of("xx", k, g)
                    for j in range(3):
                        q = 3 * k + j
                        o = bank[:, 96 * j:96 * j + 96]
                        pe.matmul(o, Xs[:, 256 * q:256 * q + 128], const["mix_cos"], start=True, stop=False)
                        mm = pe.matmul(o, Xs[:, 256 * q + 128:256 * q + 256], const["mix_sin"], start=False, stop=True)
                    send(mm, "xx", k, g)

                def fc1(m, g):
                    u, j = m // 2, m % 2
                    if m == p.ends("fc1")[0]:
                        pe.wait_ge(s["mlp_ready"], 4)
                    pe.wait_ge(s["h_new_ok"], at("h_new", ph, L, g, u + 1))
                    bank = bank_of("fc1", m, g)
                    x = h_split[:, 512 * (u % 8):512 * (u % 8) + 512].bitcast(F32R)
                    for w in (fc1_hi, fc1_lo):
                        mm = pe.matmul(bank[:], w[:, 128 * j:128 * j + 128].bitcast(F32R), x, start=(w is fc1_hi), stop=(w is fc1_lo))
                    send(mm, "fc1", m, g)

                def fc2(m, g):
                    p.taken(pe, ("fc1", 2 * m), ("fc1", 2 * m + 1), g=g)
                    bank = bank_of("fc2", m, g)
                    for j in range(2):
                        mm = pe.matmul(bank[64 * j:64 * j + 64, :], fc2_w, G1[2 * (m % 2) + j], start=True, stop=True)
                    send(mm, "fc2", m, g)

                def fc3(t, g):
                    p.taken(pe, *[("fc2", 8 * t + i) for i in range(8)], g=g)
                    bank = bank_of("fc3", t, g)
                    for k in range(2):
                        for xb in range(4):
                            mm = pe.matmul(bank[32 * xb:32 * xb + 32, :], fc3_pad[:, k, :], G2[:, 2 * xb + k, :],
                                           start=(k == 0), stop=(k == 1), skip_group_check=True)
                    send(mm, "fc3", t, g)

                def fin(t, g):
                    p.taken(pe, ("fc3", t), g=g)
                    bank = bank_of("fin", t, g)
                    for j in range(4):
                        mm = pe.transpose(bank[:, 128 * j:128 * j + 128], G3[:, 128 * j:128 * j + 128], ident)
                    send(mm, "fin", t, g)

                return dict(xt=xt, i1=i1, t2=t2, acc=acc, turn=turn, back=back, f1=f1, tr=tr, f2=f2, xx=xx,
                            fc1=fc1, fc2=fc2, fc3=fc3, fin=fin)

            def before_last():
                pe.wait_ge(s["mlp_loaded"], 16 * 13)
                pe.wait_ge(s["h_new_ok"], at("h_new", "last", LAYERS - 1, 0, 0))
                pe.matmul(pT[0][:, 0:1], fc1_raw[:, 0:128], bet[:, LAYERS:LAYERS + 1], start=True, stop=True).then_inc(s["fc1_bias"], 1)

            phases(pe, "PE", mix, steps, before_last)
            token_pe(pe)

        @block.scalar
        def _(act):
            act.sem_inc(s["s_free"], 2)
            act.sem_inc(s["squared"], 2)
            act.sem_inc(s["stored0"], 16)
            act.sem_inc(s["stored1"], 16)

            def mix(L):
                for k in range(12):
                    act.wait_ge(s["s_full"], at("s_out", "mix", L, 0, k + 1))
                    half, q = k // 6, k % 6
                    src = pS[k % 2][:, 0:384].rearrange("p (k r o) -> p k r o", k=6, r=2)
                    act.copy(y_mix[:, 6 * half:6 * half + 6, :, 2 * q + 1, :], src).then_inc(s["s_free"], 1)

            def steps(p):
                ph, L = p.ph, p.L
                take = lambda op, n, g: p.sent(act, op, n, g)

                def xt(t, g):
                    if first_group(g):
                        act.wait_ge(s["fc0_chain"], 1)
                    act.copy(xT[0:48, t, :], take("xt", t, g)[0:48, :]).then_inc(s["s_free"], 1)

                def i1(n, g):
                    act.copy(Z.rearrange("p (o r k) -> p r k o", o=C, r=2)[:, n % 2],
                             take("i1", n, g)[:, 0:384].rearrange("p (k o) -> p k o", o=C)).then_inc(s["s_free"], 1)

                def t2(n, g):
                    act.copy(T2[0:96, 512 * n:512 * n + 512], take("t2", n, g)[0:96, :]).then_inc(s["s_free"], 1)

                def acc(n, g):
                    act.wait_ge(s["acc_full"], at("acc", ph, L, g, n + 1))
                    act.copy(raw_of(n), pA[n % 2][:])
                    if n >= 2 or not first_group(g):
                        act.wait_ge(s["summed"], at("summed", ph, L, g, n - 1))
                    act.activation(sq[n % 2], pA[n % 2][:], ACT.Square, scale=float(C) ** -0.5).then_inc(s["squared"], 1)

                def gelu(n, g):
                    act.wait_ge(s["turned"], at("turned", ph, L, g, n + 1))
                    if ph == "first" and first_group(g) and n == 0:
                        act.wait_ge(s["ln_loaded"], 16 * 4 * 2 * 2)
                    if ph == "last":
                        act.copy(h_split[:, 512 * (n % 8):512 * (n % 8) + 512].bitcast(F32R), pT[n % 2][:]).then_inc(s["h_new_ok"], 1)
                        return
                    if n % 4 == 0 and ph != "last":
                        act.wait_ge(s[f"stored{n // 4}"], at("stored", ph, L, g, 0) + 16)
                    alone(act)
                    col = {"first": slice(0, 1), "mid": bass.ds(L + 1, 1)}[ph]
                    act.activation(h_new[:, 512 * n:512 * n + 512], pT[n % 2][:], ACT.Gelu if ph == "mid" else ACT.Identity,
                                   bias=bet[:, col], scale=gam[:, col]).then_inc(s["h_new_ok"], 1)

                def f1(k, g):
                    act.copy(V.rearrange("p (c x) -> p c x", x=S)[:, :, 16 * k:16 * k + 16],
                             take("f1", k, g)[:].rearrange("p (x c) -> p c x", c=C)).then_inc(s["s_free"], 1)

                def f2(k, g):
                    act.copy(Xs.rearrange("p (j c) -> p j c", c=C)[:, :, 8 * k:8 * k + 8],
                             take("f2", k, g)[:, 0:384].rearrange("p (c j) -> p j c", j=48)).then_inc(s["s_free"], 1)

                def fc1(m, g):
                    bank = take("fc1", m, g)
                    if m == p.ends("fc1")[0]:
                        act.wait_ge(s["mlp_ready"], 4)
                    act.activation(G1[m % 4], bank[:], ACT.Gelu, bias=fc1_b).then_inc(s["s_free"], 1)

                def fc2(m, g):
                    act.activation(G2[:, m % 8, :], take("fc2", m, g)[:], ACT.Gelu, bias=fc2_b).then_inc(s["d_free"], 1)

                def fc3(t, g):
                    act.copy(G3, take("fc3", t, g)[:]).then_inc(s["s_free"], 1)

                def fin(t, g):
                    bank = take("fin", t, g)
                    alone(act)
                    for k in range(2):
                        ins_ = act.activation(
                            tok[:, bass.ds(g * 128 + 64 * t, 64)].rearrange("p (b k q j) -> p b k q j", b=4, k=2, q=4)[:, :, k],
                            bank[:].rearrange("p (q b r) -> p b q r", q=4, b=4)[:, :, :, 2 * k:2 * k + 2],
                            ACT.Identity, bias=fc3_b)
                    ins_.then_inc(s["s_free"], 1)

                return dict(xt=xt, i1=i1, t2=t2, acc=acc, gelu=gelu, f1=f1, f2=f2, fc1=fc1, fc2=fc2, fc3=fc3, fin=fin)

            phases(act, "ACT", mix, steps)
            token_act(act)

        @block.vector
        def _(dve):
            dve.sem_inc(s["d_free"], 2)
            dve.memset(conv_bd[:], 0.0).then_inc(s["conv_cleared"], 1)
            dve.memset(T2[:, 0:1536], 0.0).then_inc(s["fc0_clear"], 1)
            dve.wait_ge(s["fc0_clear"], 1)
            dve.memset(T2[64:65, 0:1024], 1.0).then_inc(s["fc0_chain"], 1)
            dve.wait_ge(s["fc0_loaded"], 16 * 17)
            dve.tensor_copy(fc0[64:65], fc0_row.rearrange("p (x o) -> p x o", x=1).broadcast_to([1, 16, C])).then_inc(s["fc0_chain"], 1)
            dve.wait_ge(s["fc0_chain"], 2)
            dve.reduce_sum(fc0_mean, fc0, axis=AX).then_inc(s["fc0_chain"], 1)
            dve.wait_ge(s["fc0_chain"], 3)
            dve.scalar_tensor_tensor(out=fc0, in0=fc0_mean.rearrange("p (x o) -> p x o", o=1).broadcast_to([P, 16, C]),
                                     scalar=-1.0 / C, in1=fc0, op0=ALU.mult, op1=ALU.add).then_inc(s["fc0_chain"], 1)

            def mix(L):
                dve.wait_ge(s["conv_loaded"], 80 * L + 80)
                cv = conv_bd[:].rearrange("p (x o) -> p x o", x=4)
                cm = small[:, 64:68]
                dve.reduce_sum(cm, cv, axis=AX)
                dve.reduce_sum(small[0:B, 68:69], cbias[0:B, :], axis=AX).then_inc(s["conv_chain"], 1)
                dve.wait_ge(s["conv_chain"], 2 * L + 1)
                dve.scalar_tensor_tensor(out=cv, in0=cm.rearrange("p (x o) -> p x o", o=1).broadcast_to([P, 4, C]),
                                         scalar=-1.0 / C, in1=cv, op0=ALU.mult, op1=ALU.add)
                dve.scalar_tensor_tensor(out=cbias[0:B, :], in0=small[0:B, 68:69].broadcast_to([B, C]),
                                         scalar=-1.0 / C, in1=cbias[0:B, :], op0=ALU.mult, op1=ALU.add).then_inc(s["conv_chain"], 1)
                yv = arena[:].rearrange("p (n x o) -> p n x o", x=KX, o=C)
                chain = lambda k: at("y_chain", "mix", L, 0, k)

                def centre(k):
                    half, q = k // 6, k % 6
                    v = yv[:, 12 * half:12 * half + 12, 2 * q:2 * q + 2, :]
                    mean = y_mean[:, 24 * k:24 * k + 24].rearrange("p (n x) -> p n x", x=2)
                    dve.wait_ge(s["s_free"], at("s_out", "mix", L, 0, k + 1) + 2)
                    dve.wait_ge(s["d_free"], at("d_out", "mix", L, 0, k + 1) + 2)
                    dve.reduce_sum(mean, v, axis=AX).then_inc(s["y_chain"], 1)
                    dve.wait_ge(s["y_chain"], chain(2 * k + 1))
                    for x in range(2):
                        ins = dve.scalar_tensor_tensor(out=v[:, :, x, :], in0=mean[:, :, x:x + 1].broadcast_to([P, 12, C]),
                                                       scalar=-1.0 / C, in1=v[:, :, x, :], op0=ALU.mult, op1=ALU.add)
                    ins.then_inc(s["y_chain"], 1)

                for k in range(12):
                    dve.wait_ge(s["d_full"], at("d_out", "mix", L, 0, k + 1))
                    half, q = k // 6, k % 6
                    dve.tensor_copy(y_mix[:, 6 * half:6 * half + 6, :, 2 * q, :],
                                    pD[k % 2][:, 0:384].rearrange("p (k r o) -> p k r o", k=6, r=2)).then_inc(s["d_free"], 1)
                    if k:
                        centre(k - 1)
                    if k == 1:
                        dve.wait_ge(s["y_chain"], chain(2))
                        dve.wait_ge(s["conv_chain"], 2 * L + 2)
                        dve.scalar_tensor_tensor(out=arena[0:B, 0:C], in0=cbias[0:B, :], scalar=float(NPIX), in1=arena[0:B, 0:C],
                                                 op0=ALU.mult, op1=ALU.add)
                centre(11)

            def steps(p):
                ph, L = p.ph, p.L
                take = lambda op, n, g: p.sent(dve, op, n, g)

                def i1(n, g):
                    dve.tensor_copy(Z.rearrange("p (o r k) -> p r k o", o=C, r=2)[:, n % 2],
                                    take("i1", n, g)[:, 0:384].rearrange("p (k o) -> p k o", o=C)).then_inc(s["d_free"], 1)

                def red(n, g):
                    m = n // 2
                    dve.wait_ge(s["squared"], at("squared", ph, L, g, n + 1) + 2)
                    dve.reduce_sum(var[m % 2][:, 16 * (n % 2):16 * (n % 2) + 16],
                                   sq[n % 2].rearrange("p (x o) -> p x o", x=16), axis=AX).then_inc(s["summed"], 1)

                def scale(n, g):
                    m = n // 2
                    dve.wait_ge(s["rstd_ok"], at("rstd", ph, L, g, m + 1))
                    z = raw_of(n).rearrange("p (x o) -> p x o", x=16)
                    normed = lambda k: at("normed", ph, L, g, k)
                    r = rstd[m % 2][:, 16 * (n % 2):16 * (n % 2) + 16].rearrange("p (x o) -> p x o", o=1)
                    dve.tensor_tensor(z, z, r.broadcast_to([P, 16, C]), ALU.mult).then_inc(s["normed"], 1)
                    if ph == "last":
                        hi, lo = split[n % 2][:, :, 0], split[n % 2][:, :, 1]
                        if n >= 2 or not first_group(g):
                            dve.wait_ge(s["turned"], at("turned", ph, L, g, 2 * n - 2))
                        dve.wait_ge(s["normed"], normed(3 * n + 1))
                        dve.tensor_copy(hi.bitcast(F32R), z).then_inc(s["normed"], 1)
                        dve.wait_ge(s["normed"], normed(3 * n + 2))
                        dve.tensor_tensor(lo.bitcast(F32R), z, hi, ALU.subtract).then_inc(s["normed"], 1)

                def back(n, g):
                    dve.tensor_copy(h_rows[:, 512 * n:512 * n + 512], take("back", n, g)[:]).then_inc(s["d_free"], 1)

                def tr(k, g):
                    dve.tensor_copy(TA[k], take("tr", k, g)[:]).then_inc(s["d_free"], 1)

                def xx(k, g):
                    bank = take("xx", k, g)
                    dve.tensor_copy(spec_v[:, 3 * k:3 * k + 3, :, bass.ds(GI * g, GI)],
                                    bank[:, 0:288].rearrange("p (q k b) -> p q k b", q=3, b=GI)).then_inc(s["d_free"], 1)

                return dict(i1=i1, red=red, scale=scale, back=back, tr=tr, xx=xx)

            def before_last():
                dve.wait_ge(s["fc1_bias"], 1)
                dve.scalar_tensor_tensor(out=fc1_b, in0=pT[0][:, 0:1], scalar=0.5, in1=fc1_b, op0=ALU.mult, op1=ALU.add).then_inc(s["mlp_ready"], 1)
                dve.tensor_scalar(fc1_raw, fc1_raw, gam[:, LAYERS:LAYERS + 1], None, ALU.mult).then_inc(s["mlp_ready"], 1)
                dve.wait_ge(s["mlp_ready"], 2)
                dve.tensor_copy(fc1_hi.bitcast(F32R), fc1_raw).then_inc(s["mlp_ready"], 1)
                dve.wait_ge(s["mlp_ready"], 3)
                dve.tensor_tensor(fc1_lo.bitcast(F32R), fc1_raw, fc1_hi, ALU.subtract).then_inc(s["mlp_ready"], 1)

            phases(dve, "DVE", mix, steps, before_last)
            token_dve(dve)


_INS = [
    "x", "L0_tok_fc0_w", "L0_tok_fc0_b", "L0_tok_ln0_g", "L0_tok_ln0_b", "L0_tok_w1r", "L0_tok_w1i", "L0_tok_w2r", "L0_tok_w2i",
    "L0_tok_conv_w", "L0_tok_conv_b", "L0_tok_ln_g", "L0_tok_ln_b", "L0_tok_fc1_w", "L0_tok_fc1_b", "L0_tok_fc2_w",
    "L0_tok_fc2_b", "L0_tok_fc3_w", "L0_tok_fc3_b", "L0_attn_Wq", "L0_attn_bq", "L0_attn_Wk", "L0_attn_bk", "L0_attn_Wv",
    "L0_attn_bv", "L0_ffn_gate_w", "L0_ffn_gate_b", "L0_ffn_w1", "L0_ffn_b1", "L0_ffn_w2", "L0_ffn_b2", "L1_attn_W0",
    "L1_attn_b0", "L1_attn_W1", "L1_attn_b1", "L1_ffn_gate_w", "L1_ffn_gate_b", "L1_ffn_w1", "L1_ffn_b1", "L1_ffn_w2",
    "L1_ffn_b2", "L1_ffn_gamma", "L1_ffn_beta",
]


def kernel(**inputs):
    import numpy as _np
    import concourse.bacc as _bacc
    from concourse import mybir as _mybir
    from concourse.bass_utils import run_bass_kernel_spmd as _run

    nc = _bacc.Bacc("TRN2", target_bir_lowering=False, num_devices=1)
    arrays, args = {}, {}
    for name in _INS + ["consts"]:
        a = CONSTS if name == "consts" else _np.ascontiguousarray(inputs[name])
        arrays[f"in_{name}_dram"] = a
        args[name] = nc.dram_tensor(f"in_{name}_dram", a.shape, _mybir.dt.from_np(a.dtype), kind="ExternalInput").ap()
    B = inputs["x"].shape[0]
    out = nc.dram_tensor("out_0_dram", (B, S, S), _mybir.dt.float32, kind="ExternalOutput").ap()
    build(nc, args, out, B)
    r = _run(nc, [arrays], core_ids=[0])
    return r.results[0]["out_0_dram"]
```
